# Optimizing a Trainium2 kernel written in Bass

```python
import numpy as np
import jax
import jax.numpy as jnp

def _softmax(x, axis=-1):
    return jax.nn.softmax(x, axis=axis)

def _gelu(x):
    return jax.nn.gelu(x, approximate=True)

def _silu(x):
    return jax.nn.silu(x)

def _sigmoid(x):
    return jax.nn.sigmoid(x)

def _layernorm(x, axis=-1, eps=1e-05):
    m = jnp.mean(x, axis=axis, keepdims=True)
    v = jnp.var(x, axis=axis, keepdims=True)
    return (x - m) / jnp.sqrt(v + eps)

def _scatter_add(tgt, idx, src, axis=0):
    return tgt.at[idx].add(src)

def _segment_sum(src, seg, n):
    return jax.ops.segment_sum(src, seg, n)
kernel_name = 'mk_gps_d2_gnn_r8_18c931'

def setup_inputs(seed: int=0):
    np.random.seed(seed)
    _w = jnp.asarray

    def _rec_inputs():
        import jax
        import jax.numpy as jnp
        _gk = jax.random.key(seed)
        x = -8.776e-05 + 1 * jax.random.normal(jax.random.fold_in(_gk, 1), (6250, 256), jnp.float32)
        src = jax.random.randint(jax.random.fold_in(_gk, 2), (100000,), 0, 6250, jnp.int32)
        dst = jnp.minimum((6250 * jax.random.uniform(jax.random.fold_in(_gk, 3), (100000,)) ** 2.0).astype(jnp.int32), 49999)
        _o = jnp.argsort(dst, stable=True)
        src = src[_o]
        dst = dst[_o]
        edge_weight = jax.random.uniform(jax.random.fold_in(_gk, 12), (100000,), jnp.float32, 0.0, 0.999998)
        return (x, src, dst, edge_weight)
    x, src, dst, edge_weight = _rec_inputs()

    def _L0_gnn_setup():
        import jax, jax.numpy as jnp
        import numpy as np
        N, E, D, H, C = (2500, 40000, 256, 8, 32)
        NEG_SLOPE = 0.2
        key = jax.random.key(seed)
        ks = jax.random.split(key, 9)
        s = 1.0 / np.sqrt(D)
        x = jax.random.normal(ks[0], (N, D), dtype=jnp.float32)
        edge_index = jax.random.randint(ks[1], (2, E), 0, N, dtype=jnp.int32)
        edge_attr = jax.random.uniform(ks[2], (E,), dtype=jnp.float32, minval=0.05, maxval=1.0)
        W_l = jax.random.normal(ks[3], (D, H * C), dtype=jnp.float32) * s
        b_l = jax.random.normal(ks[4], (H * C,), dtype=jnp.float32) * 0.01
        W_r = jax.random.normal(ks[5], (D, H * C), dtype=jnp.float32) * s
        b_r = jax.random.normal(ks[6], (H * C,), dtype=jnp.float32) * 0.01
        att = jax.random.normal(ks[7], (H, C), dtype=jnp.float32) * (1.0 / np.sqrt(C))
        bias = jax.random.normal(ks[8], (H * C,), dtype=jnp.float32) * 0.01
        return {'x': x, 'edge_index': edge_index, 'edge_attr': edge_attr, 'W_l': W_l, 'b_l': b_l, 'W_r': W_r, 'b_r': b_r, 'att': att, 'bias': bias}
    _L0_gnn_all = _L0_gnn_setup()
    _L0_gnn_in = {k: v for k, v in _L0_gnn_all.items() if k in ('W_l', 'b_l', 'W_r', 'b_r', 'att', 'bias')}
    del _L0_gnn_all

    def _L0_mix_setup():
        import jax, jax.numpy as jnp
        import numpy as np
        B, L, D, H = (4, 2048, 256, 8)
        DK = D // H

        def _heads(t):
            b, l, d = t.shape
            return t.reshape(b, l, H, DK).transpose(0, 2, 1, 3)
        key = jax.random.key(seed)
        ks = jax.random.split(key, 9)
        s = 0.02
        return {'x': jax.random.normal(ks[0], (B, L, D), dtype=jnp.float32), 'Wq': jax.random.normal(ks[1], (D, D), dtype=jnp.float32) * s, 'bq': jnp.zeros((D,), dtype=jnp.float32), 'Wk': jax.random.normal(ks[2], (D, D), dtype=jnp.float32) * s, 'bk': jnp.zeros((D,), dtype=jnp.float32), 'Wv': jax.random.normal(ks[3], (D, D), dtype=jnp.float32) * s, 'bv': jnp.zeros((D,), dtype=jnp.float32), 'Wfc': jax.random.normal(ks[4], (D, D), dtype=jnp.float32) * s, 'bfc': jnp.zeros((D,), dtype=jnp.float32)}
    _L0_mix_all = _L0_mix_setup()
    _L0_mix_in = {k: v for k, v in _L0_mix_all.items() if k in ('Wq', 'bq', 'Wk', 'bk', 'Wv', 'bv', 'Wfc', 'bfc')}
    del _L0_mix_all

    def _L0_ffn_setup():
        import jax, jax.numpy as jnp
        import numpy as np
        B, S, D, E, H, K = (4, 512, 256, 8, 512, 2)
        key = jax.random.key(seed)
        ks = jax.random.split(key, 6)
        x = jax.random.normal(ks[0], (B, S, D), jnp.float32)
        Wg = jax.random.normal(ks[1], (D, E), jnp.float32) * 0.02
        bg = jnp.zeros((E,), jnp.float32)
        W1 = jax.random.normal(ks[2], (E, D, H), jnp.float32) * 0.02
        b1 = jnp.zeros((E, H), jnp.float32)
        W2 = jax.random.normal(ks[3], (E, H, D), jnp.float32) * 0.02
        b2 = jnp.zeros((E, D), jnp.float32)
        return {'x': x, 'Wg': Wg, 'bg': bg, 'W1': W1, 'b1': b1, 'W2': W2, 'b2': b2}
    _L0_ffn_all = _L0_ffn_setup()
    _L0_ffn_in = {k: v for k, v in _L0_ffn_all.items() if k in ('Wg', 'bg', 'W1', 'b1', 'W2', 'b2')}
    del _L0_ffn_all

    def _L1_gnn_setup():
        import jax, jax.numpy as jnp
        import numpy as np
        N_NODES = 6250

        def gcn_conv(x, W, b, src, dst, n_nodes):
            h = x @ W
            ones = jnp.ones(src.shape[0], dtype=h.dtype)
            deg = jax.ops.segment_sum(ones, dst, num_segments=n_nodes) + 1.0
            dinv = jax.lax.rsqrt(deg)
            norm = dinv[src] * dinv[dst]
            msg = h[src] * norm[:, None]
            agg = jax.ops.segment_sum(msg, dst, num_segments=n_nodes)
            agg = agg + h * (dinv * dinv)[:, None]
            return agg + b
        key = jax.random.key(seed)
        k1, k2, k3, k4 = jax.random.split(key, 4)
        embedding = jax.random.normal(k1, (N_NODES, 256), dtype=jnp.float32)
        edge_index = jax.random.randint(k2, (2, 100000), 0, N_NODES, dtype=jnp.int64)
        W1 = jax.random.normal(k3, (256, 64), dtype=jnp.float32) / np.sqrt(256.0)
        b1 = jnp.zeros((64,), dtype=jnp.float32)
        W2 = jax.random.normal(k4, (64, 256), dtype=jnp.float32) / np.sqrt(64.0)
        b2 = jnp.zeros((256,), dtype=jnp.float32)
        return {'embedding': embedding, 'edge_index': edge_index, 'W1': W1, 'b1': b1, 'W2': W2, 'b2': b2}
    _L1_gnn_all = _L1_gnn_setup()
    _L1_gnn_in = {k: v for k, v in _L1_gnn_all.items() if k in ('W1', 'b1', 'W2', 'b2')}
    del _L1_gnn_all

    def _L1_mix_setup():
        import jax, jax.numpy as jnp
        import numpy as np
        MIDC = 256
        HEADS = 8
        HEADC = MIDC // HEADS
        EPS = 1e-05

        def _ln(x, gamma, beta):
            mu = jnp.mean(x, axis=-1, keepdims=True)
            var = jnp.var(x, axis=-1, keepdims=True)
            return (x - mu) * jax.lax.rsqrt(var + EPS) * gamma + beta
        key = jax.random.key(seed)
        ks = jax.random.split(key, 8)
        B, HW, C = (8, 512, MIDC)
        s = 1.0 / np.sqrt(C)
        return {'x': jax.random.normal(ks[0], (B, HW, C), jnp.float32), 'w_qkv': jax.random.normal(ks[1], (C, 3 * C), jnp.float32) * s, 'b_qkv': jnp.zeros((3 * C,), jnp.float32), 'kln_g': jnp.ones((HEADC,), jnp.float32), 'kln_b': jnp.zeros((HEADC,), jnp.float32), 'vln_g': jnp.ones((HEADC,), jnp.float32), 'vln_b': jnp.zeros((HEADC,), jnp.float32), 'w1': jax.random.normal(ks[2], (C, C), jnp.float32) * s, 'b1': jnp.zeros((C,), jnp.float32), 'w2': jax.random.normal(ks[3], (C, C), jnp.float32) * s, 'b2': jnp.zeros((C,), jnp.float32)}
    _L1_mix_all = _L1_mix_setup()
    _L1_mix_in = {k: v for k, v in _L1_mix_all.items() if k in ('w_qkv', 'b_qkv', 'kln_g', 'kln_b', 'vln_g', 'vln_b', 'w1', 'b1', 'w2', 'b2')}
    del _L1_mix_all

    def _L1_ffn_setup():
        import math
        import jax, jax.numpy as jnp
        import numpy as np
        CAPACITY_FACTOR = 1.25
        key = jax.random.key(seed)
        ks = jax.random.split(key, 5)
        B, L, D, F, E = (8, 1024, 256, 1024, 8)
        h = jax.random.normal(ks[0], (B, L, D), dtype=jnp.float32)
        gate_w = jax.random.normal(ks[1], (D, E), dtype=jnp.float32) * 0.02
        gate_b = jnp.zeros((E,), dtype=jnp.float32)
        w1 = jax.random.normal(ks[2], (E, D, F), dtype=jnp.float32) * (1.0 / math.sqrt(D))
        b1 = jnp.zeros((E, F), dtype=jnp.float32)
        w2 = jax.random.normal(ks[3], (E, F, D), dtype=jnp.float32) * (1.0 / math.sqrt(F))
        b2 = jnp.zeros((E, D), dtype=jnp.float32)
        return {'h': h, 'gate_w': gate_w, 'gate_b': gate_b, 'w1': w1, 'b1': b1, 'w2': w2, 'b2': b2}
    _L1_ffn_all = _L1_ffn_setup()
    _L1_ffn_in = {k: v for k, v in _L1_ffn_all.items() if k in ('gate_w', 'gate_b', 'w1', 'b1', 'w2', 'b2')}
    del _L1_ffn_all
    return {'x': x, 'src': src, 'dst': dst, 'edge_weight': edge_weight, 'L0_gnn_W_l': _L0_gnn_in['W_l'], 'L0_gnn_b_l': _L0_gnn_in['b_l'], 'L0_gnn_W_r': _L0_gnn_in['W_r'], 'L0_gnn_b_r': _L0_gnn_in['b_r'], 'L0_gnn_att': _L0_gnn_in['att'], 'L0_gnn_bias': _L0_gnn_in['bias'], 'L0_mix_Wq': _L0_mix_in['Wq'], 'L0_mix_bq': _L0_mix_in['bq'], 'L0_mix_Wk': _L0_mix_in['Wk'], 'L0_mix_bk': _L0_mix_in['bk'], 'L0_mix_Wv': _L0_mix_in['Wv'], 'L0_mix_bv': _L0_mix_in['bv'], 'L0_mix_Wfc': _L0_mix_in['Wfc'], 'L0_mix_bfc': _L0_mix_in['bfc'], 'L0_ffn_Wg': _L0_ffn_in['Wg'], 'L0_ffn_bg': _L0_ffn_in['bg'], 'L0_ffn_W1': _L0_ffn_in['W1'], 'L0_ffn_b1': _L0_ffn_in['b1'], 'L0_ffn_W2': _L0_ffn_in['W2'], 'L0_ffn_b2': _L0_ffn_in['b2'], 'L1_gnn_W1': _L1_gnn_in['W1'], 'L1_gnn_b1': _L1_gnn_in['b1'], 'L1_gnn_W2': _L1_gnn_in['W2'], 'L1_gnn_b2': _L1_gnn_in['b2'], 'L1_mix_w_qkv': _L1_mix_in['w_qkv'], 'L1_mix_b_qkv': _L1_mix_in['b_qkv'], 'L1_mix_kln_g': _L1_mix_in['kln_g'], 'L1_mix_kln_b': _L1_mix_in['kln_b'], 'L1_mix_vln_g': _L1_mix_in['vln_g'], 'L1_mix_vln_b': _L1_mix_in['vln_b'], 'L1_mix_w1': _L1_mix_in['w1'], 'L1_mix_b1': _L1_mix_in['b1'], 'L1_mix_w2': _L1_mix_in['w2'], 'L1_mix_b2': _L1_mix_in['b2'], 'L1_ffn_gate_w': _L1_ffn_in['gate_w'], 'L1_ffn_gate_b': _L1_ffn_in['gate_b'], 'L1_ffn_w1': _L1_ffn_in['w1'], 'L1_ffn_b1': _L1_ffn_in['b1'], 'L1_ffn_w2': _L1_ffn_in['w2'], 'L1_ffn_b2': _L1_ffn_in['b2']}

def reference(x, src, dst, edge_weight, L0_gnn_W_l, L0_gnn_b_l, L0_gnn_W_r, L0_gnn_b_r, L0_gnn_att, L0_gnn_bias, L0_mix_Wq, L0_mix_bq, L0_mix_Wk, L0_mix_bk, L0_mix_Wv, L0_mix_bv, L0_mix_Wfc, L0_mix_bfc, L0_ffn_Wg, L0_ffn_bg, L0_ffn_W1, L0_ffn_b1, L0_ffn_W2, L0_ffn_b2, L1_gnn_W1, L1_gnn_b1, L1_gnn_W2, L1_gnn_b2, L1_mix_w_qkv, L1_mix_b_qkv, L1_mix_kln_g, L1_mix_kln_b, L1_mix_vln_g, L1_mix_vln_b, L1_mix_w1, L1_mix_b1, L1_mix_w2, L1_mix_b2, L1_ffn_gate_w, L1_ffn_gate_b, L1_ffn_w1, L1_ffn_b1, L1_ffn_w2, L1_ffn_b2):
    import jax
    import jax.numpy as jnp

    def _L0_gnn_ref(x, edge_index, edge_attr, W_l, b_l, W_r, b_r, att, bias):
        import jax, jax.numpy as jnp
        import numpy as np
        N, E, D, H, C = (2500, 40000, 256, 8, 32)
        NEG_SLOPE = 0.2
        n = x.shape[0]
        x_l = (x @ W_l + b_l).reshape(n, H, C)
        x_r = (x @ W_r + b_r).reshape(n, H, C)
        src, dst = (edge_index[0], edge_index[1])
        x_j = x_l[src]
        g = jax.nn.leaky_relu(x_r[dst] + x_j, NEG_SLOPE)
        alpha = jnp.einsum('ehc,hc->eh', g, att)
        alpha = alpha + jnp.log(edge_attr)[:, None]
        amax = jax.ops.segment_max(alpha, dst, num_segments=n)
        ex = jnp.exp(alpha - amax[dst])
        denom = jax.ops.segment_sum(ex, dst, num_segments=n)
        alpha = ex / (denom[dst] + 1e-16)
        out = jax.ops.segment_sum(x_j * alpha[..., None], dst, num_segments=n)
        return out.reshape(n, H * C) + bias

    def _L0_mix_ref(x, Wq, bq, Wk, bk, Wv, bv, Wfc, bfc):
        import jax, jax.numpy as jnp
        import numpy as np
        B, L, D, H = (4, 2048, 256, 8)
        DK = D // H

        def _heads(t):
            b, l, d = t.shape
            return t.reshape(b, l, H, DK).transpose(0, 2, 1, 3)
        q = _heads(x @ Wq.T + bq)
        k = _heads(x @ Wk.T + bk)
        v = _heads(x @ Wv.T + bv)
        seq_len = q.shape[-2]
        p_attn = jnp.einsum('bhnd,bhne->bhde', k, v) / seq_len
        out = jnp.einsum('bhnd,bhde->bhne', q, p_attn)
        out = out.transpose(0, 2, 1, 3).reshape(x.shape[0], seq_len, H * DK)
        return out @ Wfc.T + bfc

    def _L0_ffn_ref(x, Wg, bg, W1, b1, W2, b2):
        import jax, jax.numpy as jnp
        import numpy as np
        B, S, D, E, H, K = (4, 512, 256, 8, 512, 2)
        Bv, Sv, Dv = x.shape
        gate_scores = x @ Wg + bg
        _, idx = jax.lax.top_k(gate_scores, K)
        mask = jax.nn.one_hot(idx, E, dtype=x.dtype).sum(axis=-2)
        xf = x.reshape(-1, Dv)
        mf = mask.reshape(-1, E)
        h = jax.nn.gelu(jnp.einsum('td,edh->teh', xf, W1) + b1[None], approximate=False)
        y = jnp.einsum('teh,ehd->ted', h, W2) + b2[None]
        out = jnp.einsum('ted,te->td', y, mf)
        return out.reshape(Bv, Sv, Dv)

    def _L1_gnn_ref(embedding, edge_index, W1, b1, W2, b2):
        import jax, jax.numpy as jnp
        import numpy as np
        N_NODES = 6250

        def gcn_conv(x, W, b, src, dst, n_nodes):
            h = x @ W
            ones = jnp.ones(src.shape[0], dtype=h.dtype)
            deg = jax.ops.segment_sum(ones, dst, num_segments=n_nodes) + 1.0
            dinv = jax.lax.rsqrt(deg)
            norm = dinv[src] * dinv[dst]
            msg = h[src] * norm[:, None]
            agg = jax.ops.segment_sum(msg, dst, num_segments=n_nodes)
            agg = agg + h * (dinv * dinv)[:, None]
            return agg + b
        src, dst = (edge_index[0], edge_index[1])
        n = embedding.shape[0]
        h1 = jax.nn.relu(gcn_conv(embedding, W1, b1, src, dst, n))
        h2 = jax.nn.relu(gcn_conv(h1, W2, b2, src, dst, n))
        return h2

    def _L1_mix_ref(x, w_qkv, b_qkv, kln_g, kln_b, vln_g, vln_b, w1, b1, w2, b2):
        import jax, jax.numpy as jnp
        import numpy as np
        MIDC = 256
        HEADS = 8
        HEADC = MIDC // HEADS
        EPS = 1e-05

        def _ln(x, gamma, beta):
            mu = jnp.mean(x, axis=-1, keepdims=True)
            var = jnp.var(x, axis=-1, keepdims=True)
            return (x - mu) * jax.lax.rsqrt(var + EPS) * gamma + beta
        B, HW, C = x.shape
        bias = x
        qkv = (x @ w_qkv + b_qkv).reshape(B, HW, HEADS, 3 * HEADC)
        qkv = qkv.transpose(0, 2, 1, 3)
        q, k, v = jnp.split(qkv, 3, axis=-1)
        k = _ln(k, kln_g, kln_b)
        v = _ln(v, vln_g, vln_b)
        kv = jnp.einsum('bhnd,bhne->bhde', k, v) / HW
        out = jnp.einsum('bhnd,bhde->bhne', q, kv)
        out = out.transpose(0, 2, 1, 3).reshape(B, HW, C)
        ret = out + bias
        h = jax.nn.gelu(ret @ w1 + b1, approximate=False)
        return h @ w2 + b2 + bias

    def _L1_ffn_ref(h, gate_w, gate_b, w1, b1, w2, b2):
        import math
        import jax, jax.numpy as jnp
        import numpy as np
        CAPACITY_FACTOR = 1.25
        B, L, D = h.shape
        E = gate_w.shape[1]
        T = B * L
        C = max(1, math.ceil(CAPACITY_FACTOR * T / E))
        x = h.reshape(T, D)
        logits = x @ gate_w + gate_b
        probs = jax.nn.softmax(logits, axis=-1)
        idx = jnp.argmax(probs, axis=-1)
        prb = jnp.take_along_axis(probs, idx[:, None], axis=1)[:, 0]
        one_hot = jax.nn.one_hot(idx, E, dtype=jnp.float32)
        pos = (jnp.cumsum(one_hot, axis=0) * one_hot).sum(-1).astype(jnp.int32) - 1
        kept = pos < C
        pos_safe = jnp.where(kept, pos, C)
        buf = jnp.zeros((E, C, D), dtype=h.dtype).at[idx, pos_safe].set(x, mode='drop')
        hmid = jax.nn.relu(jnp.einsum('ecd,edf->ecf', buf, w1) + b1[:, None, :])
        ybuf = jnp.einsum('ecf,efd->ecd', hmid, w2) + b2[:, None, :]
        pos_g = jnp.minimum(pos, C - 1)
        y_tok = ybuf[idx, pos_g] * (prb * kept)[:, None]
        y = y_tok.reshape(B, L, D)
        y = jnp.nan_to_num(y, nan=0.0, posinf=10000.0, neginf=-10000.0)
        return y
    edge_index = jnp.stack([src, dst])
    xn = _layernorm(x, axis=-1)
    x = x + _L0_gnn_ref(xn, edge_index, edge_weight, L0_gnn_W_l, L0_gnn_b_l, L0_gnn_W_r, L0_gnn_b_r, L0_gnn_att, L0_gnn_bias) + _L0_mix_ref(xn[None], L0_mix_Wq, L0_mix_bq, L0_mix_Wk, L0_mix_bk, L0_mix_Wv, L0_mix_bv, L0_mix_Wfc, L0_mix_bfc)[0]
    x = x + _L0_ffn_ref(_layernorm(x, axis=-1)[None], L0_ffn_Wg, L0_ffn_bg, L0_ffn_W1, L0_ffn_b1, L0_ffn_W2, L0_ffn_b2)[0]
    xn = _layernorm(x, axis=-1)
    x = x + _L1_gnn_ref(xn, edge_index, L1_gnn_W1, L1_gnn_b1, L1_gnn_W2, L1_gnn_b2) + _L1_mix_ref(xn[None], L1_mix_w_qkv, L1_mix_b_qkv, L1_mix_kln_g, L1_mix_kln_b, L1_mix_vln_g, L1_mix_vln_b, L1_mix_w1, L1_mix_b1, L1_mix_w2, L1_mix_b2)[0]
    x = x + _L1_ffn_ref(_layernorm(x, axis=-1)[None], L1_ffn_gate_w, L1_ffn_gate_b, L1_ffn_w1, L1_ffn_b1, L1_ffn_w2, L1_ffn_b2)[0]
    return x

_drawn_inputs = setup_inputs


def setup_inputs(seed=0):
    import zlib

    import numpy as np

    out = dict(_drawn_inputs(seed))
    spreads = {'L0_mix_bq': (0.0, 0.8),
     'L0_mix_bk': (0.0, 0.624),
     'L0_mix_bv': (0.0, 0.615),
     'L0_mix_bfc': (0.0, 0.361),
     'L0_ffn_bg': (0.0, 0.428),
     'L0_ffn_b1': (0.0, 0.8),
     'L0_ffn_b2': (0.0, 0.1),
     'L1_gnn_b1': (0.0, 1.122),
     'L1_gnn_b2': (0.0, 0.635),
     'L1_mix_b_qkv': (0.0, 0.1),
     'L1_mix_kln_g': (1.0, 0.2),
     'L1_mix_kln_b': (0.0, 0.294),
     'L1_mix_vln_g': (1.0, 0.2),
     'L1_mix_vln_b': (0.0, 0.1),
     'L1_mix_b1': (0.0, 0.58),
     'L1_mix_b2': (0.0, 0.465),
     'L1_ffn_gate_b': (0.0, 0.349),
     'L1_ffn_b1': (0.0, 2.0),
     'L1_ffn_b2': (0.0, 2.0)}
    factors = {'L0_gnn_b_l': 23.576,
     'L0_gnn_b_r': 200.0,
     'L0_gnn_bias': 22.747,
     'L0_mix_Wq': 4.247,
     'L0_mix_Wk': 5.553,
     'L0_mix_Wv': 5.551,
     'L0_mix_Wfc': 4.192,
     'L0_gnn_W_r': 2.947,
     'L1_ffn_w1': 3.592}
    for name, (base, spread) in spreads.items():
        noise = np.random.default_rng([zlib.crc32(name.encode()), seed]).standard_normal(out[name].shape)
        drawn = base * np.exp(spread * noise) if base else spread * noise
        out[name] = jnp.asarray(drawn.astype(out[name].dtype))
    for name, factor in factors.items():
        out[name] = (out[name] * factor).astype(out[name].dtype)
    return out
```

```python
from contextlib import ExitStack

import numpy as np

import concourse.bass as bass
from concourse import mybir

ALU = mybir.AluOpType
ACT = mybir.ActivationFunctionType
AX = mybir.AxisListType
F32 = mybir.dt.float32
I32 = mybir.dt.int32
U32 = mybir.dt.uint32

P = 128
N = 6250
D = 256
E = 100000
H = 8
HC = D // H
KC = D // P
NB = (N + P - 1) // P
LAST = N - (NB - 1) * P
NP = NB * P
NT = (E + P - 1) // P
EP = NT * P
GS = 8
NG = (NT + NB - 1 + GS - 1) // GS
NG += NG % 2
NS = NG * GS
SJ = (NS + P - 1) // P
SPAD = SJ * P
LW = D + H
AW = D + H + 2
CH = P // H
CS = NS // CH
CL = CS * P
MASKED = -1.0e30
EPS = 1e-5
SLOPE = 0.2
MH = 64
NE = 8
F0 = 512
T0 = (2 * N) // P + 1 + NE - 1
T0 += T0 % 2
F1 = 1024
CAP = -(-5 * N // (4 * NE))
CT = (CAP + P - 1) // P
FMAX = 3.4028234e38
assert NS % CH == 0 and LAST < P and NB % 7 == 0


class Chain:

    def __init__(self, eng, sem):
        self.eng, self.sem, self.base, self.n, self.first = eng, sem, 0, 0, 0

    def did(self, ins):
        ins.then_inc(self.sem, 1)
        self.n += 1

    def sync(self):
        self.eng.wait_ge(self.sem, self.base + self.n)

    def begin(self, per):
        self.first, self.per, self.n = self.base + self.n, per, 0

    def at(self, k):
        self.base, self.n = self.first + k * self.per, 0

    def end(self, steps):
        assert self.n == self.per, (self.n, self.per)
        self.base, self.n = self.first + steps * self.per, 0


def pipeline(eng, count, unroll, *stages):
    stages = [(stage + (count,))[0:3] for stage in stages]
    most = max(lag for lag, _, _ in stages)

    def emit(k):
        for lag, work, n in stages:
            if 0 <= k - lag < n:
                work(k - lag, (k - lag) % unroll, (k - lag) // unroll)

    first = -(-most // unroll) + 1
    last = min(n for _, _, n in stages) // unroll
    if last - first < 2:
        first = last = 0
    for k in range(first * unroll):
        emit(k)
    if last > first:
        with eng.Fori(first, last) as i:
            for j in range(unroll):
                for lag, work, _ in stages:
                    work(i * unroll + (j - lag), (j - lag) % unroll, i + (j - lag) // unroll)
    for k in range(last * unroll, count + most):
        emit(k)


def at_least(k, n):
    return not isinstance(k, int) or k >= n


class Chip:
    pass


def end_stage(nc, m):
    nc.clear_and_free_semaphores(m.live)
    m.live.clear()
    nc.all_engine_barrier()


def edge_steps(nc, m, a):
    with ExitStack() as ctx:
        def sb(name, shape, dt=F32):
            return ctx.enter_context(nc.sbuf_tensor("es_" + name, shape, dt))

        def ps(name):
            return ctx.enter_context(nc.psum_tensor("es_" + name, [P, 512], F32))

        pads = sb("pads", [1, 2, EP - E], I32)
        padw = sb("padw", [1, EP - E])
        ends = sb("ends", [1, 2, NT], I32)
        endb = sb("endb", [1, 2, NT], I32)
        endf = sb("endf", [1, 2, NT])
        zero = sb("zero", [1, NT])
        inc = sb("inc", [1, NT])
        row = sb("row", [1, 2, NT])
        ones = sb("ones", [1, P])
        bc = sb("bc", [P, 2, NT])
        tio = m.big1[:, 0:NT]
        junk = m.big1[:, NT:2 * NT]
        sval = sb("sval", [P, SJ])
        cnt = sb("cnt", [P, SJ])
        tsel = sb("tsel", [P, SJ])
        qsel = sb("qsel", [P, SJ])
        breal = sb("breal", [P, SJ])
        boff = sb("boff", [P, SJ])
        bcl = sb("bcl", [P, SJ])
        bint = sb("bint", [P, SJ], I32)
        tidx = sb("tidx", [P, SJ], U32)
        rs = sb("rs", [P, SJ, P], I32)
        rd = sb("rd", [P, SJ, P], I32)
        rw = m.big0[:, 0:SPAD].rearrange("p (j e) -> p j e", e=P)
        fs = m.big0[:, SPAD:2 * SPAD].rearrange("p (j e) -> p j e", e=P)
        fd = m.big0[:, 2 * SPAD:3 * SPAD].rearrange("p (j e) -> p j e", e=P)
        fl = m.big0[:, 3 * SPAD:4 * SPAD].rearrange("p (j e) -> p j e", e=P)
        bank = [ps(f"bank{i}") for i in range(4)]

        copied, padset = m.sem("es_copied"), m.sem("es_padset")
        padded, endsin, planned = m.sem("es_padded"), m.sem("es_endsin"), m.sem("es_planned")
        spread, spreadback, ioted = m.sem("es_spread"), m.sem("es_spreadback"), m.sem("es_ioted")
        rowsin, stored, floats = m.sem("es_rowsin"), m.sem("es_stored"), m.sem("es_floats")
        turned, turnedback, chain = m.sem("es_turned"), m.sem("es_turnedback"), m.sem("es_chain")
        identset = m.sem("es_identset")
        zeroset, zeroed = m.sem("es_zeroset"), m.sem("es_zeroed")
        ndst, ZT = NT // 2, 16
        zeros = m.big1[:, 2 * CL - ZT * D:2 * CL]

        with nc.Block() as block:
            @block.sync
            def _(sp):
                sp.dma_start(m.src_p[0:E].rearrange("(a n) -> a n", a=16), a["src"].rearrange("(a n) -> a n", a=16)).then_inc(copied, 16)
                sp.dma_start(m.dst_p[0:E].rearrange("(a n) -> a n", a=16), a["dst"].rearrange("(a n) -> a n", a=16)).then_inc(copied, 16)
                sp.dma_start(m.w_p[0:E].rearrange("(a n) -> a n", a=16), a["edge_weight"].rearrange("(a n) -> a n", a=16)).then_inc(copied, 16)
                sp.wait_ge(padset, 3)
                sp.dma_start(m.src_p[E:EP].rearrange("(a n) -> a n", a=1), pads[:, 0, :]).then_inc(padded, 16)
                sp.dma_start(m.dst_p[E:EP].rearrange("(a n) -> a n", a=1), pads[:, 1, :]).then_inc(padded, 16)
                sp.dma_start(m.w_p[E:EP].rearrange("(a n) -> a n", a=1), padw[:, :]).then_inc(padded, 16)
                sp.wait_ge(copied, 48)
                sp.wait_ge(padded, 48)
                tiles = m.dst_p.rearrange("(t e) -> e t", e=P)
                sp.dma_start(ends[:, 0, :], tiles[0:1, :], allow_slow_non_contiguous=True).then_inc(endsin, 16)
                sp.dma_start(ends[:, 1, :], tiles[P - 1:P, :], allow_slow_non_contiguous=True).then_inc(endsin, 16)
                sp.wait_ge(planned, 2)
                sp.dma_start(m.btab_d.rearrange("(j p) -> p j", p=P), bint[:, :], allow_slow_non_contiguous=True).then_inc(stored, 16)
                sp.wait_ge(floats, 1)
                sp.dma_start(m.key_d.rearrange("(j p) e -> p j e", p=P), fd[:, :, :]).then_inc(stored, 16)
                sp.wait_ge(stored, 32)
                sp.dma_start(m.btab[:, :], m.btab_d.rearrange("(a n) -> a n", a=1)).then_inc(stored, 16)
                sp.wait_ge(stored, 48)

            @block.scalar
            def _(act):
                act.wait_ge(zeroset, 1)
                n = 0
                for buf in (m.buf0_d, m.buf1_d):
                    rows = buf.shape[0] // P
                    for lo in range(0, rows, ZT):
                        hi = min(rows, lo + ZT)
                        act.dma_start(buf[lo * P:hi * P, :].rearrange("(p b) d -> p (b d)", p=P), zeros[:, 0:(hi - lo) * D]).then_inc(zeroed, 16)
                        n += 16
                act.wait_ge(zeroed, n)

            @block.gpsimd
            def _(pool):
                nc.gpsimd.memset(m.ident[:, :], 0.0).then_inc(identset, 1)
                pool.wait_ge(identset, 1)
                nc.gpsimd.affine_select(out=m.ident[:, :], in_=m.ident[:, :], compare_op=ALU.not_equal, fill=1.0,
                                        base=0, pattern=[[-1, P]], channel_multiplier=1).then_inc(ioted, 1)
                nc.gpsimd.iota(m.iota[:, :], [[1, P]], base=0, channel_multiplier=0,
                               allow_small_or_imprecise_dtypes=True).then_inc(ioted, 1)
                nc.gpsimd.iota(tio[:, :], [[1, NT]], base=0, channel_multiplier=0,
                               allow_small_or_imprecise_dtypes=True).then_inc(ioted, 1)
                nc.gpsimd.iota(sval[:, :], [[P, SJ]], base=0, channel_multiplier=1,
                               allow_small_or_imprecise_dtypes=True).then_inc(ioted, 1)
                pool.wait_ge(planned, 1)
                for j in range(SJ):
                    at = bass.IndirectOffsetOnAxis(ap=tidx[:, j:j + 1], axis=0)
                    for rows, table in ((rs, m.src_p), (rd, m.dst_p), (rw, m.w_p)):
                        nc.gpsimd.indirect_dma_start(rows[:, j, :], None, table.rearrange("(t e) -> t e", e=P), at)\
                            .then_inc(rowsin, 16)

            @block.vector
            def _(dve):
                c = Chain(dve, chain)
                nc.vector.memset(zeros, 0.0).then_inc(zeroset, 1)
                nc.vector.memset(pads[:, 0, :], 0).then_inc(padset, 1)
                nc.vector.memset(pads[:, 1, :], N).then_inc(padset, 1)
                nc.vector.memset(padw[:, :], 1.0).then_inc(padset, 1)
                c.did(nc.vector.memset(zero[:, :], 0.0))
                c.did(nc.vector.memset(ones[:, :], 1.0))
                dve.wait_ge(endsin, 32)
                c.did(nc.vector.tensor_scalar(endb[:, :, :], ends[:, :, :], 7, None, ALU.arith_shift_right))
                c.sync()
                c.did(nc.vector.tensor_copy(endf[:, :, :], endb[:, :, :]))
                c.sync()
                c.did(nc.vector.tensor_tensor(inc[:, :], endf[:, 1, :], endf[:, 0, :], ALU.subtract))
                c.sync()
                c.did(nc.vector.tensor_scalar(inc[:, :], inc[:, :], 1.0, None, ALU.add))
                c.sync()
                c.did(nc.vector.tensor_tensor_scan(row[:, 0, :], inc[:, :], zero[:, :], 0.0, ALU.add, ALU.add))
                c.sync()
                c.did(nc.vector.tensor_tensor(row[:, 0, :], row[:, 0, :], inc[:, :], ALU.subtract))
                c.sync()
                nc.vector.tensor_tensor(row[:, 1, :], endf[:, 0, :], row[:, 0, :], ALU.subtract).then_inc(spread, 1)
                dve.wait_ge(spreadback, 1)
                for i in range(4):
                    c.did(nc.vector.tensor_copy(bc[:, i // 2, (i % 2) * ndst:(i % 2 + 1) * ndst], bank[i][:, 0:ndst]))
                c.sync()
                dve.wait_ge(ioted, 4)
                for j in range(SJ):
                    c.did(nc.vector.tensor_scalar(junk[:, :], bc[:, 0, :], sval[:, j:j + 1], None, ALU.is_le, ALU.add,
                                                  accum_out=cnt[:, j:j + 1]))
                    c.sync()
                c.did(nc.vector.tensor_scalar(tsel[:, :], cnt[:, :], -1.0, None, ALU.add))
                c.sync()
                nc.vector.tensor_copy(tidx[:, :], tsel[:, :]).then_inc(planned, 1)
                for j in range(SJ):
                    c.did(nc.vector.scalar_tensor_tensor(junk[:, :], tio[:, :], tsel[:, j:j + 1], bc[:, 1, :],
                                                         ALU.is_equal, ALU.mult, accum_out=qsel[:, j:j + 1]))
                    c.sync()
                c.did(nc.vector.tensor_tensor(breal[:, :], qsel[:, :], sval[:, :], ALU.add))
                c.sync()
                c.did(nc.vector.tensor_scalar(boff[:, :], breal[:, :], float(P), None, ALU.mult))
                c.did(nc.vector.tensor_scalar(bcl[:, :], breal[:, :], float(NB - 1), None, ALU.min))
                c.sync()
                nc.vector.tensor_copy(bint[:, :], bcl[:, :]).then_inc(planned, 1)
                dve.wait_ge(rowsin, 16 * 3 * SJ)
                nc.vector.tensor_copy(fd[:, :, :], rd[:, :, :]).then_inc(floats, 1)
                nc.vector.tensor_copy(fs[:, :, :], rs[:, :, :]).then_inc(floats, 1)
                dve.wait_ge(floats, 1)
                for j in range(SJ):
                    ins = nc.vector.tensor_scalar(fl[:, j, :], fd[:, j, :], boff[:, j:j + 1], None, ALU.subtract)
                ins.then_inc(floats, 1)
                for q, (out, w) in enumerate(((m.src, 4), (m.src, 3), (m.dl, 4), (m.dl, 3), (m.w, 4), (m.w, 3))):
                    dve.wait_ge(turned, q + 1)
                    o = 4 * P * (q % 2)
                    nc.vector.tensor_copy(out[:, o:o + w * P], bank[q % 4][:, 0:w * P]).then_inc(turnedback, 1)

            @block.tensor
            def _(pe):
                pe.wait_ge(spread, 1)
                for i in range(4):
                    last = nc.tensor.matmul(bank[i][:, 0:ndst], ones[:, :], row[:, i // 2, (i % 2) * ndst:(i % 2 + 1) * ndst],
                                            start=True, stop=True)
                last.then_inc(spreadback, 1)
                pe.wait_ge(floats, 3)
                pe.wait_ge(ioted, 4)
                for q in range(6):
                    rows = (fs, fl, rw)[q // 2]
                    if q >= 4:
                        pe.wait_ge(turnedback, q - 3)
                    for i in range(4 if q % 2 == 0 else SJ - 4):
                        last = nc.tensor.transpose(bank[q % 4][:, i * P:(i + 1) * P], rows[:, 4 * (q % 2) + i, :], m.ident[:, :])
                    last.then_inc(turned, 1)


def blocks_of(nc, m, engine, step, n):
    return nc.values_load_multi_w_load_instructions(m.btab[0:1, bass.ds(step, n)], engines=(engine,), min_val=0, max_val=NB - 1)[1]


def experts_of(nc, m, engine, tile, n):
    return nc.values_load_multi_w_load_instructions(m.etab[0:1, bass.ds(tile, n)], engines=(engine,), min_val=0, max_val=NE - 1)[1]


def bc_row(vector, n=P):
    return vector.partition_broadcast(n)


def finish_stats(dve, act, which, nc, m, st, c, s_var, s_std):
    if which == 1:
        act.wait_ge(s_var, 1)
        nc.scalar.activation(m.tmp1[:, :], m.tmp0[:, :], ACT.Sqrt).then_inc(s_std, 1)
        return
    c.did(nc.vector.tensor_tensor(m.tmp0[:, :], st[:, :, 1], st[:, :, 4], ALU.subtract))
    c.did(nc.vector.tensor_tensor(m.tmp1[:, :], st[:, :, 2], st[:, :, 5], ALU.add))
    c.did(nc.vector.tensor_tensor(m.mean[:, :], st[:, :, 1], st[:, :, 4], ALU.add))
    c.sync()
    c.did(nc.vector.tensor_tensor(m.tmp0[:, :], m.tmp0[:, :], m.tmp0[:, :], ALU.mult))
    c.did(nc.vector.tensor_scalar(m.mean[:, :], m.mean[:, :], 0.5, None, ALU.mult))
    c.sync()
    c.did(nc.vector.scalar_tensor_tensor(m.tmp0[:, :], m.tmp0[:, :], D / 4.0, m.tmp1[:, :], ALU.mult, ALU.add))
    c.sync()
    nc.vector.tensor_scalar(m.tmp0[:, :], m.tmp0[:, :], 1.0 / D, EPS, ALU.mult, ALU.add).then_inc(s_var, 1)
    dve.wait_ge(s_std, 1)
    c.did(nc.vector.reciprocal(m.rstd[:, :], m.tmp1[:, :]))
    c.sync()


def project_nodes(nc, m, a):
    with ExitStack() as ctx:
        def sb(name, shape, dt=F32):
            return ctx.enter_context(nc.sbuf_tensor("pn_" + name, shape, dt))

        x = m.big1[:, 0:NB * D].rearrange("p (b d) -> p b d", d=D)
        xr = m.big0[:, 0:NB * LW].rearrange("p (b d) -> p b d", d=LW)
        m.xr = xr
        st = sb("st", [P, NB, 6])
        wl, wr, wkv = sb("wl", [P, KC, LW]), sb("wr", [P, KC, LW]), sb("wkv", [P, KC, 2 * D])
        wlt, wrt = sb("wlt", [P, KC, D]), sb("wrt", [P, KC, D])
        bl, br, bkv = sb("bl", [P, LW]), sb("br", [P, LW]), sb("bkv", [P, 2 * D])
        bcol = sb("bcol", [P, 2, KC])
        bwide = sb("bwide", [P, 2, KC, P])
        attc = sb("attc", [P, KC])
        attm = sb("attm", [P, KC, H])
        attl = sb("attl", [P, KC, H])
        xn = sb("xn", [P, 2, D])
        xt = sb("xt", [P, 2, D])
        xls = sb("xls", [P, 2, LW])
        kv = sb("kv", [P, 2, 2 * D])
        bank = [ctx.enter_context(nc.psum_tensor(f"pn_bank{i}", [P, 512], F32)) for i in range(8)]
        xt_ps, xl_ps, xr_ps, kv_ps, kvsum = bank[0:2], bank[2], bank[3], bank[4:6], bank[6:8]

        names = ("xin padz stats zeroed weights masked attset folded foldedback var std "
                 "xn_ready xn_free xt_made xt_ready xt_bank xt_used xtst0 xtst1 xl_made xr_made kv_made xl_back xr_back "
                 "kv_back xlst0 xlst1 kv_used kv_done chain consts").split()
        s = {n: m.sem("pn_" + n) for n in names}
        xt_stored, xl_stored = [s["xtst0"], s["xtst1"]], [s["xlst0"], s["xlst1"]]

        with nc.Block() as block:
            @block.sync
            def _(sp):
                sp.wait_ge(s["padz"], 1)
                for q in range(4):
                    lo, hi = q * (NB - 1) // 4, (q + 1) * (NB - 1) // 4
                    sp.dma_start(x[:, lo:hi, :], a["x"][lo * P:hi * P, :].rearrange("(b p) d -> p b d", p=P)).then_inc(s["xin"], 16)
                sp.dma_start(x[0:LAST, NB - 1, :], a["x"][(NB - 1) * P:N, :]).then_inc(s["xin"], 16)
                for out, w in ((wl[:, :, 0:D], "L0_gnn_W_l"), (wr[:, :, 0:D], "L0_gnn_W_r"),
                               (wkv[:, :, 0:D], "WkT"), (wkv[:, :, D:2 * D], "WvT"), (wlt[:, :, :], "W_lT"),
                               (wrt[:, :, :], "W_rT")):
                    sp.dma_start(out, a[w].rearrange("(c p) n -> p c n", p=P)).then_inc(s["weights"], 16)
                for out, w in ((bl[:, 0:D], "L0_gnn_b_l"), (br[:, 0:D], "L0_gnn_b_r"), (bkv[:, 0:D], "L0_mix_bk"),
                               (bkv[:, D:2 * D], "L0_mix_bv")):
                    sp.dma_start(out, a[w].partition_broadcast(P)).then_inc(s["weights"], 16)
                for out, w in ((bcol[:, 0, :], "L0_gnn_b_l"), (bcol[:, 1, :], "L0_gnn_b_r")):
                    sp.dma_start(out, a[w].rearrange("(c p) -> p c", p=P), allow_slow_non_contiguous=True).then_inc(s["weights"], 16)
                sp.dma_start(attc[:, :], a["L0_gnn_att"].rearrange("h c -> (h c)").rearrange("(c p) -> p c", p=P), allow_slow_non_contiguous=True).then_inc(s["weights"], 16)

                def store_xt(k, u, r):
                    sp.wait_ge(s["xt_ready"], k + 1)
                    sp.dma_start(m.xnt_d[k] if isinstance(k, int) else m.xnt_d[bass.ds(k, 1)].rearrange("a p d -> (a p) d"),
                                 xt[:, u, :]).then_inc(xt_stored[u], 16)

                def store_xl(k, u, r):
                    sp.wait_ge(s["xl_back"], k + 1)
                    sp.dma_start(m.xl_d[k] if isinstance(k, int) else m.xl_d[bass.ds(k, 1)].rearrange("a p d -> (a p) d"),
                                 xls[:, u, :]).then_inc(xl_stored[u], 16)
                pipeline(sp, NB, 2, (0, store_xt), (0, store_xl))
                for u in range(2):
                    sp.wait_ge(xt_stored[u], 16 * ((NB + 1 - u) // 2))
                    sp.wait_ge(xl_stored[u], 16 * ((NB + 1 - u) // 2))

            @block.gpsimd
            def _(pool):
                nc.gpsimd.memset(attm[:, :, :], 1.0).then_inc(s["masked"], 1)
                pool.wait_ge(s["masked"], 1)
                nc.gpsimd.affine_select(out=attm[:, :, :], in_=attm[:, :, :], compare_op=ALU.is_ge, fill=0.0, base=0,
                                        pattern=[[P, KC], [-HC, H]], channel_multiplier=1).then_inc(s["masked"], 1)
                pool.wait_ge(s["masked"], 2)
                nc.gpsimd.affine_select(out=attm[:, :, :], in_=attm[:, :, :], compare_op=ALU.is_ge, fill=0.0, base=HC - 1,
                                        pattern=[[-P, KC], [HC, H]], channel_multiplier=-1).then_inc(s["masked"], 1)

            @block.vector
            def _(dve):
                c = Chain(dve, s["chain"])
                nc.vector.memset(x[:, NB - 1, :], 0.0).then_inc(s["padz"], 1)
                dve.wait_ge(s["weights"], 16 * 13)
                dve.wait_ge(s["masked"], 3)
                for q in range(KC):
                    c.did(nc.vector.tensor_scalar(m.atta[:, q, :], attm[:, q, :], attc[:, q:q + 1], (1 - SLOPE) / 2,
                                                  ALU.mult, ALU.mult))
                    c.did(nc.vector.tensor_scalar(attl[:, q, :], attm[:, q, :], attc[:, q:q + 1], (1 + SLOPE) / 2,
                                                  ALU.mult, ALU.mult))
                    for w in range(2):
                        c.did(nc.vector.tensor_scalar(bwide[:, w, q, :], m.iota[:, :], 0.0, bcol[:, w, q:q + 1],
                                                      ALU.mult, ALU.add))
                c.sync()
                nc.vector.memset(m.ones[:, :], 1.0).then_inc(s["attset"], 1)
                dve.wait_ge(s["folded"], 1)
                for w, (wt, bt) in enumerate(((wl, bl), (wr, br))):
                    for q in range(KC):
                        c.did(nc.vector.tensor_copy(wt[:, q, D:LW], bank[w][:, H * q:H * q + H]))
                    c.did(nc.vector.tensor_copy(bt[:, D:LW], bank[w][:, H * KC:H * KC + H]))
                c.sync()
                nc.vector.memset(m.tmp0[:, 0:1], 0.0).then_inc(s["foldedback"], 1)
                dve.wait_ge(s["xin"], 16 * 5)
                for b in range(NB):
                    ins = nc.vector.bn_stats(st[:, b, :], x[:, b, :])
                c.did(ins)
                c.sync()
                finish_stats(dve, None, 0, nc, m, st, c, s["var"], s["std"])

                def normalise(k, u, r):
                    if at_least(k, 2):
                        dve.wait_ge(s["xt_made"], k - 1)
                    xk = x[:, k, :] if isinstance(k, int) else x[:, bass.ds(k, 1), :].rearrange("p a d -> p (a d)")
                    nc.vector.tensor_scalar(xn[:, u, :], xk, m.mean[:, bass.ds(k, 1)], m.rstd[:, bass.ds(k, 1)],
                                            ALU.subtract, ALU.mult).then_inc(s["xn_ready"], 1)

                def evacuate(k, u, r):
                    dve.wait_ge(s["xl_made"], k + 1)
                    if at_least(k, 2):
                        dve.wait_ge(xl_stored[u], 16 * r)
                    nc.vector.tensor_tensor(xls[:, u, :], xl_ps[:, 0:LW], bl[:, :], ALU.add).then_inc(s["xl_back"], 1)
                    dve.wait_ge(s["xr_made"], k + 1)
                    nc.vector.tensor_tensor(xr[:, bass.ds(k, 1), :].rearrange("p a d -> p (a d)"), xr_ps[:, 0:LW], br[:, :],
                                            ALU.add).then_inc(s["xr_back"], 1)
                    dve.wait_ge(s["kv_made"], k + 1)
                    if at_least(k, 2):
                        dve.wait_ge(s["kv_used"], k - 1)
                    nc.vector.tensor_tensor(kv[:, u, :], kv_ps[u][:, :], bkv[:, :], ALU.add).then_inc(s["kv_back"], 1)
                pipeline(dve, NB, 2, (0, normalise), (2, evacuate))
                dve.wait_ge(s["kv_used"], NB)
                for q in range(KC):
                    ins = nc.vector.tensor_copy(m.kvt[:, q, :], kvsum[q][:, 0:P])
                ins.then_inc(s["consts"], 1)

            @block.scalar
            def _(act):
                finish_stats(None, act, 1, nc, m, st, None, s["var"], s["std"])

                def evacuate(k, u, r):
                    act.wait_ge(s["xt_made"], k + 1)
                    if at_least(k, 2):
                        act.wait_ge(s["kv_made"], k - 1)
                        act.wait_ge(xt_stored[u], 16 * r)
                    nc.scalar.copy(xt[:, u, :], xt_ps[u][:, 0:D]).then_inc(s["xt_ready"], 1)
                pipeline(act, NB, 2, (0, evacuate))

            @block.tensor
            def _(pe):
                pe.wait_ge(s["attset"], 1)
                for w, wt in enumerate((wlt, wrt)):
                    for q in range(KC):
                        for h in range(KC):
                            nc.tensor.matmul(bank[w][:, H * q:H * q + H], wt[:, h, q * P:(q + 1) * P], attl[:, h, :],
                                             start=(h == 0), stop=(h == KC - 1))
                    for h in range(KC):
                        last = nc.tensor.matmul(bank[w][:, H * KC:H * KC + H], bwide[:, w, h, :], attl[:, h, :],
                                                start=(h == 0), stop=(h == KC - 1))
                last.then_inc(s["folded"], 1)
                pe.wait_ge(s["foldedback"], 1)

                def turn(k, u, r):
                    pe.wait_ge(s["xn_ready"], k + 1)
                    if at_least(k, 2):
                        pe.wait_ge(s["xt_ready"], k - 1)
                    for q in range(KC):
                        last = nc.tensor.transpose(xt_ps[u][:, q * P:(q + 1) * P], xn[:, u, q * P:(q + 1) * P], m.ident[:, :])
                    last.then_inc(s["xt_made"], 1)

                def project(k, u, r):
                    pe.wait_ge(s["xt_ready"], k + 1)
                    for out, w, n, made, back in ((xl_ps, wl, LW, "xl_made", "xl_back"), (xr_ps, wr, LW, "xr_made", "xr_back"),
                                                  (kv_ps[u], wkv, 2 * D, "kv_made", None)):
                        if back and at_least(k, 1):
                            pe.wait_ge(s[back], k)
                        if not back and at_least(k, 2):
                            pe.wait_ge(s["kv_back"], k - 1)
                        for q in range(KC):
                            last = nc.tensor.matmul(out[:, 0:n], xt[:, u, q * P:(q + 1) * P], w[:, q, :],
                                                    start=(q == 0), stop=(q == KC - 1))
                        last.then_inc(s[made], 1)

                def sum_kv(k, u, r):
                    rows = LAST if isinstance(k, int) and k == NB - 1 else P
                    first, final = isinstance(k, int) and k == 0, isinstance(k, int) and k == NB - 1
                    pe.wait_ge(s["kv_back"], k + 1)
                    for q in range(KC):
                        last = nc.tensor.matmul(kvsum[q][:, 0:P], kv[0:rows, u, D + q * P:D + (q + 1) * P],
                                                kv[0:rows, u, q * P:(q + 1) * P], start=first, stop=final)
                    last.then_inc(s["kv_used"], 1)
                pipeline(pe, NB, 2, (0, turn), (1, project), (3, sum_kv))



def score_edges(nc, m, a):
    with ExitStack() as ctx:
        def sb(name, shape, dt=F32):
            return ctx.enter_context(nc.sbuf_tensor("se_" + name, shape, dt))

        def ps(name, shape):
            return ctx.enter_context(nc.psum_tensor("se_" + name, shape, F32))

        GP = GS // 2
        HS = GS // 2
        idx = sb("idx", [P, 4, HS], U32)
        xj = sb("xj", [P, 2, GS, LW])
        half_of = lambda u: xj[:, u // 2, (u % 2) * HS:(u % 2 + 1) * HS, :]
        oh = sb("oh", [P, 2, GS, P])
        oht = sb("oht", [P, 2, GS, P])
        z = sb("z", [P, 2, GS, LW])
        zt = sb("zt", [P, 2, 512])
        oht_ps = ps("oht_ps", [P, 512])
        z_ps = [ps(f"z_ps{i}", [P, 2, 512]) for i in range(2)]
        zt_ps = [ps(f"zt_ps{i}", [P, 512]) for i in range(2)]
        al_ps = ps("al_ps", [P, 512])
        s = {n: m.sem("se_" + n) for n in
             "indexed issued xj0 xj1 xj2 xj3 st0 st1 st2 st3 oh_ready oht_made oht_ready z_made z_ready zt_made zt_ready att_made al_ready keys".split()}
        landed, stored = [s[f"xj{u}"] for u in range(4)], [s[f"st{u}"] for u in range(4)]
        key = m.big1[:, 0:CL]
        table = m.xl_d.rearrange("b p d -> (b p) d")

        with nc.Block() as block:
            @block.gpsimd
            def _(pool):
                def gather(h, u, r):
                    if at_least(h, 4):
                        pool.wait_ge(landed[u], 16 * HS * r)
                        pool.wait_ge(s["z_ready"], 2 * h - 6)
                        pool.wait_ge(stored[u], 16 * r)
                    nc.gpsimd.tensor_copy(idx[:, u, :], m.src[:, bass.ds(h * HS, HS)]).then_inc(s["indexed"], 1)
                    pool.wait_ge(s["indexed"], h + 1)
                    pool.sem_inc(s["issued"], 1)
                    for k in range(HS):
                        nc.gpsimd.indirect_dma_start(half_of(u)[:, k, :], None, table,
                                                     bass.IndirectOffsetOnAxis(ap=idx[:, u, k:k + 1], axis=0)).then_inc(landed[u], 16)
                pipeline(pool, 2 * NG, 4, (0, gather))

            @block.sync
            def _(sp):
                kd = m.key_d[0:NS, :].rearrange("(c j) e -> c (j e)", c=CH)
                for c in range(CH):
                    sp.dma_start(key[c * H:(c + 1) * H, :], kd[c].partition_broadcast(H)).then_inc(s["keys"], 16)

                def store(h, u, r):
                    sp.wait_ge(landed[u], 16 * HS * (r + 1))
                    sp.dma_start(m.xj_d[bass.ds(h, 1)].rearrange("a p n -> (a p) n"),
                                 half_of(u).rearrange("p k d -> p (k d)")).then_inc(stored[u], 16)
                pipeline(sp, 2 * NG, 4, (0, store))
                sp.wait_ge(s["keys"], 16 * CH)
                for u in range(4):
                    sp.wait_ge(stored[u], 16 * (2 * NG // 4))

            @block.vector
            def _(dve):
                def one_hot(q, v, r):
                    if v % GP:
                        return
                    u, g = v // GP, 2 * r + v // GP
                    if at_least(q, 2 * GP):
                        dve.wait_ge(s["oht_made"], 2 * (g - 1))
                    nc.vector.tensor_tensor(oh[:, u, :, :], m.iota[:, :].unsqueeze(1).to_broadcast([P, GS, P]),
                                            m.dl[:, bass.ds(g * GS, GS)].unsqueeze(2).to_broadcast([P, GS, P]),
                                            ALU.is_equal).then_inc(s["oh_ready"], 1)

                def add(q, v, r):
                    u, k = v // GP, 2 * (v % GP)
                    if v % 2 == 0:
                        dve.wait_ge(landed[v // 2], 16 * HS * (r + 1))
                    if v % GP == 0:
                        if at_least(q, 2 * GP):
                            dve.wait_ge(s["al_ready"], 2 * r + v // GP - 1)
                    dve.wait_ge(s["z_made"], q + 1)
                    if at_least(q, 2 * GP):
                        dve.wait_ge(s["zt_made"], q - (2 * GP - 1))
                    nc.vector.tensor_tensor(z[:, u, k:k + 2, :], z_ps[v % 2][:, :, 0:LW], xj[:, u, k:k + 2, :],
                                            ALU.add).then_inc(s["z_ready"], 1)

                def scores(q, v, r):
                    if v % GP != GP - 1:
                        return
                    u, g = v // GP, 2 * r + v // GP
                    dve.wait_ge(s["att_made"], q + 1)
                    dve.wait_ge(s["z_ready"], q + 1)
                    nc.vector.tensor_tensor(m.ex[:, bass.ds(g * GS * H, GS * H)].rearrange("p (k h) -> p k h", h=H),
                                            al_ps[:, 0:GS * H].rearrange("p (k h) -> p k h", h=H), z[:, u, :, D:LW],
                                            ALU.add).then_inc(s["al_ready"], 1)
                pipeline(dve, NS // 2, 2 * GP, (7, scores), (0, one_hot), (3, add))

            @block.scalar
            def _(act):
                def one_hot_turned(q, v, r):
                    if v % 2:
                        return
                    u, g, half = v // GP, 2 * r + v // GP, (v % GP) // 2
                    act.wait_ge(s["oht_made"], 2 * g + half + 1)
                    if at_least(q, 2 * GP):
                        act.wait_ge(s["z_made"], GP * (g - 1))
                    nc.scalar.copy(oht[:, u, 4 * half:4 * half + 4, :].rearrange("p k n -> p (k n)"), oht_ps[:, :]).then_inc(s["oht_ready"], 1)

                def absolute(q, v, r):
                    act.wait_ge(s["zt_made"], q + 1)
                    if at_least(q, 2):
                        act.wait_ge(s["att_made"], q - 1)
                    nc.scalar.activation(zt[:, v % 2, :], zt_ps[v % 2][:, :], ACT.Abs).then_inc(s["zt_ready"], 1)
                pipeline(act, NS // 2, 2 * GP, (0, one_hot_turned), (5, absolute))

            @block.tensor
            def _(pe):
                def turn_one_hot(q, v, r):
                    if v % 2:
                        return
                    u, g, half = v // GP, 2 * r + v // GP, (v % GP) // 2
                    pe.wait_ge(s["oh_ready"], g + 1)
                    if at_least(q, 2):
                        pe.wait_ge(s["oht_ready"], 2 * g + half)
                    for k in range(4):
                        last = nc.tensor.transpose(oht_ps[:, k * P:(k + 1) * P], oh[:, u, 4 * half + k, :], m.ident[:, :])
                    last.then_inc(s["oht_made"], 1)

                def expand(q, v, r):
                    u, k = v // GP, 2 * (v % GP)
                    g = 2 * r + v // GP
                    pe.wait_ge(s["oht_ready"], 2 * g + (v % GP) // 2 + 1)
                    if at_least(q, 2):
                        pe.wait_ge(s["z_ready"], q - 1)
                    blocks = blocks_of(nc, m, mybir.EngineType.PE, q * 2, 2)
                    for i in range(2):
                        last = nc.tensor.matmul(z_ps[v % 2][:, i, 0:LW], oht[:, u, k + i, :], of_block(m.xr, blocks[i]),
                                                start=True, stop=True)
                    last.then_inc(s["z_made"], 1)

                def turn(q, v, r):
                    u, k = v // GP, 2 * (v % GP)
                    pe.wait_ge(s["z_ready"], q + 1)
                    if at_least(q, 2):
                        pe.wait_ge(s["zt_ready"], q - 1)
                    for i in range(2):
                        for c in range(KC):
                            last = nc.tensor.transpose(zt_ps[v % 2][:, i * D + c * P:i * D + (c + 1) * P],
                                                       z[:, u, k + i, c * P:(c + 1) * P], m.ident[:, :])
                    last.then_inc(s["zt_made"], 1)

                def attend(q, v, r):
                    k, g = 2 * (v % GP), 2 * r + v // GP
                    pe.wait_ge(s["zt_ready"], q + 1)
                    if v % GP == 0 and at_least(q, GP):
                        pe.wait_ge(s["al_ready"], g)
                    for i in range(2):
                        for c in range(KC):
                            last = nc.tensor.matmul(al_ps[:, (k + i) * H:(k + i + 1) * H],
                                                    zt[:, v % 2, i * D + c * P:i * D + (c + 1) * P], m.atta[:, c, :],
                                                    start=(c == 0), stop=(c == KC - 1))
                    last.then_inc(s["att_made"], 1)
                pipeline(pe, NS // 2, 2 * GP, (0, turn_one_hot), (2, expand), (4, turn), (6, attend))



def normalise_edges(nc, m, a):
    with ExitStack() as ctx:
        def sb(name, shape, dt=F32):
            return ctx.enter_context(nc.sbuf_tensor("ne_" + name, shape, dt))

        small, lnw, empty = sb("small", [P, NS]), sb("lnw", [P, NS]), sb("empty", [P, NS])
        cols = sb("cols", [P, 4])
        cki, carry = sb("cki", [P, 1]), sb("carry", [P, 2])
        rows = sb("rows", [1, 6, P])
        bank = [ctx.enter_context(nc.psum_tensor(f"ne_bank{i}", [P, 512], F32)) for i in range(4)]
        s = {n: m.sem("ne_" + n) for n in "w ln logw turned back cols rowps rows colps exps exped unturned done chain".split()}
        key, run = m.big1[:, 0:CL], m.big1[:, CL:2 * CL + 1]
        al, top = m.big0[:, 0:CL], m.big0[:, CL:2 * CL]
        exv = m.ex[:, :].rearrange("p (c j h) -> p c j h", c=CH, h=H)
        NQ4 = CS // 4
        assert CS % 4 == 0

        with nc.Block() as block:
            @block.vector
            def _(dve):
                c = Chain(dve, s["chain"])
                V = nc.vector
                w = m.w[:, 0:NS]
                c.did(V.tensor_scalar(small[:, :], w, 2.0 ** -60, None, ALU.is_lt))
                c.did(V.tensor_scalar(empty[:, :], w, 0.0, MASKED, ALU.is_le, ALU.mult))
                c.sync()
                c.did(V.tensor_scalar(lnw[:, :], small[:, :], 2.0 ** 60, 1.0, ALU.mult, ALU.add))
                c.sync()
                c.did(V.tensor_tensor(lnw[:, :], lnw[:, :], w, ALU.mult))
                c.sync()
                V.tensor_scalar(lnw[:, :], lnw[:, :], 2.0 ** -63, None, ALU.max).then_inc(s["w"], 1)
                c.did(V.memset(run[:, 0:1], 0.0))
                c.did(V.memset(run[:, CL:CL + 1], 0.0))
                c.did(V.tensor_tensor(run[:, 1:CL], key[:, 1:CL], key[:, 0:CL - 1], ALU.is_equal))
                c.sync()
                c.did(V.tensor_scalar(run[:, 1:CL], run[:, 1:CL], -1.0, -MASKED, ALU.add, ALU.mult))
                dve.wait_ge(s["ln"], 1)
                c.did(V.scalar_tensor_tensor(lnw[:, :], small[:, :], -60.0 * float(np.log(2.0)), lnw[:, :], ALU.mult, ALU.add))
                c.sync()
                c.did(V.tensor_tensor(lnw[:, :], lnw[:, :], empty[:, :], ALU.add))
                c.sync()
                V.tensor_tensor(top.rearrange("p (j c h) -> p c j h", c=CH, h=H), exv,
                                lnw[:, :].rearrange("p (c j) -> p c j", c=CH).unsqueeze(3).to_broadcast([P, CH, CS, H]),
                                ALU.add).then_inc(s["logw"], 1)
                for q in range(NQ4):
                    dve.wait_ge(s["turned"], q + 1)
                    V.tensor_copy(al[:, q * 512:(q + 1) * 512], bank[q % 4][:, :]).then_inc(s["back"], 1)
                dve.wait_ge(s["back"], NQ4)
                dve.wait_ge(s["turned"], NQ4)
                c.sync()

                def scan(out, forward, initial):
                    if forward:
                        c.did(V.tensor_tensor_scan(out, run[:, 0:CL], al, initial, ALU.add, ALU.max))
                    else:
                        c.did(V.tensor_tensor_scan(out[:, ::-1], run[:, 1:CL + 1][:, ::-1], top[:, ::-1], initial, ALU.add, ALU.max))
                    c.sync()

                c.did(V.tensor_copy(cols[:, 1:2], key[:, 0:1]))
                c.did(V.tensor_copy(cols[:, 2:3], key[:, CL - 1:CL]))
                c.sync()
                for turn, (out, forward) in enumerate(((top, True), (key, False))):
                    scan(out, forward, MASKED)
                    V.tensor_copy(cols[:, 0:1], out[:, CL - 1:CL] if forward else out[:, 0:1]).then_inc(s["cols"], 1)
                    dve.wait_ge(s["rowps"], turn + 1)
                    for i in range(3):
                        v = bank[0][0:1, i * P:(i + 1) * P].rearrange("a (c h) -> a h c", h=H)
                        c.did(V.tensor_copy(rows[:, i, :].rearrange("a (h c) -> a h c", h=H), v if forward else v[:, :, ::-1]))
                    c.sync()
                    far, near = (rows[:, 2, :], rows[:, 1, :]) if forward else (rows[:, 1, :], rows[:, 2, :])
                    hc = lambda r: r.rearrange("a (h c) -> a h c", h=H)
                    c.did(V.memset(rows[:, 3, :], 0.0))
                    c.sync()
                    c.did(V.tensor_tensor(hc(rows[:, 3, :])[:, :, 1:CH], hc(near)[:, :, 1:CH], hc(far)[:, :, 0:CH - 1], ALU.is_equal))
                    c.did(V.tensor_tensor(rows[:, 4, :], near, far, ALU.is_equal))
                    c.sync()
                    c.did(V.tensor_tensor(rows[:, 4, :], rows[:, 4, :], rows[:, 3, :], ALU.mult))
                    c.sync()
                    c.did(V.tensor_scalar(rows[:, 3:5, :], rows[:, 3:5, :], -1.0, -MASKED, ALU.add, ALU.mult))
                    c.sync()
                    c.did(V.tensor_tensor_scan(rows[:, 5, :], rows[:, 4, :], rows[:, 0, :], MASKED, ALU.add, ALU.max))
                    c.did(V.memset(rows[:, 1, :], MASKED))
                    c.sync()
                    c.did(V.tensor_tensor(hc(rows[:, 1, :])[:, :, 1:CH], hc(rows[:, 5, :])[:, :, 0:CH - 1],
                                          hc(rows[:, 3, :])[:, :, 1:CH], ALU.add))
                    c.sync()
                    v = rows[:, 2, :].rearrange("a (c h) -> a h c", h=H)
                    V.tensor_copy(v if forward else v[:, :, ::-1], hc(rows[:, 1, :])).then_inc(s["rows"], 1)
                    dve.wait_ge(s["colps"], turn + 1)
                    c.did(V.tensor_copy(carry[:, turn:turn + 1], bank[1][:, 0:1]))
                    c.sync()
                    scan(out, forward, carry[:, turn:turn + 1])
                for q in range(4):
                    o = slice(q * CL // 4, (q + 1) * CL // 4)
                    V.tensor_tensor(al[:, o], al[:, o], key[:, o], ALU.subtract).then_inc(s["exps"], 1)
                for q in range(NQ4):
                    dve.wait_ge(s["unturned"], q + 1)
                    V.tensor_copy(exv[:, :, 4 * q:4 * q + 4, :].rearrange("p c j h -> p j c h"),
                                  bank[q % 4][:, :].rearrange("p (j c h) -> p j c h", j=4, h=H)).then_inc(s["done"], 1)

            @block.scalar
            def _(act):
                act.wait_ge(s["w"], 1)
                nc.scalar.activation(lnw[:, :], lnw[:, :], ACT.Ln).then_inc(s["ln"], 1)
                for q in range(4):
                    act.wait_ge(s["exps"], q + 1)
                    o = slice(q * CL // 4, (q + 1) * CL // 4)
                    nc.scalar.activation(al[:, o], al[:, o], ACT.Exp).then_inc(s["exped"], 1)

            @block.tensor
            def _(pe):
                pe.wait_ge(s["logw"], 1)
                for q in range(NQ4):
                    if q >= 4:
                        pe.wait_ge(s["back"], q - 3)
                    for i in range(4):
                        last = nc.tensor.transpose(bank[q % 4][:, i * P:(i + 1) * P], top[:, (4 * q + i) * P:(4 * q + i + 1) * P], m.ident[:, :])
                    last.then_inc(s["turned"], 1)
                for turn in range(2):
                    pe.wait_ge(s["cols"], turn + 1)
                    for i in range(3):
                        last = nc.tensor.matmul(bank[0][0:1, i * P:(i + 1) * P], cols[:, i:i + 1], m.ident[:, :], start=True, stop=True)
                    last.then_inc(s["rowps"], 1)
                    pe.wait_ge(s["rows"], turn + 1)
                    nc.tensor.matmul(bank[1][:, 0:1], rows[:, 2, :], m.ones[0:1, 0:1], start=True, stop=True).then_inc(s["colps"], 1)
                for q in range(NQ4):
                    if q >= 4:
                        pe.wait_ge(s["done"], q - 3)
                    pe.wait_ge(s["exped"], min(4, (512 * (q + 1) * 4 - 1) // CL + 1))
                    for i in range(4):
                        j = 4 * q + i
                        last = nc.tensor.transpose(bank[q % 4][:, i * P:(i + 1) * P], al[:, j * P:(j + 1) * P], m.ident[:, :])
                    last.then_inc(s["unturned"], 1)


def aggregate_edges(nc, m, a):
    with ExitStack() as ctx:
        def sb(name, shape, dt=F32):
            return ctx.enter_context(nc.sbuf_tensor("ae_" + name, shape, dt))

        v = sb("v", [P, 3, GS, AW])
        oh = sb("oh", [P, 2, GS, P])
        bank = [ctx.enter_context(nc.psum_tensor(f"ae_bank{i}", [P, 512], F32)) for i in range(8)]
        acc = m.big1[:, 0:NB * AW].rearrange("p (b d) -> p b d", d=AW)
        m.acc = acc
        acc1 = m.big0[:, 0:NB * AW].rearrange("p (b d) -> p b d", d=AW)
        s = {n: m.sem("ae_" + n) for n in "in0 in1 in2 oh_ready low_ready high_ready ex_ready summed added zeroed".split()}
        landed = [s["in0"], s["in1"], s["in2"]]
        LOW = 3
        U = 6

        def exps(g, k0, k1):
            return m.ex[:, bass.ds((g * GS + k0) * H, (k1 - k0) * H)].rearrange("p (k h) -> p k h", h=H)

        def scaled(u, g, k0, k1):
            x = v[:, u, k0:k1, 0:D].rearrange("p k (h c) -> p k h c", h=H)
            return x, exps(g, k0, k1).unsqueeze(3).to_broadcast([P, k1 - k0, H, HC])

        with nc.Block() as block:
            @block.sync
            def _(sp):
                sp.wait_ge(s["zeroed"], 2)

                def load(g, w, r):
                    if at_least(g, 3):
                        sp.wait_ge(s["summed"], GS * (g - 2))
                    for i in range(2):
                        sp.dma_start(v[:, w % 3, i * GS // 2:(i + 1) * GS // 2, 0:LW],
                                     m.xj_d[bass.ds(2 * g + i, 1)].rearrange("a p (k d) -> (a p) k d", d=LW)).then_inc(landed[w % 3], 16)
                pipeline(sp, NG, U, (0, load))

            @block.scalar
            def _(act):
                def weights(g, w, r):
                    act.wait_ge(landed[w % 3], 32 * (2 * r + w // 3 + 1))
                    nc.scalar.copy(v[:, w % 3, :, D:LW], exps(g, 0, GS)).then_inc(s["ex_ready"], 1)
                pipeline(act, NG, U, (0, weights))

            @block.gpsimd
            def _(pool):
                def scale_high(g, w, r):
                    pool.wait_ge(landed[w % 3], 32 * (2 * r + w // 3 + 1))
                    x, ex = scaled(w % 3, g, LOW, GS)
                    nc.gpsimd.tensor_tensor(x, x, ex, ALU.mult).then_inc(s["high_ready"], 1)
                pipeline(pool, NG, U, (0, scale_high))

            @block.vector
            def _(dve):
                V = nc.vector
                V.memset(v[:, :, :, LW:AW], 1.0).then_inc(s["zeroed"], 1)
                V.memset(acc[:, :, :], 0.0).then_inc(s["zeroed"], 1)
                V.memset(acc1[:, :, :], 0.0).then_inc(s["zeroed"], 1)
                dve.wait_ge(s["zeroed"], 3)

                def prepare(g, w, r):
                    if at_least(g, 2):
                        dve.wait_ge(s["summed"], GS * (g - 1))
                    V.tensor_tensor(oh[:, w % 2, :, :], m.iota[:, :].unsqueeze(1).to_broadcast([P, GS, P]),
                                    m.dl[:, bass.ds(g * GS, GS)].unsqueeze(2).to_broadcast([P, GS, P]),
                                    ALU.is_equal).then_inc(s["oh_ready"], 1)
                    dve.wait_ge(landed[w % 3], 32 * (2 * r + w // 3 + 1))
                    x, ex = scaled(w % 3, g, 0, LOW)
                    V.tensor_tensor(x, x, ex, ALU.mult).then_inc(s["low_ready"], 1)

                def add(g, w, r):
                    blocks = blocks_of(nc, m, mybir.EngineType.DVE, g * GS, GS)
                    for k in range(GS):
                        t = g * GS + k
                        dve.wait_ge(s["summed"], t + 1)
                        if at_least(t, 2):
                            dve.wait_ge(s["added"], t - 1)
                        to = of_block((acc, acc1)[k % 2], blocks[k])
                        V.tensor_tensor(to, to, bank[k][:, 0:AW], ALU.add).then_inc(s["added"], 1)
                pipeline(dve, NG, U, (0, prepare), (1, add))
                dve.wait_ge(s["added"], NS)
                V.tensor_tensor(acc[:, :, :], acc[:, :, :], acc1[:, :, :], ALU.add)

            @block.tensor
            def _(pe):
                def total(g, w, r):
                    pe.wait_ge(s["oh_ready"], g + 1)
                    pe.wait_ge(s["ex_ready"], g + 1)
                    pe.wait_ge(s["low_ready"], g + 1)
                    for k in range(GS):
                        if k == LOW:
                            pe.wait_ge(s["high_ready"], g + 1)
                        if at_least(g, 1):
                            pe.wait_ge(s["added"], GS * (g - 1) + k + 1)
                        nc.tensor.matmul(bank[k][:, 0:AW], oh[:, w % 2, k, :], v[:, w % 3, k, :], start=True, stop=True)\
                            .then_inc(s["summed"], 1)
                pipeline(pe, NG, U, (0, total))


def block_rows(table, k):
    return table[bass.ds(k, 1)].rearrange("a p d -> (a p) d")


def of_block(t, k):
    return t[:, bass.ds(k, 1), :].rearrange("p a d -> p (a d)")


def finish_attention(nc, m, a):
    with ExitStack() as ctx:
        def sb(name, shape, dt=F32):
            return ctx.enter_context(nc.sbuf_tensor("fa_" + name, shape, dt))

        wfct, wq = sb("wfct", [P, KC, D]), sb("wq", [P, KC, D])
        bq = sb("bq", [P, KC])
        bqw = sb("bqw", [P, KC, P])
        bias, bfc = sb("bias", [P, D]), sb("bfc", [P, D])
        bd = m.bd
        t1, m0 = sb("t1", [P, KC, D]), sb("m0", [P, KC, D])
        rden = sb("rden", [P, NB, H])
        xs, xt = sb("xs", [P, 2, D]), sb("xt", [P, 2, D])
        xb, ga = sb("xb", [P, 2, D]), sb("ga", [P, 2, D])
        bank = [ctx.enter_context(nc.psum_tensor(f"fa_bank{i}", [P, 512], F32)) for i in range(6)]
        s = {n: m.sem("fa_" + n) for n in ("weights masked t1_made t1_back m0_made m0_back x0 x1 xt0 xt1 xb_ready mixed "
                                           "ga_ready gb_ready res_ready sqrt_in sqrt chain stat").split()}
        x_in, xt_in = [s["x0"], s["x1"]], [s["xt0"], s["xt1"]]

        with nc.Block() as block:
            @block.sync
            def _(sp):
                for out, w in ((wfct, "WfcT"), (wq, "L0_mix_Wq")):
                    sp.dma_start(out[:, :, :], a[w].rearrange("(c p) n -> p c n", p=P)).then_inc(s["weights"], 16)
                sp.dma_start(bq[:, :], a["L0_mix_bq"].rearrange("(c p) -> p c", p=P), allow_slow_non_contiguous=True).then_inc(s["weights"], 16)
                sp.dma_start(bias[:, :], a["L0_gnn_bias"].partition_broadcast(P)).then_inc(s["weights"], 16)
                sp.dma_start(bfc[:, :], a["L0_mix_bfc"].partition_broadcast(P)).then_inc(s["weights"], 16)

                def load(k, u, r):
                    if at_least(k, 2):
                        sp.wait_ge(s["xb_ready"], k - 1)
                        sp.wait_ge(s["mixed"], k - 1)
                    if isinstance(k, int) and k == NB - 1:
                        sp.dma_start(xs[0:LAST, u, :], a["x"][k * P:N, :]).then_inc(x_in[u], 16)
                    else:
                        sp.dma_start(xs[:, u, :], a["x"][bass.ds(k * P, P), :]).then_inc(x_in[u], 16)
                    sp.dma_start(xt[:, u, :], block_rows(m.xnt_d, k)).then_inc(xt_in[u], 16)
                pipeline(sp, NB, 2, (0, load))

            @block.gpsimd
            def _(pool):
                nc.gpsimd.memset(bd[:, :, :], 1.0 / N).then_inc(s["masked"], 1)
                for h in range(P // HC):
                    o = bd[:, :, h * HC:(h + 1) * HC]
                    pool.wait_ge(s["masked"], 1 + 2 * h)
                    nc.gpsimd.affine_select(out=o, in_=o, compare_op=ALU.is_ge, fill=0.0, base=-HC * h,
                                            pattern=[[0, KC], [0, HC]], channel_multiplier=1).then_inc(s["masked"], 1)
                    pool.wait_ge(s["masked"], 2 + 2 * h)
                    nc.gpsimd.affine_select(out=o, in_=o, compare_op=ALU.is_ge, fill=0.0, base=HC * h + HC - 1,
                                            pattern=[[0, KC], [0, HC]], channel_multiplier=-1).then_inc(s["masked"], 1)
                pool.wait_ge(s["m0_back"], 2)

                def add_bias(k, u, r):
                    pool.wait_ge(x_in[u], 16 * (r + 1))
                    if at_least(k, 2):
                        pool.wait_ge(s["gb_ready"], k - 1)
                    nc.gpsimd.tensor_tensor(xb[:, u, :], xs[:, u, :], bias[:, :], ALU.add).then_inc(s["xb_ready"], 1)
                pipeline(pool, NB, 2, (0, add_bias))

            @block.vector
            def _(dve):
                c = Chain(dve, s["chain"])
                V = nc.vector
                V.tensor_scalar(m.tmp0[:, :], m.acc[:, :, LW], 1.0, None, ALU.add).then_inc(s["sqrt_in"], 1)
                c.did(V.tensor_scalar(rden[:, :, :], m.acc[:, :, D:LW], 1e-16, None, ALU.add))
                c.sync()
                c.did(V.reciprocal(rden[:, :, :], rden[:, :, :]))
                dve.wait_ge(s["sqrt"], 1)
                c.did(V.reciprocal(m.dinv[:, :], m.tmp1[:, :]))
                dve.wait_ge(s["masked"], 1 + 2 * P // HC)
                c.did(V.tensor_tensor(m.kvt[:, :, :], m.kvt[:, :, :], bd[:, :, :], ALU.mult))
                dve.wait_ge(s["weights"], 80)
                for q in range(KC):
                    c.did(V.tensor_scalar(bqw[:, q, :], m.iota[:, :], 0.0, bq[:, q:q + 1], ALU.mult, ALU.add))
                c.did(V.tensor_tensor(bias[:, :], bias[:, :], bfc[:, :], ALU.add))
                c.sync()
                V.memset(m.tmp0[:, 0:1], 0.0).then_inc(s["t1_back"], 1)
                dve.wait_ge(s["t1_made"], 1)
                for q in range(KC):
                    ins = V.tensor_copy(t1[:, q, :], bank[q][:, 0:D])
                ins.then_inc(s["t1_back"], 1)
                dve.wait_ge(s["m0_made"], 1)
                for q in range(KC):
                    ins = V.tensor_copy(m0[:, q, :], bank[2 + q][:, 0:D])
                ins.then_inc(s["m0_back"], 1)
                V.tensor_tensor(bias[:, :], bias[:, :], bank[4][:, 0:D], ALU.add).then_inc(s["m0_back"], 1)

                def combine(k, u, r):
                    rd = of_block(rden, k).unsqueeze(2).to_broadcast([P, H, HC])
                    if at_least(k, 2):
                        dve.wait_ge(s["gb_ready"], k - 1)
                    V.tensor_tensor(ga[:, u, :].rearrange("p (h c) -> p h c", h=H),
                                    m.acc[:, bass.ds(k, 1), 0:D].rearrange("p a (h c) -> p (a h) c", h=H), rd,
                                    ALU.mult).then_inc(s["ga_ready"], 1)

                def add(k, u, r):
                    dve.wait_ge(s["ga_ready"], k + 1)
                    dve.wait_ge(s["xb_ready"], k + 1)
                    V.tensor_tensor(ga[:, u, :], ga[:, u, :], xb[:, u, :], ALU.add).then_inc(s["gb_ready"], 1)

                def finish(k, u, r):
                    dve.wait_ge(s["gb_ready"], k + 1)
                    dve.wait_ge(s["mixed"], k + 1)
                    V.tensor_tensor(m.acc[:, bass.ds(k, 1), 0:D].rearrange("p a d -> p (a d)"), ga[:, u, :], bank[u][:, 0:D],
                                    ALU.add).then_inc(s["res_ready"], 1)

                def stats(k, u, r):
                    dve.wait_ge(s["res_ready"], k + 1)
                    V.bn_stats(of_block(m.st, k), m.acc[:, bass.ds(k, 1), 0:D].rearrange("p a d -> p (a d)")).then_inc(s["stat"], 1)
                pipeline(dve, NB, 2, (2, stats), (1, finish), (0, combine), (0, add))

            @block.scalar
            def _(act):
                act.wait_ge(s["sqrt_in"], 1)
                nc.scalar.activation(m.tmp1[:, :], m.tmp0[:, :], ACT.Sqrt).then_inc(s["sqrt"], 1)

            @block.tensor
            def _(pe):
                pe.wait_ge(s["t1_back"], 1)
                for q in range(KC):
                    last = nc.tensor.matmul(bank[q][:, 0:D], m.kvt[:, q, :], wfct[:, q, :], start=True, stop=True)
                last.then_inc(s["t1_made"], 1)
                pe.wait_ge(s["t1_back"], 2)
                for q in range(KC):
                    for h in range(KC):
                        nc.tensor.matmul(bank[2 + q][:, 0:D], wq[:, h, q * P:(q + 1) * P], t1[:, h, :],
                                         start=(h == 0), stop=(h == KC - 1))
                for h in range(KC):
                    last = nc.tensor.matmul(bank[4][:, 0:D], bqw[:, h, :], t1[:, h, :], start=(h == 0), stop=(h == KC - 1))
                last.then_inc(s["m0_made"], 1)
                pe.wait_ge(s["m0_back"], 2)

                def mix(k, u, r):
                    pe.wait_ge(xt_in[u], 16 * (r + 1))
                    if at_least(k, 2):
                        pe.wait_ge(s["res_ready"], k - 1)
                    for q in range(KC):
                        last = nc.tensor.matmul(bank[u][:, 0:D], xt[:, u, q * P:(q + 1) * P], m0[:, q, :],
                                                start=(q == 0), stop=(q == KC - 1))
                    last.then_inc(s["mixed"], 1)
                pipeline(pe, NB, 2, (0, mix))


def top_one(V, c, m, score, mask, best, cand):
    e8 = m.e8[:, :].unsqueeze(1).to_broadcast([P, NB, NE])
    c.did(V.tensor_reduce(best[:, :], score, AX.X, ALU.max))
    c.sync()
    c.did(V.tensor_tensor(cand, score, best[:, :].unsqueeze(2).to_broadcast([P, NB, NE]), ALU.is_equal))
    c.sync()
    c.did(V.tensor_tensor(cand, cand, e8, ALU.mult))
    c.sync()
    c.did(V.tensor_reduce(m.tmp1[:, :], cand, AX.X, ALU.min))
    c.sync()
    c.did(V.tensor_tensor(mask, e8, m.tmp1[:, :].unsqueeze(2).to_broadcast([P, NB, NE]), ALU.is_equal))
    c.sync()


def route(nc, m, a, layer):
    with ExitStack() as ctx:
        def sb(name, shape, dt=F32):
            return ctx.enter_context(nc.sbuf_tensor(f"r{layer}_" + name, shape, dt))

        wg, bg = sb("wg", [P, KC, NE]), sb("bg", [P, NE])
        xn, xt = sb("xn", [P, 2, D]), sb("xt", [P, 2, D])
        score = sb("score", [P, NB, NE])
        mask1, mask2, both = sb("mask1", [P, NB, NE]), sb("mask2", [P, NB, NE]), sb("both", [P, NB, NE])
        cand, tot, incl = sb("cand", [P, NB, NE]), sb("tot", [P, NE, NB]), sb("incl", [P, NE, NB])
        slot, notfirst = sb("slot", [P, NB, NE]), sb("notfirst", [P, NE, NB])
        valid, best, tri = sb("valid", [P, NB]), sb("best", [P, NB]), sb("tri", [P, P])
        base, tiles, tint = sb("base", [P, NE]), sb("tiles", [P, NE]), sb("tint", [P, NE], I32)
        trow = sb("trow", [1, T0])
        sf = sb("sf", [P, 2, NB])
        disp = sb("disp", [P, 2, 7, D])
        didx = sb("didx", [P, 2, 2, 7], U32)
        bank = [ctx.enter_context(nc.psum_tensor(f"r{layer}_bank{i}", [P, 512], F32)) for i in range(6)]
        s = {n: m.sem(f"r{layer}_" + n) for n in ("weights masks var std xn_ready xt_made xt_ready g_made g_back counted "
                                                  "totals chain l_in exped slots d_ready indexed issued sent0 sent1").split()}
        sent = [s["sent0"], s["sent1"]]
        buf = (m.buf0_d, m.buf1_d)[layer]
        res = m.acc
        pairs = 2 - layer

        def rows_of(k):
            return res[:, bass.ds(k, 1), 0:D].rearrange("p a d -> p (a d)")

        with nc.Block() as block:
            @block.sync
            def _(sp):
                w, b = (("L0_ffn_Wg", "L0_ffn_bg"), ("L1_ffn_gate_w", "L1_ffn_gate_b"))[layer]
                sp.dma_start(wg[:, :, :], a[w].rearrange("(c p) n -> p c n", p=P)).then_inc(s["weights"], 16)
                sp.dma_start(bg[:, :], a[b].partition_broadcast(P)).then_inc(s["weights"], 16)

            @block.gpsimd
            def _(pool):
                nc.gpsimd.memset(tri[:, :], 1.0).then_inc(s["masks"], 1)
                nc.gpsimd.memset(valid[:, :], 1.0).then_inc(s["masks"], 1)
                nc.gpsimd.memset(notfirst[:, :, :], 1.0).then_inc(s["masks"], 1)
                nc.gpsimd.iota(m.e8[:, :], [[1, NE]], base=-NE, channel_multiplier=0,
                               allow_small_or_imprecise_dtypes=True).then_inc(s["masks"], 1)
                pool.wait_ge(s["masks"], 4)
                nc.gpsimd.affine_select(out=tri[:, :], in_=tri[:, :], compare_op=ALU.is_ge, fill=0.0, base=-1,
                                        pattern=[[1, P]], channel_multiplier=-1).then_inc(s["masks"], 1)
                nc.gpsimd.affine_select(out=valid[:, :], in_=valid[:, :], compare_op=ALU.is_ge, fill=0.0, base=N - 1,
                                        pattern=[[-P, NB]], channel_multiplier=-1).then_inc(s["masks"], 1)
                nc.gpsimd.affine_select(out=notfirst[:, :, :], in_=notfirst[:, :, :], compare_op=ALU.is_ge, fill=0.0, base=-1,
                                        pattern=[[0, NE], [1, NB]], channel_multiplier=0).then_inc(s["masks"], 1)
                pool.wait_ge(s["slots"], 1)

                def dispatch(g, u, r):
                    if at_least(g, 2):
                        pool.wait_ge(sent[u], 16 * 7 * pairs * r)
                    for e in range(pairs):
                        nc.gpsimd.tensor_copy(didx[:, u, e, :], m.slots[:, e, bass.ds(g * 7, 7)]).then_inc(s["indexed"], 1)
                    pool.wait_ge(s["d_ready"], 7 * g + 7)
                    pool.sem_inc(s["issued"], 1)
                    pool.wait_ge(s["indexed"], pairs * (g + 1))
                    pool.sem_inc(s["issued"], 1)
                    for i in range(7):
                        for e in range(pairs):
                            nc.gpsimd.indirect_dma_start(buf, bass.IndirectOffsetOnAxis(ap=didx[:, u, e, i:i + 1], axis=0),
                                                         disp[:, u, i, :], None, bounds_check=buf.shape[0] - 1,
                                                         oob_is_err=False).then_inc(sent[u], 16)
                pipeline(pool, NB // 7, 2, (0, dispatch))
                for u in range(2):
                    pool.wait_ge(sent[u], 16 * 7 * pairs * ((NB // 7 + 1 - u) // 2))

            @block.vector
            def _(dve):
                c = Chain(dve, s["chain"])
                V = nc.vector
                finish_stats(dve, None, 0, nc, m, m.st, c, s["var"], s["std"])
                dve.wait_ge(s["weights"], 32)

                def normalise(k, u, r):
                    if at_least(k, 2):
                        dve.wait_ge(s["xt_made"], k - 1)
                    V.tensor_scalar(xn[:, u, :], rows_of(k), m.mean[:, bass.ds(k, 1)], m.rstd[:, bass.ds(k, 1)],
                                    ALU.subtract, ALU.mult).then_inc(s["xn_ready"], 1)

                def gate(k, u, r):
                    dve.wait_ge(s["g_made"], k + 1)
                    V.tensor_tensor(of_block(score, k), bank[2 + u][:, 0:NE], bg[:, :], ALU.add).then_inc(s["g_back"], 1)
                pipeline(dve, NB, 2, (0, normalise), (2, gate))
                dve.wait_ge(s["g_back"], NB)
                dve.wait_ge(s["masks"], 7)
                vb = valid[:, :].unsqueeze(2).to_broadcast([P, NB, NE])
                top_one(V, c, m, score[:, :, :], mask1[:, :, :], best, cand[:, :, :])
                if layer == 0:
                    c.did(V.scalar_tensor_tensor(slot[:, :, :], mask1[:, :, :], MASKED, score[:, :, :], ALU.mult, ALU.add))
                    c.sync()
                    top_one(V, c, m, slot[:, :, :], mask2[:, :, :], best, cand[:, :, :])
                    c.did(V.tensor_tensor(mask2[:, :, :], mask2[:, :, :], vb, ALU.mult))
                else:
                    c.did(V.tensor_tensor(slot[:, :, :], score[:, :, :], best[:, :].unsqueeze(2).to_broadcast([P, NB, NE]), ALU.subtract))
                    c.sync()
                    V.memset(m.tmp0[:, 0:1], 0.0).then_inc(s["l_in"], 1)
                    dve.wait_ge(s["exped"], 1)
                    c.did(V.tensor_reduce(m.prob[:, :], slot[:, :, :], AX.X, ALU.add))
                    c.sync()
                    c.did(V.reciprocal(m.prob[:, :], m.prob[:, :]))
                c.did(V.tensor_tensor(mask1[:, :, :], mask1[:, :, :], vb, ALU.mult))
                c.sync()
                if layer == 0:
                    V.tensor_tensor(both[:, :, :], mask1[:, :, :], mask2[:, :, :], ALU.add).then_inc(s["counted"], 1)
                else:
                    V.tensor_copy(both[:, :, :], mask1[:, :, :]).then_inc(s["counted"], 1)
                dve.wait_ge(s["totals"], 1)
                c.did(V.tensor_copy(tot[:, :, :], bank[5][:, 0:NB * NE].rearrange("p (b e) -> p e b", e=NE)))
                c.sync()
                flat = lambda t: t[:, :, :].rearrange("p e b -> p (e b)")
                c.did(V.tensor_tensor_scan(flat(incl), flat(notfirst), flat(tot), 0.0, ALU.mult, ALU.add))
                c.sync()
                c.did(V.tensor_tensor(flat(tot), flat(incl), flat(tot), ALU.subtract))
                c.did(V.tensor_scalar(tiles[:, :], incl[:, :, NB - 1], float(P - 1), None, ALU.add))
                c.sync()
                c.did(V.tensor_tensor(slot[:, :, :], bank[4][:, 0:NB * NE].rearrange("p (b e) -> p b e", e=NE),
                                      tot[:, :, :].rearrange("p e b -> p b e"), ALU.add))
                if layer == 0:
                    c.did(V.tensor_copy(tint[:, :], tiles[:, :]))
                    c.sync()
                    c.did(V.tensor_scalar(tint[:, :], tint[:, :], 7, None, ALU.arith_shift_right))
                    c.sync()
                    c.did(V.tensor_copy(tiles[:, :], tint[:, :]))
                    c.did(V.memset(best[:, 0:NE], 0.0))
                    c.sync()
                    c.did(V.tensor_tensor_scan(base[:, :], tiles[:, :], best[:, 0:NE], 0.0, ALU.add, ALU.add))
                    c.sync()
                    c.did(V.tensor_tensor(base[:, :], base[:, :], tiles[:, :], ALU.subtract))
                    c.sync()
                    c.did(V.memset(trow[:, :], -1.0))
                    c.sync()
                    for e in range(NE):
                        c.did(V.scalar_tensor_tensor(trow[:, :], m.iota[0:1, 0:T0], base[0:1, e:e + 1], trow[:, :], ALU.is_ge, ALU.add))
                        c.sync()
                    c.did(V.tensor_copy(m.etab[:, :], trow[:, :]))
                    c.did(V.tensor_scalar(base[:, :], base[:, :], float(P), None, ALU.mult))
                    c.sync()
                    c.did(V.tensor_tensor(slot[:, :, :], slot[:, :, :], base[:, :].unsqueeze(1).to_broadcast([P, NB, NE]), ALU.add))
                c.sync()
                for e, mask in enumerate((mask1, mask2)[0:pairs]):
                    c.did(V.tensor_tensor(cand[:, :, :], mask[:, :, :], slot[:, :, :], ALU.mult))
                    c.sync()
                    c.did(V.tensor_reduce(sf[:, e, :], cand[:, :, :], AX.X, ALU.add))
                    c.sync()
                c.did(V.tensor_scalar(valid[:, :], valid[:, :], -1.0, -1.0e6, ALU.add, ALU.mult))
                c.sync()
                if layer == 0:
                    for e in range(2):
                        c.did(V.tensor_copy(m.back[:, e, :], sf[:, e, :]))
                        c.did(V.tensor_tensor(m.slots[:, e, :], sf[:, e, :], valid[:, :], ALU.add))
                else:
                    e8 = m.e8[:, :].unsqueeze(1).to_broadcast([P, NB, NE])
                    c.did(V.tensor_tensor(cand[:, :, :], mask1[:, :, :], e8, ALU.mult))
                    c.did(V.tensor_scalar(m.tmp0[:, :], sf[:, 0, :], float(CAP), None, ALU.is_ge))
                    c.did(V.tensor_scalar(sf[:, 1, :], sf[:, 0, :], float(CAP - 1), None, ALU.min))
                    c.sync()
                    c.did(V.tensor_reduce(best[:, :], cand[:, :, :], AX.X, ALU.add))
                    c.sync()
                    c.did(V.tensor_scalar(best[:, :], best[:, :], -1.0, None, ALU.min))
                    c.sync()
                    c.did(V.tensor_scalar(best[:, :], best[:, :], float(NE), float(CT * P), ALU.add, ALU.mult))
                    c.sync()
                    for e in range(2):
                        c.did(V.tensor_tensor(sf[:, e, :], sf[:, e, :], best[:, :], ALU.add))
                    c.did(V.scalar_tensor_tensor(valid[:, :], m.tmp0[:, :], 1.0e6, valid[:, :], ALU.mult, ALU.add))
                    c.did(V.tensor_scalar(m.tmp1[:, :], m.tmp0[:, :], -1.0, 1.0, ALU.mult, ALU.add))
                    c.sync()
                    c.did(V.tensor_tensor(m.prob[:, :], m.prob[:, :], m.tmp1[:, :], ALU.mult))
                    c.did(V.tensor_copy(m.back[:, 0, :], sf[:, 1, :]))
                    c.did(V.tensor_tensor(m.slots[:, 0, :], sf[:, 0, :], valid[:, :], ALU.add))
                c.sync()
                V.memset(m.tmp0[:, 0:1], 0.0).then_inc(s["slots"], 1)

                def disperse(k, v, r):
                    g = 2 * r + v // 7
                    if v % 7 == 0 and at_least(k, 14):
                        dve.wait_ge(sent[v // 7], 16 * 7 * pairs * r)
                    V.tensor_scalar(disp[:, v // 7, v % 7, :], rows_of(k), m.mean[:, bass.ds(k, 1)], m.rstd[:, bass.ds(k, 1)],
                                    ALU.subtract, ALU.mult).then_inc(s["d_ready"], 1)
                pipeline(dve, NB, 14, (0, disperse))

            @block.scalar
            def _(act):
                finish_stats(None, act, 1, nc, m, m.st, None, s["var"], s["std"])

                def evacuate(k, u, r):
                    act.wait_ge(s["xt_made"], k + 1)
                    if at_least(k, 2):
                        act.wait_ge(s["g_made"], k - 1)
                    nc.scalar.copy(xt[:, u, :], bank[u][:, 0:D]).then_inc(s["xt_ready"], 1)
                pipeline(act, NB, 2, (0, evacuate))
                if layer == 1:
                    act.wait_ge(s["l_in"], 1)
                    nc.scalar.activation(slot[:, :, :], slot[:, :, :], ACT.Exp).then_inc(s["exped"], 1)

            @block.tensor
            def _(pe):
                def turn(k, u, r):
                    pe.wait_ge(s["xn_ready"], k + 1)
                    if at_least(k, 2):
                        pe.wait_ge(s["xt_ready"], k - 1)
                    for q in range(KC):
                        last = nc.tensor.transpose(bank[u][:, q * P:(q + 1) * P], xn[:, u, q * P:(q + 1) * P], m.ident[:, :])
                    last.then_inc(s["xt_made"], 1)

                def gate(k, u, r):
                    pe.wait_ge(s["xt_ready"], k + 1)
                    if at_least(k, 2):
                        pe.wait_ge(s["g_back"], k - 1)
                    else:
                        pe.wait_ge(s["weights"], 32)
                    for q in range(KC):
                        last = nc.tensor.matmul(bank[2 + u][:, 0:NE], xt[:, u, q * P:(q + 1) * P], wg[:, q, :],
                                                start=(q == 0), stop=(q == KC - 1))
                    last.then_inc(s["g_made"], 1)
                pipeline(pe, NB, 2, (0, turn), (1, gate))
                pe.wait_ge(s["counted"], 1)
                flat = both[:, :, :].rearrange("p b e -> p (b e)")
                nc.tensor.matmul(bank[4][:, 0:NB * NE], tri[:, :], flat, start=True, stop=True)
                nc.tensor.matmul(bank[5][:, 0:NB * NE], m.ones[:, :], flat, start=True, stop=True).then_inc(s["totals"], 1)



def experts0(nc, m, a):
    with ExitStack() as ctx:
        def sb(name, shape, dt=F32):
            return ctx.enter_context(nc.sbuf_tensor("e0_" + name, shape, dt))

        FC = F0 // P
        w1 = m.big0[:, 0:KC * NE * F0].rearrange("p (c n) -> p c n", c=KC)
        b1 = m.big0[:, KC * NE * F0:(KC + 1) * NE * F0].rearrange("p (e f) -> p e f", e=NE)
        w2, b2 = sb("w2", [P, FC, NE * D]), sb("b2", [P, NE, D])
        xs, xt = sb("xs", [P, 2, D]), sb("xt", [P, 2, D])
        hb, hg, ht = sb("hb", [P, F0]), sb("hg", [P, F0]), sb("ht", [P, 2, F0])
        y = sb("y", [P, 2, D])
        bank = [ctx.enter_context(nc.psum_tensor(f"e0_bank{i}", [P, 512], F32)) for i in range(8)]
        xt_ps, h_ps, ht_ps, y_ps = bank[0:2], bank[2:4], bank[4:6], bank[6:8]
        s = {n: m.sem("e0_" + n) for n in ("weights x0 x1 y0 y1 xt_made xt_ready h_made hb_ready hg_ready ht_made ht_ready "
                                           "y_made y_ready").split()}
        x_in, y_out = [s["x0"], s["x1"]], [s["y0"], s["y1"]]

        with nc.Block() as block:
            @block.sync
            def _(sp):
                for c in range(KC):
                    sp.dma_start(w1[:, c, :].rearrange("p (e f) -> p e f", e=NE),
                                 a["L0_ffn_W1"][:, c * P:(c + 1) * P, :].rearrange("e p f -> p e f")).then_inc(s["weights"], 16)
                for c in range(FC):
                    sp.dma_start(w2[:, c, :].rearrange("p (e f) -> p e f", e=NE),
                                 a["L0_ffn_W2"][:, c * P:(c + 1) * P, :].rearrange("e p f -> p e f")).then_inc(s["weights"], 16)
                sp.dma_start(b1[:, :, :].rearrange("p e f -> p (e f)"), a["L0_ffn_b1"].rearrange("e f -> (e f)").partition_broadcast(P))\
                    .then_inc(s["weights"], 16)
                sp.dma_start(b2[:, :, :].rearrange("p e f -> p (e f)"), a["L0_ffn_b2"].rearrange("e f -> (e f)").partition_broadcast(P))\
                    .then_inc(s["weights"], 16)

                def load(j, u, r):
                    if at_least(j, 2):
                        sp.wait_ge(s["xt_made"], j - 1)
                    sp.dma_start(xs[:, u, :], m.buf0_d[bass.ds(j * P, P), :]).then_inc(x_in[u], 16)

                def store(j, u, r):
                    sp.wait_ge(s["y_ready"], j + 1)
                    sp.dma_start(m.y0_d[bass.ds(j * P, P), :], y[:, u, :]).then_inc(y_out[u], 16)
                pipeline(sp, T0, 2, (0, load), (6, store))
                for u in range(2):
                    sp.wait_ge(y_out[u], 16 * T0 // 2)

            @block.vector
            def _(dve):
                V = nc.vector

                bias1_e = []

                def bias1(j, u, r):
                    if u == 0:
                        bias1_e[:] = experts_of(nc, m, mybir.EngineType.DVE, j, 2)
                    e = bias1_e[u]
                    dve.wait_ge(s["h_made"], j + 1)
                    if at_least(j, 1):
                        dve.wait_ge(s["hg_ready"], j)
                    V.tensor_tensor(hb[:, :], h_ps[u][:, :], of_block(b1, e), ALU.add).then_inc(s["hb_ready"], 1)

                def turned(j, u, r):
                    dve.wait_ge(s["ht_made"], j + 1)
                    if at_least(j, 2):
                        dve.wait_ge(s["y_made"], j - 1)
                    V.tensor_copy(ht[:, u, :], ht_ps[u][:, :]).then_inc(s["ht_ready"], 1)

                bias2_e = []

                def bias2(j, u, r):
                    if u == 0:
                        bias2_e[:] = experts_of(nc, m, mybir.EngineType.DVE, j, 2)
                    e = bias2_e[u]
                    dve.wait_ge(s["y_made"], j + 1)
                    if at_least(j, 2):
                        dve.wait_ge(y_out[u], 16 * r)
                    V.tensor_tensor(y[:, u, :], y_ps[u][:, 0:D], of_block(b2, e), ALU.add).then_inc(s["y_ready"], 1)
                dve.wait_ge(s["weights"], 16 * (KC + FC + 2))
                pipeline(dve, T0, 2, (0, bias1), (1, turned), (2, bias2))

            @block.scalar
            def _(act):
                def evacuate(j, u, r):
                    act.wait_ge(s["xt_made"], j + 1)
                    if at_least(j, 2):
                        act.wait_ge(s["h_made"], j - 1)
                    nc.scalar.copy(xt[:, u, :], xt_ps[u][:, 0:D]).then_inc(s["xt_ready"], 1)

                def gelu(j, u, r):
                    act.wait_ge(s["hb_ready"], j + 1)
                    if at_least(j, 1):
                        act.wait_ge(s["ht_made"], j)
                    nc.scalar.activation(hg[:, :], hb[:, :], ACT.Gelu).then_inc(s["hg_ready"], 1)
                pipeline(act, T0, 2, (0, evacuate), (1, gelu))

            @block.tensor
            def _(pe):
                def turn(j, u, r):
                    pe.wait_ge(x_in[u], 16 * (r + 1))
                    if at_least(j, 2):
                        pe.wait_ge(s["xt_ready"], j - 1)
                    for c in range(KC):
                        last = nc.tensor.transpose(xt_ps[u][:, c * P:(c + 1) * P], xs[:, u, c * P:(c + 1) * P], m.ident[:, :])
                    last.then_inc(s["xt_made"], 1)

                up_e = []

                def up(j, u, r):
                    if u == 0:
                        up_e[:] = experts_of(nc, m, mybir.EngineType.PE, j, 2)
                    e = up_e[u]
                    pe.wait_ge(s["xt_ready"], j + 1)
                    if at_least(j, 2):
                        pe.wait_ge(s["hb_ready"], j - 1)
                    for c in range(KC):
                        last = nc.tensor.matmul(h_ps[u][:, :], xt[:, u, c * P:(c + 1) * P], w1[:, c, bass.ds(e * F0, F0)],
                                                start=(c == 0), stop=(c == KC - 1))
                    last.then_inc(s["h_made"], 1)

                def turn_h(j, u, r):
                    pe.wait_ge(s["hg_ready"], j + 1)
                    if at_least(j, 2):
                        pe.wait_ge(s["ht_ready"], j - 1)
                    for c in range(FC):
                        last = nc.tensor.transpose(ht_ps[u][:, c * P:(c + 1) * P], hg[:, c * P:(c + 1) * P], m.ident[:, :])
                    last.then_inc(s["ht_made"], 1)

                down_e = []

                def down(j, u, r):
                    if u == 0:
                        down_e[:] = experts_of(nc, m, mybir.EngineType.PE, j, 2)
                    e = down_e[u]
                    pe.wait_ge(s["ht_ready"], j + 1)
                    if at_least(j, 2):
                        pe.wait_ge(s["y_ready"], j - 1)
                    for c in range(FC):
                        last = nc.tensor.matmul(y_ps[u][:, 0:D], ht[:, u, c * P:(c + 1) * P], w2[:, c, bass.ds(e * D, D)],
                                                start=(c == 0), stop=(c == FC - 1))
                    last.then_inc(s["y_made"], 1)
                pe.wait_ge(s["weights"], 16 * (KC + FC + 2))
                pipeline(pe, T0, 2, (0, turn), (2, up), (4, down), (3, turn_h))


def start_layer1(nc, m, a):
    with ExitStack() as ctx:
        def sb(name, shape, dt=F32):
            return ctx.enter_context(nc.sbuf_tensor("s1_" + name, shape, dt))

        w1 = sb("w1", [P, KC, MH])
        xn, xt = sb("xn", [P, 2, D]), sb("xt", [P, 2, D])
        bank = [ctx.enter_context(nc.psum_tensor(f"s1_bank{i}", [P, 512], F32)) for i in range(4)]
        s = {n: m.sem("s1_" + n) for n in "weights chain var std xn_ready xt_made xt_ready xts0 xts1 h_made t_ready stored".split()}
        xt_stored = [s["xts0"], s["xts1"]]

        with nc.Block() as block:
            @block.sync
            def _(sp):
                sp.dma_start(w1[:, :, :], a["L1_gnn_W1"].rearrange("(c p) n -> p c n", p=P)).then_inc(s["weights"], 16)

                def store(k, u, r):
                    sp.wait_ge(s["xt_ready"], k + 1)
                    sp.dma_start(block_rows(m.xnt_d, k), xt[:, u, :]).then_inc(xt_stored[u], 16)
                pipeline(sp, NB, 2, (0, store))
                sp.wait_ge(s["t_ready"], NB)
                sp.dma_start(m.t_d.rearrange("b p n -> p b n"), m.table[:, :, :]).then_inc(s["stored"], 16)
                sp.wait_ge(s["stored"], 16)
                for u in range(2):
                    sp.wait_ge(xt_stored[u], 16 * ((NB + 1 - u) // 2))

            @block.vector
            def _(dve):
                c = Chain(dve, s["chain"])
                finish_stats(dve, None, 0, nc, m, m.st, c, s["var"], s["std"])

                def normalise(k, u, r):
                    if at_least(k, 2):
                        dve.wait_ge(s["xt_made"], k - 1)
                    nc.vector.tensor_scalar(xn[:, u, :], of_block(m.acc, k)[:, 0:D], m.mean[:, bass.ds(k, 1)],
                                            m.rstd[:, bass.ds(k, 1)], ALU.subtract, ALU.mult).then_inc(s["xn_ready"], 1)

                def scale(k, u, r):
                    dve.wait_ge(s["h_made"], k + 1)
                    nc.vector.tensor_scalar(of_block(m.table, k), bank[2 + u][:, 0:MH], m.dinv[:, bass.ds(k, 1)], None,
                                            ALU.mult).then_inc(s["t_ready"], 1)
                pipeline(dve, NB, 2, (0, normalise), (2, scale))

            @block.scalar
            def _(act):
                finish_stats(None, act, 1, nc, m, m.st, None, s["var"], s["std"])

                def evacuate(k, u, r):
                    act.wait_ge(s["xt_made"], k + 1)
                    if at_least(k, 2):
                        act.wait_ge(s["h_made"], k - 1)
                        act.wait_ge(xt_stored[u], 16 * r)
                    nc.scalar.copy(xt[:, u, :], bank[u][:, 0:D]).then_inc(s["xt_ready"], 1)
                pipeline(act, NB, 2, (0, evacuate))

            @block.tensor
            def _(pe):
                def turn(k, u, r):
                    pe.wait_ge(s["xn_ready"], k + 1)
                    if at_least(k, 2):
                        pe.wait_ge(s["xt_ready"], k - 1)
                    for q in range(KC):
                        last = nc.tensor.transpose(bank[u][:, q * P:(q + 1) * P], xn[:, u, q * P:(q + 1) * P], m.ident[:, :])
                    last.then_inc(s["xt_made"], 1)

                def project(k, u, r):
                    if not at_least(k, 1):
                        pe.wait_ge(s["weights"], 16)
                    pe.wait_ge(s["xt_ready"], k + 1)
                    if at_least(k, 2):
                        pe.wait_ge(s["t_ready"], k - 1)
                    for q in range(KC):
                        last = nc.tensor.matmul(bank[2 + u][:, 0:MH], xt[:, u, q * P:(q + 1) * P], w1[:, q, :],
                                                start=(q == 0), stop=(q == KC - 1))
                    last.then_inc(s["h_made"], 1)
                pipeline(pe, NB, 2, (0, turn), (1, project))


def convolve(nc, m, a, which):
    with ExitStack() as ctx:
        def sb(name, shape, dt=F32):
            return ctx.enter_context(nc.sbuf_tensor(f"v{which}_" + name, shape, dt))

        NR = NG // 2
        idx, rows = sb("idx", [P, 2, GS], U32), sb("rows", [P, 2, GS, MH])
        oh = sb("oh", [P, 2, GS, P])
        xt = sb("xt", [P, D])
        bank = [ctx.enter_context(nc.psum_tensor(f"v{which}_bank{i}", [P, 512], F32)) for i in range(8)]
        s = {n: m.sem(f"v{which}_" + n) for n in "indexed issued in0 in1 oh_ready summed added zeroed xt_in weights".split()}
        landed = [s["in0"], s["in1"]]
        table = m.t_d.rearrange("b p n -> (b p) n")
        if which == 0:
            wkv, bkv = sb("wkv", [P, KC, 2, H, HC]), sb("bkv", [P, 2, H, HC])
            wmean, bmean = sb("wmean", [P, KC, 2, H]), sb("bmean", [P, 2, H])
            kvb, sq = sb("kvb", [P, 2, H, HC]), sb("sq", [P, 2, H, HC])
            var, std, rstd = sb("var", [P, 2, H]), sb("std", [P, 2, H]), sb("rstd", [P, 2, H])
            kn, vn = sb("kn", [P, KC, P + 1]), sb("vn", [P, D])
            s.update({n: m.sem("v0_" + n) for n in ("chain centred kv_made kvb_ready squared summed16 var_ready std_ready rstd_ready "
                                                    "kn_ready kv_used").split()})
            mixed = s["kv_made"]
        else:
            w2, b2 = sb("w2", [P, KC, D]), sb("b2", [P, D])
            ht, xb = sb("ht", [P, KC, P]), sb("xb", [P, D])
            s.update({n: m.sem("v1_" + n) for n in "ht_made ht_ready out_made xn_ready xb_ready mixed res_ready".split()})
            mixed = s["ht_made"]

        with nc.Block() as block:
            @block.gpsimd
            def _(pool):
                def gather(g, u, r):
                    if at_least(g, 2):
                        pool.wait_ge(landed[u], 16 * GS * r)
                        pool.wait_ge(s["summed"], g - 1)
                    nc.gpsimd.tensor_copy(idx[:, u, :], m.src[:, bass.ds(g * GS, GS)]).then_inc(s["indexed"], 1)
                    pool.wait_ge(s["indexed"], g + 1)
                    pool.sem_inc(s["issued"], 1)
                    for k in range(GS):
                        nc.gpsimd.indirect_dma_start(rows[:, u, k, :], None, table,
                                                     bass.IndirectOffsetOnAxis(ap=idx[:, u, k:k + 1], axis=0)).then_inc(landed[u], 16)
                pipeline(pool, NG, 2, (0, gather))

            @block.sync
            def _(sp):
                if which == 0:
                    w = a["L1_mix_w_qkv"].rearrange("(c p) (h t d) -> c t p h d", p=P, h=H, t=3)
                    b = a["L1_mix_b_qkv"].rearrange("(h t d) -> t h d", h=H, t=3)
                    for t in range(2):
                        for c in range(KC):
                            sp.dma_start(wkv[:, c, t, :, :], w[c, 1 + t]).then_inc(s["weights"], 16)
                        sp.dma_start(bkv[:, t, :, :], b[1 + t].partition_broadcast(P)).then_inc(s["weights"], 16)
                else:
                    sp.dma_start(w2[:, :, :], a["L1_mix_w2"].rearrange("(c p) n -> p c n", p=P)).then_inc(s["weights"], 16)
                    sp.dma_start(b2[:, :], a["L1_mix_b2"].partition_broadcast(P)).then_inc(s["weights"], 16)

                def load(k, u, r):
                    if at_least(k, 1):
                        sp.wait_ge(mixed, k)
                    sp.dma_start(xt[:, :], block_rows(m.xnt_d, k)).then_inc(s["xt_in"], 16)
                pipeline(sp, NB, 1, (0, load))

            @block.vector
            def _(dve):
                V = nc.vector
                V.memset(m.agg[:, :, :], 0.0).then_inc(s["zeroed"], 1)
                dve.wait_ge(s["zeroed"], 1)
                if which == 0:
                    c = Chain(dve, s["chain"])
                    dve.wait_ge(s["weights"], 16 * 2 * (KC + 1))
                    for w, mean in [(wkv[:, q], wmean[:, q]) for q in range(KC)] + [(bkv, bmean)]:
                        for t in range(2):
                            c.did(V.tensor_reduce(mean[:, t, :], w[:, t, :, :], AX.X, ALU.add))
                            c.sync()
                            c.did(V.scalar_tensor_tensor(w[:, t, :, :], mean[:, t, :].unsqueeze(2).to_broadcast([P, H, HC]),
                                                         -1.0 / HC, w[:, t, :, :], ALU.mult, ALU.add))
                    c.sync()
                    V.memset(kn[:, :, P:P + 1], 1.0).then_inc(s["centred"], 1)

                def one_hot(g, u):
                    if at_least(g, 2):
                        dve.wait_ge(s["summed"], g - 1)
                    V.tensor_tensor(oh[:, u, :, :], m.iota[:, :].unsqueeze(1).to_broadcast([P, GS, P]),
                                    m.dl[:, bass.ds(g * GS, GS)].unsqueeze(2).to_broadcast([P, GS, P]),
                                    ALU.is_equal).then_inc(s["oh_ready"], 1)

                def add(g, u):
                    dve.wait_ge(s["summed"], g + 1)
                    blocks = blocks_of(nc, m, mybir.EngineType.DVE, g * GS, GS)
                    for k in range(GS):
                        t = g * GS + k
                        if at_least(t, 1):
                            dve.wait_ge(s["added"], t)
                        V.tensor_tensor(of_block(m.agg, blocks[k]), of_block(m.agg, blocks[k]), bank[u][:, k * MH:(k + 1) * MH],
                                        ALU.add).then_inc(s["added"], 1)

                def variance(k, u, r):
                    dve.wait_ge(s["squared"], k + 1)
                    V.tensor_reduce(var[:, :, :], sq[:, :, :, :], AX.X, ALU.add).then_inc(s["summed16"], 1)
                    dve.wait_ge(s["summed16"], k + 1)
                    if at_least(k, 1):
                        dve.wait_ge(s["std_ready"], k)
                    V.tensor_scalar(var[:, :, :], var[:, :, :], 1.0 / HC, EPS, ALU.mult, ALU.add).then_inc(s["var_ready"], 1)

                def scale(k, u, r):
                    dve.wait_ge(s["std_ready"], k + 1)
                    if at_least(k, 1):
                        dve.wait_ge(s["kv_used"], k)
                        dve.wait_ge(s["kn_ready"], 2 * k)
                    V.reciprocal(rstd[:, :, :], std[:, :, :]).then_inc(s["rstd_ready"], 1)
                    dve.wait_ge(s["rstd_ready"], k + 1)
                    wide = rstd[:, :, :].unsqueeze(3).to_broadcast([P, 2, H, HC])
                    V.tensor_tensor(kn[:, :, 0:P].rearrange("p c (h d) -> p c h d", d=HC),
                                    kvb[:, 0, :, :].rearrange("p (c h) d -> p c h d", c=KC),
                                    rstd[:, 0, :].rearrange("p (c h) -> p c h", c=KC).unsqueeze(3).to_broadcast([P, KC, H // KC, HC]),
                                    ALU.mult).then_inc(s["kn_ready"], 1)
                    V.tensor_tensor(vn[:, :].rearrange("p (h d) -> p h d", d=HC), kvb[:, 1, :, :], wide[:, 1],
                                    ALU.mult).then_inc(s["kn_ready"], 1)

                def add_bias(k, u, r):
                    dve.wait_ge(s["kv_made"], k + 1)
                    if at_least(k, 1):
                        dve.wait_ge(s["kn_ready"], 2 * k)
                    V.tensor_tensor(kvb[:, :, :, :].rearrange("p t h d -> p (t h d)"), bank[2][:, :],
                                    bkv[:, :, :, :].rearrange("p t h d -> p (t h d)"), ALU.add).then_inc(s["kvb_ready"], 1)

                def normalise(k, u, r):
                    if at_least(k, 1):
                        dve.wait_ge(s["res_ready"], k)
                    V.tensor_scalar(xb[:, :], of_block(m.acc, k)[:, 0:D], m.mean[:, bass.ds(k, 1)], m.rstd[:, bass.ds(k, 1)],
                                    ALU.subtract, ALU.mult).then_inc(s["xn_ready"], 1)
                    dve.wait_ge(s["xn_ready"], k + 1)
                    V.tensor_tensor(xb[:, :], xb[:, :], b2[:, :], ALU.add).then_inc(s["xb_ready"], 1)

                def finish(k, u, r):
                    dve.wait_ge(s["xb_ready"], k + 1)
                    dve.wait_ge(s["out_made"], k + 1)
                    V.tensor_tensor(xb[:, :], xb[:, :], bank[3][:, 0:D], ALU.add).then_inc(s["mixed"], 1)
                    dve.wait_ge(s["mixed"], k + 1)
                    res = of_block(m.acc, k)[:, 0:D]
                    V.tensor_tensor(res, res, xb[:, :], ALU.add).then_inc(s["res_ready"], 1)

                conv = ((0, lambda k, u, r: one_hot(2 * k, 0)), (1, lambda k, u, r: add(2 * k + 1, 1)),
                        (0, lambda k, u, r: one_hot(2 * k + 1, 1)), (0, lambda k, u, r: add(2 * k, 0)))
                if which == 0:
                    pipeline(dve, NR, 1, conv[0], conv[1], (1, variance, NB), conv[2], conv[3], (1, scale, NB), (0, add_bias, NB))
                else:
                    dve.wait_ge(s["weights"], 32)
                    pipeline(dve, NR, 1, conv[0], conv[1], (1, normalise, NB), conv[2], conv[3], (1, finish, NB))

            @block.scalar
            def _(act):
                def root(k, u, r):
                    act.wait_ge(s["var_ready"], k + 1)
                    if at_least(k, 1):
                        act.wait_ge(s["rstd_ready"], k)
                    nc.scalar.activation(std[:, :, :], var[:, :, :], ACT.Sqrt).then_inc(s["std_ready"], 1)

                def square(k, u, r):
                    act.wait_ge(s["kvb_ready"], k + 1)
                    if at_least(k, 1):
                        act.wait_ge(s["summed16"], k)
                    nc.scalar.activation(sq[:, :, :, :], kvb[:, :, :, :], ACT.Square).then_inc(s["squared"], 1)

                def gelu(k, u, r):
                    act.wait_ge(s["ht_made"], k + 1)
                    if at_least(k, 1):
                        act.wait_ge(s["out_made"], k)
                    for q in range(KC):
                        last = nc.scalar.activation(ht[:, q, :], bank[2][:, q * P:(q + 1) * P], ACT.Gelu, bias=m.c2[:, q:q + 1])
                    last.then_inc(s["ht_ready"], 1)
                if which == 0:
                    pipeline(act, NB, 1, (1, root), (0, square))
                else:
                    pipeline(act, NB, 1, (0, gelu))

            @block.tensor
            def _(pe):
                def total(g, u):
                    pe.wait_ge(s["oh_ready"], g + 1)
                    pe.wait_ge(landed[u], 16 * GS * ((g - u) // 2 + 1))
                    if at_least(g, 2):
                        pe.wait_ge(s["added"], GS * (g - 1))
                    for k in range(GS):
                        last = nc.tensor.matmul(bank[u][:, k * MH:(k + 1) * MH], oh[:, u, k, :], rows[:, u, k, :],
                                                start=True, stop=True)
                    last.then_inc(s["summed"], 1)

                def project(k, u, r):
                    pe.wait_ge(s["xt_in"], 16 * (k + 1))
                    if at_least(k, 1):
                        pe.wait_ge(s["kvb_ready"], k)
                    for q in range(KC):
                        last = nc.tensor.matmul(bank[2][:, :], xt[:, q * P:(q + 1) * P],
                                                wkv[:, q, :, :, :].rearrange("p t h d -> p (t h d)"), start=(q == 0), stop=(q == KC - 1))
                    last.then_inc(s["kv_made"], 1)

                def sum_kv(k, u, r):
                    rows_ = LAST if isinstance(k, int) and k == NB - 1 else P
                    first, final = isinstance(k, int) and k == 0, isinstance(k, int) and k == NB - 1
                    pe.wait_ge(s["kn_ready"], 2 * k + 2)
                    for q in range(KC):
                        nc.tensor.matmul(bank[4 + q][:, 0:P + 1], vn[0:rows_, q * P:(q + 1) * P], kn[0:rows_, q, :],
                                         start=first, stop=final)
                        last = nc.tensor.matmul(bank[6 + q][:, 0:P], m.ones[0:rows_, :], kn[0:rows_, q, 0:P],
                                                start=first, stop=final)
                    last.then_inc(s["kv_used"], 1)

                def up(k, u, r):
                    pe.wait_ge(s["xt_in"], 16 * (k + 1))
                    if at_least(k, 1):
                        pe.wait_ge(s["ht_ready"], k)
                    for j in range(KC):
                        for q in range(KC):
                            last = nc.tensor.matmul(bank[2][:, j * P:(j + 1) * P], m.m2[:, q, j * P:(j + 1) * P],
                                                    xt[:, q * P:(q + 1) * P], start=(q == 0), stop=(q == KC - 1))
                    last.then_inc(s["ht_made"], 1)

                def down(k, u, r):
                    pe.wait_ge(s["ht_ready"], k + 1)
                    if at_least(k, 1):
                        pe.wait_ge(s["mixed"], k)
                    for q in range(KC):
                        last = nc.tensor.matmul(bank[3][:, 0:D], ht[:, q, :], w2[:, q, :], start=(q == 0), stop=(q == KC - 1))
                    last.then_inc(s["out_made"], 1)

                even, odd = (0, lambda k, u, r: total(2 * k, 0)), (0, lambda k, u, r: total(2 * k + 1, 1))
                if which == 0:
                    pe.wait_ge(s["centred"], 1)
                    pipeline(pe, NR, 1, even, (2, sum_kv, NB), (0, project, NB), odd)
                else:
                    pe.wait_ge(s["weights"], 32)
                    pipeline(pe, NR, 1, even, (1, down, NB), (0, up, NB), odd)

        if which == 0:
            fold_mixer(nc, m, a, bank)


def fold_mixer(nc, m, a, bank):
    with ExitStack() as ctx:
        def sb(name, shape, dt=F32):
            return ctx.enter_context(nc.sbuf_tensor("fm_" + name, shape, dt))

        b1row = sb("b1row", [P, MH])
        wqt, w1 = sb("wqt", [P, KC, D]), sb("w1", [P, KC, D])
        bq, b1 = sb("bq", [P, KC]), sb("b1", [P, KC])
        kg, kb = sb("kg", [P, HC]), sb("kb", [P, HC])
        vg, vb = sb("vg", [P, 1]), sb("vb", [P, 1])
        kvt, sk, t = sb("kvt", [P, KC, P]), sb("sk", [P, KC, P]), sb("t", [P, KC, D])
        s = {n: m.sem("fm_" + n) for n in "weights chain table stored kvt t_made t_back m_made".split()}
        chunks = lambda x: x[:, :, :].rearrange("p c (h d) -> p c h d", d=HC)
        wide = lambda row: row[:, :].unsqueeze(1).to_broadcast([P, P // HC, HC])
        heads = lambda x: x.rearrange("p (h d) -> p h d", d=HC)

        with nc.Block() as block:
            @block.sync
            def _(sp):
                n = 0
                for out, v in ((b1row[:, :], a["L1_gnn_b1"].partition_broadcast(P)), (kg[:, :], a["L1_mix_kln_g"].partition_broadcast(P)),
                               (kb[:, :], a["L1_mix_kln_b"].partition_broadcast(P)),
                               (wqt[:, :, :], a["WqT1"].rearrange("(c p) n -> p c n", p=P)),
                               (w1[:, :, :], a["L1_mix_w1"].rearrange("(c p) n -> p c n", p=P))):
                    sp.dma_start(out, v).then_inc(s["weights"], 16)
                for h in range(P // HC):
                    o = slice(h * HC, (h + 1) * HC)
                    for out, v in ((vg, "L1_mix_vln_g"), (vb, "L1_mix_vln_b")):
                        sp.dma_start(out[o, :], a[v].rearrange("(p c) -> p c", c=1), allow_slow_non_contiguous=True).then_inc(s["weights"], 16)
                sp.dma_start(b1[:, :], a["L1_mix_b1"].rearrange("(c p) -> p c", p=P), allow_slow_non_contiguous=True).then_inc(s["weights"], 16)
                for h in range(H):
                    p0 = h * HC % P
                    sp.dma_start(bq[p0:p0 + HC, h * HC // P:h * HC // P + 1],
                                 a["L1_mix_b_qkv"][3 * h * HC:(3 * h + 1) * HC].rearrange("(p c) -> p c", c=1),
                                 allow_slow_non_contiguous=True).then_inc(s["weights"], 16)
                sp.wait_ge(s["table"], 1)
                sp.dma_start(m.t_d.rearrange("b p n -> p b n"), m.table[:, :, :]).then_inc(s["stored"], 16)
                sp.wait_ge(s["stored"], 16)

            @block.vector
            def _(dve):
                V, c = nc.vector, Chain(dve, s["chain"])
                dve.wait_ge(s["weights"], 16 * (5 + 2 * (P // HC) + 1 + H))
                dinv = m.dinv[:, :].unsqueeze(2).to_broadcast([P, NB, MH])
                for q in range(KC):
                    S, sv = bank[4 + q][:, 0:P], bank[4 + q][:, P:P + 1]
                    c.did(V.tensor_tensor(heads(kvt[:, q, :]), heads(S), wide(kg), ALU.mult))
                    c.did(V.tensor_tensor(heads(sk[:, q, :]), heads(bank[6 + q][:, 0:P]), wide(kg), ALU.mult))
                    c.did(V.tensor_copy(t[:, q, 0:1], sv))
                c.sync()
                for q in range(KC):
                    c.did(V.scalar_tensor_tensor(heads(kvt[:, q, :]), wide(kb), t[:, q, 0:1], heads(kvt[:, q, :]), ALU.mult, ALU.add))
                    c.did(V.scalar_tensor_tensor(heads(sk[:, q, :]), wide(kb), float(N), heads(sk[:, q, :]), ALU.mult, ALU.add))
                c.sync()
                c.did(V.tensor_scalar(kvt[:, :, :], kvt[:, :, :], vg[:, 0:1], None, ALU.mult))
                c.sync()
                c.did(V.scalar_tensor_tensor(kvt[:, :, :], sk[:, :, :], vb[:, 0:1], kvt[:, :, :], ALU.mult, ALU.add))
                c.sync()
                V.tensor_tensor(kvt[:, :, :], kvt[:, :, :], m.bd[:, :, :], ALU.mult).then_inc(s["kvt"], 1)
                c.did(V.tensor_tensor(m.agg[:, :, :], m.agg[:, :, :], m.table[:, :, :], ALU.add))
                c.sync()
                c.did(V.tensor_tensor(m.agg[:, :, :], m.agg[:, :, :], dinv, ALU.mult))
                c.sync()
                c.did(V.tensor_tensor(m.agg[:, :, :], m.agg[:, :, :], b1row[:, :].unsqueeze(1).to_broadcast([P, NB, MH]), ALU.add))
                c.sync()
                V.scalar_tensor_tensor(m.table[:, :, :], m.agg[:, :, :], 0.0, dinv, ALU.max, ALU.mult).then_inc(s["table"], 1)
                dve.wait_ge(s["t_made"], 1)
                for q in range(KC):
                    ins = V.tensor_copy(t[:, q, :], bank[q][:, 0:D])
                ins.then_inc(s["t_back"], 1)
                dve.wait_ge(s["m_made"], 1)
                for q in range(KC):
                    V.tensor_tensor(m.m2[:, q, :], w1[:, q, :], bank[2 + q][:, 0:D], ALU.add)
                    V.tensor_tensor(m.c2[:, q:q + 1], b1[:, q:q + 1], bank[4][:, q:q + 1], ALU.add)

            @block.tensor
            def _(pe):
                pe.wait_ge(s["kvt"], 1)
                for q in range(KC):
                    last = nc.tensor.matmul(bank[q][:, 0:D], kvt[:, q, :], w1[:, q, :], start=True, stop=True)
                last.then_inc(s["t_made"], 1)
                pe.wait_ge(s["t_back"], 1)
                for q in range(KC):
                    for h in range(KC):
                        nc.tensor.matmul(bank[2 + q][:, 0:D], wqt[:, h, q * P:(q + 1) * P], t[:, h, :],
                                         start=(h == 0), stop=(h == KC - 1))
                for q in range(KC):
                    for h in range(KC):
                        last = nc.tensor.matmul(bank[4][:, q:q + 1], t[:, h, q * P:(q + 1) * P], bq[:, h:h + 1],
                                                start=(h == 0), stop=(h == KC - 1))
                last.then_inc(s["m_made"], 1)


def finish_convolution(nc, m, a):
    with ExitStack() as ctx:
        def sb(name, shape, dt=F32):
            return ctx.enter_context(nc.sbuf_tensor("fc_" + name, shape, dt))

        w2, ut, us = sb("w2", [MH + 1, D]), sb("ut", [MH + 1, 2, P]), sb("us", [P, 2, MH])
        bank = [ctx.enter_context(nc.psum_tensor(f"fc_bank{i}", [P, 512], F32)) for i in range(4)]
        s = {n: m.sem("fc_" + n) for n in "weights chain ones u_ready ut_made ut_ready made res_ready stat".split()}

        with nc.Block() as block:
            @block.sync
            def _(sp):
                sp.dma_start(w2[0:MH, :], a["L1_gnn_W2"]).then_inc(s["weights"], 16)
                sp.dma_start(w2[MH:MH + 1, :], a["L1_gnn_b2"].rearrange("(a n) -> a n", a=1)).then_inc(s["weights"], 16)

            @block.vector
            def _(dve):
                V, c = nc.vector, Chain(dve, s["chain"])
                V.memset(ut[MH:MH + 1, :, :], 1.0).then_inc(s["ones"], 1)
                c.did(V.tensor_tensor(m.agg[:, :, :], m.agg[:, :, :], m.table[:, :, :], ALU.add))
                c.sync()

                def scale(k, u, r):
                    if at_least(k, 2):
                        dve.wait_ge(s["ut_made"], k - 1)
                    V.tensor_scalar(us[:, u, :], of_block(m.agg, k), m.dinv[:, bass.ds(k, 1)], None, ALU.mult).then_inc(s["u_ready"], 1)

                def finish(k, u, r):
                    dve.wait_ge(s["made"], k + 1)
                    res = of_block(m.acc, k)[:, 0:D]
                    V.scalar_tensor_tensor(res, bank[2 + u][:, 0:D], 0.0, res, ALU.max, ALU.add).then_inc(s["res_ready"], 1)

                def stats(k, u, r):
                    dve.wait_ge(s["res_ready"], k + 1)
                    V.bn_stats(of_block(m.st, k), of_block(m.acc, k)[:, 0:D]).then_inc(s["stat"], 1)
                pipeline(dve, NB, 2, (0, scale), (2, finish), (3, stats))

            @block.scalar
            def _(act):
                def evacuate(k, u, r):
                    act.wait_ge(s["ut_made"], k + 1)
                    if at_least(k, 2):
                        act.wait_ge(s["made"], k - 1)
                    nc.scalar.copy(ut[0:MH, u, :], bank[u][0:MH, 0:P]).then_inc(s["ut_ready"], 1)
                pipeline(act, NB, 2, (0, evacuate))

            @block.tensor
            def _(pe):
                def turn(k, u, r):
                    if at_least(k, 2):
                        pe.wait_ge(s["ut_ready"], k - 1)
                    pe.wait_ge(s["u_ready"], k + 1)
                    nc.tensor.matmul(bank[u][0:MH, 0:P], us[:, u, :], m.ident[:, :], start=True, stop=True).then_inc(s["ut_made"], 1)

                def project(k, u, r):
                    pe.wait_ge(s["ut_ready"], k + 1)
                    if at_least(k, 2):
                        pe.wait_ge(s["res_ready"], k - 1)
                    nc.tensor.matmul(bank[2 + u][:, 0:D], ut[:, u, :], w2[:, :], start=True, stop=True).then_inc(s["made"], 1)
                pe.wait_ge(s["weights"], 32)
                pe.wait_ge(s["ones"], 1)
                pipeline(pe, NB, 2, (0, turn), (1, project))


def experts1(nc, m, a):
    with ExitStack() as ctx:
        def sb(name, shape, dt=F32):
            return ctx.enter_context(nc.sbuf_tensor("e1_" + name, shape, dt))

        FC, UT = F1 // P, CT // 2
        UR = UT * P
        NU = 2 * NE
        W = KC * F1
        w1 = m.big0[:, 0:2 * W].rearrange("p (u c f) -> p u c f", u=2, c=KC)
        w2 = m.big0[:, 2 * W:2 * W + 2 * FC * D].rearrange("p (u f d) -> p u f d", u=2, f=FC)
        b1, b2 = sb("b1", [P, NE, FC]), sb("b2", [P, NE, D])
        b1e = sb("b1e", [P, 2, FC])
        xs, xt = sb("xs", [P, UT, D]), sb("xt", [P, KC, UR])
        ht, y = sb("ht", [P, FC, UR]), sb("y", [P, UT, D])
        bank = [ctx.enter_context(nc.psum_tensor(f"e1_bank{i}", [P, 512], F32)) for i in range(8)]
        xt_ps, h_ps, y_ps = bank[0:2], bank[2:5], bank[5:8]
        s = {n: m.sem("e1_" + n) for n in "biases w0 w1 x_in y_out xt_made xt_ready h_made h_ready down y_made y_ready".split()}
        w_in = [s["w0"], s["w1"]]

        with nc.Block() as block:
            @block.sync
            def _(sp):
                sp.dma_start(b1[:, :, :], a["L1_ffn_b1"].rearrange("e (f p) -> p e f", p=P), allow_slow_non_contiguous=True)\
                    .then_inc(s["biases"], 16)
                sp.dma_start(b2[:, :, :].rearrange("p e f -> p (e f)"), a["L1_ffn_b2"].rearrange("e f -> (e f)").partition_broadcast(P))\
                    .then_inc(s["biases"], 16)

                def load(j, v, r):
                    if at_least(j, 1):
                        sp.wait_ge(s["xt_made"], j)
                    sp.dma_start(xs[:, :, :], m.buf1_d[bass.ds(j * UR, UR), :].rearrange("(t p) d -> p t d", p=P)).then_inc(s["x_in"], 16)
                    if v % 2 == 0:
                        u, e = v // 2, 2 * r + v // 2
                        if at_least(j, 4):
                            sp.wait_ge(s["down"], j - 2)
                        sp.dma_start(w1[:, u, :, :], a["L1_ffn_w1"][bass.ds(e, 1)].rearrange("a (c p) f -> p (a c) f", p=P)).then_inc(w_in[u], 16)
                        sp.dma_start(w2[:, u, :, :], a["L1_ffn_w2"][bass.ds(e, 1)].rearrange("a (f p) d -> p (a f) d", p=P)).then_inc(w_in[u], 16)

                def store(j, v, r):
                    sp.wait_ge(s["y_ready"], UT * (j + 1))
                    sp.dma_start(m.y1_d[bass.ds(j * UR, UR), :].rearrange("(t p) d -> p t d", p=P), y[:, :, :]).then_inc(s["y_out"], 16)
                pipeline(sp, NU, 4, (0, load), (3, store))
                sp.wait_ge(s["y_out"], 16 * NU)

            @block.vector
            def _(dve):
                V = nc.vector

                def turned(j, v, r):
                    dve.wait_ge(s["xt_made"], j + 1)
                    if at_least(j, 1):
                        dve.wait_ge(s["h_made"], FC * j)
                    if v % 2 == 0:
                        if at_least(j, 4):
                            dve.wait_ge(s["h_ready"], FC * (j - 2))
                        V.tensor_copy(b1e[:, v // 2, :], of_block(b1, 2 * r + v // 2))
                    for q in range(KC):
                        V.tensor_copy(xt[:, q, :], xt_ps[q][:, :]).then_inc(s["xt_ready"], 1)

                def finish(j, v, r):
                    e = 2 * r + v // 2
                    if at_least(j, 1):
                        dve.wait_ge(s["y_out"], 16 * j)
                    for t in range(UT):
                        dve.wait_ge(s["y_made"], UT * j + t + 1)
                        V.tensor_tensor(y[:, t, :], y_ps[(UT * v + t) % 2][:, 0:D], of_block(b2, e), ALU.add).then_inc(s["y_ready"], 1)
                dve.wait_ge(s["biases"], 32)
                pipeline(dve, NU, 4, (0, turned), (1, finish))

            @block.scalar
            def _(act):
                def relu(j, v, r):
                    if at_least(j, 1):
                        act.wait_ge(s["down"], j)
                    act.wait_ge(s["xt_ready"], KC * (j + 1))
                    for f in range(FC):
                        act.wait_ge(s["h_made"], FC * j + f + 1)
                        nc.scalar.activation(ht[:, f, :], h_ps[f % 2][:, :], ACT.Relu,
                                             bias=b1e[:, v // 2, f:f + 1]).then_inc(s["h_ready"], 1)
                pipeline(act, NU, 4, (0, relu))

            @block.tensor
            def _(pe):
                def turn(j, v, r):
                    pe.wait_ge(s["x_in"], 16 * (j + 1))
                    if at_least(j, 1):
                        pe.wait_ge(s["xt_ready"], KC * j)
                    for q in range(KC):
                        for t in range(UT):
                            last = nc.tensor.transpose(xt_ps[q][:, t * P:(t + 1) * P], xs[:, t, q * P:(q + 1) * P], m.ident[:, :])
                    last.then_inc(s["xt_made"], 1)

                def up(j, v, r):
                    u = v // 2
                    if v % 2 == 0:
                        pe.wait_ge(w_in[u], 32 * (r + 1))
                    pe.wait_ge(s["xt_ready"], KC * (j + 1))
                    for f in range(FC):
                        if f >= 2 or at_least(j, 1):
                            pe.wait_ge(s["h_ready"], FC * j + f - 1)
                        for q in range(KC):
                            last = nc.tensor.matmul(h_ps[f % 2][:, :], w1[:, u, q, f * P:(f + 1) * P], xt[:, q, :],
                                                    start=(q == 0), stop=(q == KC - 1))
                        last.then_inc(s["h_made"], 1)

                def down(j, v, r):
                    u = v // 2
                    pe.wait_ge(s["h_ready"], FC * (j + 1))
                    for t in range(UT):
                        if t >= 2 or at_least(j, 1):
                            pe.wait_ge(s["y_ready"], UT * j + t - 1)
                        for f in range(FC):
                            last = nc.tensor.matmul(y_ps[(UT * v + t) % 2][:, 0:D], ht[:, f, t * P:(t + 1) * P], w2[:, u, f, :],
                                                    start=(f == 0), stop=(f == FC - 1))
                        last.then_inc(s["y_made"], 1)
                    nc.tensor.transpose(xt_ps[0][0:1, 0:P], m.ident[:, 0:1], m.ident[:, :]).then_inc(s["down"], 1)
                pipeline(pe, NU, 4, (1, up), (0, turn), (1, down))


def combine_experts(nc, m, a, layer):
    with ExitStack() as ctx:
        def sb(name, shape, dt=F32):
            return ctx.enter_context(nc.sbuf_tensor(f"c{layer}_" + name, shape, dt))

        pairs, G = 2 - layer, 7
        NGR = NB // G
        idx = sb("idx", [P, 2, pairs, G], U32)
        y = sb("y", [P, 2, pairs, G, D])
        consts, bad = sb("consts", [P, 3]), sb("bad", [P, 3, G, D], mybir.dt.uint8)
        s = {n: m.sem(f"c{layer}_" + n) for n in "indexed issued y0 y1 used stat chain out0 out1".split()}
        y_in, out_done = [s["y0"], s["y1"]], [s["out0"], s["out1"]]
        table = (m.y0_d, m.y1_d)[layer]

        with nc.Block() as block:
            @block.gpsimd
            def _(pool):
                def gather(g, u, r):
                    if at_least(g, 2):
                        pool.wait_ge(y_in[u], 16 * G * pairs * r)
                        pool.wait_ge(s["used"], g - 1)
                        if layer:
                            pool.wait_ge(out_done[u], 16 * r)
                    for e in range(pairs):
                        nc.gpsimd.tensor_copy(idx[:, u, e, :], m.back[:, e, bass.ds(g * G, G)]).then_inc(s["indexed"], 1)
                    pool.wait_ge(s["indexed"], pairs * (g + 1))
                    pool.sem_inc(s["issued"], 1)
                    for i in range(G):
                        for e in range(pairs):
                            nc.gpsimd.indirect_dma_start(y[:, u, e, i, :], None, table,
                                                         bass.IndirectOffsetOnAxis(ap=idx[:, u, e, i:i + 1], axis=0))\
                                .then_inc(y_in[u], 16)
                pipeline(pool, NGR, 2, (0, gather))

            @block.vector
            def _(dve):
                V = nc.vector
                c = Chain(dve, s["chain"])
                if layer:
                    for i, v in enumerate((0.0, 10000.0, -10000.0)):
                        c.did(V.memset(consts[:, i:i + 1], v))
                    c.sync()
                    c.begin(7)
                else:
                    c.begin(1)

                def combine(g, u, r):
                    dve.wait_ge(y_in[u], 16 * G * pairs * (r + 1))
                    c.at(g)
                    yk, res = y[:, u, 0, :, :], m.acc[:, bass.ds(g * G, G), 0:D]
                    if layer:
                        c.did(V.tensor_tensor(yk, yk, m.prob[:, bass.ds(g * G, G)].unsqueeze(2).to_broadcast([P, G, D]), ALU.mult))
                        c.sync()
                        c.did(V.tensor_tensor(bad[:, 0], yk, yk, ALU.not_equal))
                        c.did(V.tensor_scalar(bad[:, 1], yk, FMAX, None, ALU.is_gt))
                        c.did(V.tensor_scalar(bad[:, 2], yk, -FMAX, None, ALU.is_lt))
                        for i in range(3):
                            c.sync()
                            dve.sem_inc(s["issued"], 1)
                            c.did(V.copy_predicated(yk, bad[:, i], consts[:, i:i + 1].unsqueeze(2).to_broadcast([P, G, D])))
                        c.sync()
                        V.tensor_tensor(yk, res, yk, ALU.add).then_inc(s["used"], 1)
                    else:
                        c.did(V.tensor_tensor(yk, yk, y[:, u, 1, :, :], ALU.add))
                        c.sync()
                        V.tensor_tensor(res, res, yk, ALU.add).then_inc(s["used"], 1)
                        dve.wait_ge(s["used"], g + 1)
                        for i in range(G):
                            last = V.bn_stats(of_block(m.st, g * G + i), of_block(m.acc, g * G + i)[:, 0:D])
                        last.then_inc(s["stat"], 1)
                pipeline(dve, NGR, 2, (0, combine))

            if layer:
                @block.sync
                def _(sp):
                    def store(g, u, r):
                        sp.wait_ge(s["used"], g + 1)
                        if isinstance(g, int) and g == NGR - 1:
                            b = (NB - 1) * P
                            sp.dma_start(m.out[g * G * P:b, :].rearrange("(b p) d -> p b d", p=P), y[:, u, 0, 0:G - 1, :]).then_inc(out_done[u], 16)
                            sp.dma_start(m.out[b:N, :], y[0:LAST, u, 0, G - 1, :]).then_inc(out_done[u], 16)
                        else:
                            sp.dma_start(m.out[bass.ds(g * G * P, G * P), :].rearrange("(b p) d -> p b d", p=P), y[:, u, 0, :, :])\
                                .then_inc(out_done[u], 16)
                    pipeline(sp, NGR, 2, (0, store))
                    sp.wait_ge(out_done[0], 16 * (NGR // 2 + 2))
                    sp.wait_ge(out_done[1], 16 * (NGR // 2))


def memory(nc, ctx):
    m = Chip()

    def sb(name, shape, dt=F32):
        return ctx.enter_context(nc.sbuf_tensor(name, shape, dt))

    def dram(name, shape, dt=F32):
        return nc.dram_tensor(name, shape, dt).ap()

    m.live = []

    def sem(name):
        m.live.append(nc.alloc_semaphore(name=name))
        return m.live[-1]
    m.sem = sem
    m.src_p, m.dst_p, m.w_p = dram("src_p", [EP], I32), dram("dst_p", [EP], I32), dram("w_p", [EP])
    m.btab_d, m.key_d = dram("btab_d", [SPAD], I32), dram("key_d", [SPAD, P])
    m.xnt_d, m.xl_d = dram("xnt_d", [NB, P, D]), dram("xl_d", [NB, P, LW])
    m.ident, m.iota, m.ones = sb("ident", [P, P]), sb("iota", [P, P]), sb("ones", [P, P])
    m.btab = sb("btab", [1, SPAD], I32)
    m.src, m.dl = sb("src_steps", [P, SPAD], U32), sb("dl_steps", [P, SPAD])
    m.w = sb("w_steps", [P, SPAD])
    m.buf0_d, m.y0_d = dram("buf0_d", [T0 * P, D]), dram("y0_d", [T0 * P, D])
    m.buf1_d, m.y1_d = dram("buf1_d", [NE * CT * P, D]), dram("y1_d", [NE * CT * P, D])
    m.dinv, m.prob, m.st, m.e8 = sb("dinv", [P, NB]), sb("prob", [P, NB]), sb("st", [P, NB, 6]), sb("e8", [P, NE])
    m.slots, m.back, m.etab = sb("slots", [P, 2, NB], U32), sb("back", [P, 2, NB], U32), sb("etab", [1, T0], I32)
    m.xj_d = dram("xj_d", [2 * NG, P, GS // 2 * LW])
    m.ex = sb("ex", [P, NS * H])
    m.mean, m.rstd = sb("mean", [P, NB]), sb("rstd", [P, NB])
    m.tmp0, m.tmp1 = sb("tmp0", [P, NB]), sb("tmp1", [P, NB])
    m.atta = sb("atta", [P, KC, H])
    m.kvt, m.bd = sb("kvt", [P, KC, P]), sb("bd", [P, KC, P])
    m.t_d = dram("t_d", [NB, P, MH])
    m.m2, m.c2 = sb("m2", [P, KC, D]), sb("c2", [P, KC])
    m.big0, m.big1 = sb("big0", [P, 2 * CL]), sb("big1", [P, 2 * CL + 8])
    m.table = m.big0[:, 0:NB * MH].rearrange("p (b n) -> p b n", n=MH)
    m.agg = m.big0[:, NB * MH:2 * NB * MH].rearrange("p (b n) -> p b n", n=MH)
    return m


def build(nc, a, out):
    with ExitStack() as ctx:
        m = memory(nc, ctx)
        m.out = out
        edge_steps(nc, m, a)
        end_stage(nc, m)
        for stage in (project_nodes, score_edges, normalise_edges, aggregate_edges, finish_attention):
            stage(nc, m, a)
            end_stage(nc, m)
        route(nc, m, a, 0)
        end_stage(nc, m)
        experts0(nc, m, a)
        end_stage(nc, m)
        combine_experts(nc, m, a, 0)
        end_stage(nc, m)
        start_layer1(nc, m, a)
        end_stage(nc, m)
        for which in range(2):
            convolve(nc, m, a, which)
            end_stage(nc, m)
        finish_convolution(nc, m, a)
        end_stage(nc, m)
        route(nc, m, a, 1)
        end_stage(nc, m)
        experts1(nc, m, a)
        end_stage(nc, m)
        combine_experts(nc, m, a, 1)


TURNED = {"L0_gnn_W_l": "W_lT", "L0_gnn_W_r": "W_rT", "L0_mix_Wk": "WkT", "L0_mix_Wv": "WvT", "L0_mix_Wfc": "WfcT"}


def laid_out(inputs):
    arrays = {n: np.ascontiguousarray(v) for n, v in inputs.items() if n not in ("L0_mix_Wk", "L0_mix_Wv", "L0_mix_Wfc")}
    for name, turned in TURNED.items():
        arrays[turned] = np.ascontiguousarray(np.asarray(inputs[name]).T)
    qkv = np.asarray(inputs["L1_mix_w_qkv"]).reshape(D, H, 3 * HC)
    arrays["WqT1"] = np.ascontiguousarray(qkv[:, :, 0:HC].reshape(D, D).T)
    return arrays


def kernel(**inputs):
    import concourse.bacc as bacc
    from concourse.bass_utils import run_bass_kernel_spmd

    nc = bacc.Bacc("TRN2", target_bir_lowering=False, num_devices=1)
    arrays = laid_out(inputs)
    a = {n: nc.dram_tensor("in_" + n, v.shape, mybir.dt.from_np(v.dtype), kind="ExternalInput").ap() for n, v in arrays.items()}
    out = nc.dram_tensor("out", (N, D), F32, kind="ExternalOutput").ap()
    build(nc, a, out)
    r = run_bass_kernel_spmd(nc, [{"in_" + n: v for n, v in arrays.items()}], core_ids=[0])
    return r.results[0]["out"]
```

```python
from contextlib import ExitStack

import numpy as np

import concourse.bass as bass
from concourse import mybir

ALU = mybir.AluOpType
ACT = mybir.ActivationFunctionType
AX = mybir.AxisListType
F32 = mybir.dt.float32
BF16 = mybir.dt.bfloat16
I32 = mybir.dt.int32
U32 = mybir.dt.uint32

P = 128
N = 6250
D = 256
E = 100000
H = 8
HC = D // H
KC = D // P
NB = (N + P - 1) // P
LAST = N - (NB - 1) * P
NP = NB * P
NT = (E + P - 1) // P
EP = NT * P
GS = 8
NG = (NT + NB - 1 + GS - 1) // GS
NG += NG % 2
NS = NG * GS
SJ = (NS + P - 1) // P
SPAD = SJ * P
LW = D + H
AW = D + H + 2
CH = P // H
CS = NS // CH
CL = CS * P
MASKED = -1.0e30
EPS = 1e-5
SLOPE = 0.2
MH = 64
NE = 8
F0 = 512
T0 = (2 * N) // P + 1 + NE - 1
T0 += T0 % 2
F1 = 1024
CAP = -(-5 * N // (4 * NE))
CT = (CAP + P - 1) // P
FMAX = 3.4028234e38
assert NS % CH == 0 and LAST < P and NB % 7 == 0


class Chain:

    def __init__(self, eng, sem):
        self.eng, self.sem, self.base, self.n, self.first = eng, sem, 0, 0, 0

    def did(self, ins):
        ins.then_inc(self.sem, 1)
        self.n += 1

    def sync(self):
        self.eng.wait_ge(self.sem, self.base + self.n)

    def begin(self, per):
        self.first, self.per, self.n = self.base + self.n, per, 0

    def at(self, k):
        self.base, self.n = self.first + k * self.per, 0

    def end(self, steps):
        assert self.n == self.per, (self.n, self.per)
        self.base, self.n = self.first + steps * self.per, 0


def pipeline(eng, count, unroll, *stages):
    stages = [(stage + (count,))[0:3] for stage in stages]
    most = max(lag for lag, _, _ in stages)

    def emit(k):
        for lag, work, n in stages:
            if 0 <= k - lag < n:
                work(k - lag, (k - lag) % unroll, (k - lag) // unroll)

    first = -(-most // unroll) + 1
    last = min(n for _, _, n in stages) // unroll
    if last - first < 2:
        first = last = 0
    for k in range(first * unroll):
        emit(k)
    if last > first:
        with eng.Fori(first, last) as i:
            for j in range(unroll):
                for lag, work, _ in stages:
                    work(i * unroll + (j - lag), (j - lag) % unroll, i + (j - lag) // unroll)
    for k in range(last * unroll, count + most):
        emit(k)


def at_least(k, n):
    return not isinstance(k, int) or k >= n


class Chip:
    pass


def end_stage(nc, m):
    nc.clear_and_free_semaphores(m.live)
    m.live.clear()
    nc.all_engine_barrier()


def edge_steps(nc, m, a):
    with ExitStack() as ctx:
        def sb(name, shape, dt=F32):
            return ctx.enter_context(nc.sbuf_tensor("es_" + name, shape, dt))

        def ps(name):
            return ctx.enter_context(nc.psum_tensor("es_" + name, [P, 512], F32))

        pads = sb("pads", [1, 2, EP - E], I32)
        padw = sb("padw", [1, EP - E])
        ends = sb("ends", [1, 2, NT], I32)
        endb = sb("endb", [1, 2, NT], I32)
        endf = sb("endf", [1, 2, NT])
        zero = sb("zero", [1, NT])
        inc = sb("inc", [1, NT])
        row = sb("row", [1, 2, NT])
        ones = sb("ones", [1, P])
        bc = sb("bc", [P, 2, NT])
        tio = m.ex[:, 0:NT]
        junk = m.ex[:, NT:2 * NT]
        sval = sb("sval", [P, SJ])
        cnt = sb("cnt", [P, SJ])
        tsel = sb("tsel", [P, SJ])
        qsel = sb("qsel", [P, SJ])
        breal = sb("breal", [P, SJ])
        boff = sb("boff", [P, SJ])
        bcl = sb("bcl", [P, SJ])
        bint = sb("bint", [P, SJ], I32)
        tidx = sb("tidx", [P, SJ], U32)
        rs = sb("rs", [P, SJ, P], I32)
        rd = sb("rd", [P, SJ, P], I32)
        rw = m.big0[:, 0:SPAD].rearrange("p (j e) -> p j e", e=P)
        fs = m.big0[:, SPAD:2 * SPAD].rearrange("p (j e) -> p j e", e=P)
        fd = m.big0[:, 2 * SPAD:3 * SPAD].rearrange("p (j e) -> p j e", e=P)
        fl = m.big0[:, 3 * SPAD:4 * SPAD].rearrange("p (j e) -> p j e", e=P)
        bank = [ps(f"bank{i}") for i in range(4)]

        copied, padset = m.sem("es_copied"), m.sem("es_padset")
        padded, endsin, planned = m.sem("es_padded"), m.sem("es_endsin"), m.sem("es_planned")
        spread, spreadback, ioted = m.sem("es_spread"), m.sem("es_spreadback"), m.sem("es_ioted")
        rowsin, stored, floats = m.sem("es_rowsin"), m.sem("es_stored"), m.sem("es_floats")
        turned, turnedback, chain = m.sem("es_turned"), m.sem("es_turnedback"), m.sem("es_chain")
        identset = m.sem("es_identset")
        zeroset, zeroed = m.sem("es_zeroset"), m.sem("es_zeroed")
        ndst, ZT = NT // 2, 16
        zeros = m.ex[:, 2 * NT:2 * NT + ZT * D]
        x = m.big1[:, 0:NB * D].rearrange("p (b d) -> p b d", d=D)
        xpad, xin = m.sem("es_xpad"), m.sem("es_xin")

        with nc.Block() as block:
            @block.sync
            def _(sp):
                tiles = a["dst"][0:(NT - 1) * P].rearrange("(t e) -> e t", e=P)
                sp.dma_start(ends[:, 0, 0:NT - 1], tiles[0:1, :], allow_slow_non_contiguous=True).then_inc(endsin, 16)
                sp.dma_start(ends[:, 1, 0:NT - 1], tiles[P - 1:P, :], allow_slow_non_contiguous=True).then_inc(endsin, 16)
                sp.dma_start(ends[:, 0, NT - 1:NT], a["dst"][(NT - 1) * P:(NT - 1) * P + 1].rearrange("(a n) -> a n", a=1)).then_inc(endsin, 16)
                sp.dma_start(m.src_p[0:E].rearrange("(a n) -> a n", a=16), a["src"].rearrange("(a n) -> a n", a=16)).then_inc(copied, 16)
                sp.dma_start(m.dst_p[0:E].rearrange("(a n) -> a n", a=16), a["dst"].rearrange("(a n) -> a n", a=16)).then_inc(copied, 16)
                sp.dma_start(m.w_p[0:E].rearrange("(a n) -> a n", a=16), a["edge_weight"].rearrange("(a n) -> a n", a=16)).then_inc(copied, 16)
                sp.wait_ge(padset, 3)
                sp.dma_start(m.src_p[E:EP].rearrange("(a n) -> a n", a=1), pads[:, 0, :]).then_inc(padded, 16)
                sp.dma_start(m.dst_p[E:EP].rearrange("(a n) -> a n", a=1), pads[:, 1, :]).then_inc(padded, 16)
                sp.dma_start(m.w_p[E:EP].rearrange("(a n) -> a n", a=1), padw[:, :]).then_inc(padded, 16)
                sp.wait_ge(planned, 2)
                sp.dma_start(m.btab_d.rearrange("(j p) -> p j", p=P), bint[:, :], allow_slow_non_contiguous=True).then_inc(stored, 16)
                sp.wait_ge(floats, 1)
                sp.dma_start(m.key_d.rearrange("(j p) e -> p j e", p=P), fd[:, :, :]).then_inc(stored, 16)
                sp.wait_ge(stored, 32)
                sp.dma_start(m.btab[:, :], m.btab_d.rearrange("(a n) -> a n", a=1)).then_inc(stored, 16)
                sp.wait_ge(stored, 48)

            @block.scalar
            def _(act):
                act.wait_ge(xpad, 1)
                for q in range(4):
                    lo, hi = q * (NB - 1) // 4, (q + 1) * (NB - 1) // 4
                    act.dma_start(x[:, lo:hi, :], a["x"][lo * P:hi * P, :].rearrange("(b p) d -> p b d", p=P)).then_inc(xin, 16)
                act.dma_start(x[0:LAST, NB - 1, :], a["x"][(NB - 1) * P:N, :]).then_inc(xin, 16)
                act.wait_ge(zeroset, 1)
                n = 0
                for buf in (m.buf0_d, m.buf1_d):
                    rows = buf.shape[0] // P
                    for lo in range(0, rows, ZT):
                        hi = min(rows, lo + ZT)
                        act.dma_start(buf[lo * P:hi * P, :].rearrange("(p b) d -> p (b d)", p=P), zeros[:, 0:(hi - lo) * D]).then_inc(zeroed, 16)
                        n += 16
                act.wait_ge(zeroed, n)

            @block.gpsimd
            def _(pool):
                nc.gpsimd.memset(m.ident[:, :], 0.0).then_inc(identset, 1)
                pool.wait_ge(identset, 1)
                nc.gpsimd.affine_select(out=m.ident[:, :], in_=m.ident[:, :], compare_op=ALU.not_equal, fill=1.0,
                                        base=0, pattern=[[-1, P]], channel_multiplier=1).then_inc(ioted, 1)
                nc.gpsimd.iota(m.iota[:, :], [[1, P]], base=0, channel_multiplier=0,
                               allow_small_or_imprecise_dtypes=True).then_inc(ioted, 1)
                nc.gpsimd.iota(tio[:, :], [[1, NT]], base=0, channel_multiplier=0,
                               allow_small_or_imprecise_dtypes=True).then_inc(ioted, 1)
                nc.gpsimd.iota(sval[:, :], [[P, SJ]], base=0, channel_multiplier=1,
                               allow_small_or_imprecise_dtypes=True).then_inc(ioted, 1)
                pool.wait_ge(planned, 1)
                pool.wait_ge(copied, 48)
                pool.wait_ge(padded, 48)
                for j in range(SJ):
                    at = bass.IndirectOffsetOnAxis(ap=tidx[:, j:j + 1], axis=0)
                    for rows, table in ((rs, m.src_p), (rd, m.dst_p), (rw, m.w_p)):
                        nc.gpsimd.indirect_dma_start(rows[:, j, :], None, table.rearrange("(t e) -> t e", e=P), at)\
                            .then_inc(rowsin, 16)

            @block.vector
            def _(dve):
                c = Chain(dve, chain)
                nc.vector.memset(zeros, 0.0).then_inc(zeroset, 1)
                nc.vector.memset(x[:, NB - 1, :], 0.0).then_inc(xpad, 1)
                c.did(nc.vector.memset(ends[:, 1, NT - 1:NT], N))
                nc.vector.memset(pads[:, 0, :], 0).then_inc(padset, 1)
                nc.vector.memset(pads[:, 1, :], N).then_inc(padset, 1)
                nc.vector.memset(padw[:, :], 1.0).then_inc(padset, 1)
                c.did(nc.vector.memset(zero[:, :], 0.0))
                c.did(nc.vector.memset(ones[:, :], 1.0))
                dve.wait_ge(endsin, 48)
                c.sync()
                c.did(nc.vector.tensor_scalar(endb[:, :, :], ends[:, :, :], 7, None, ALU.arith_shift_right))
                c.sync()
                c.did(nc.vector.tensor_copy(endf[:, :, :], endb[:, :, :]))
                c.sync()
                c.did(nc.vector.tensor_tensor(inc[:, :], endf[:, 1, :], endf[:, 0, :], ALU.subtract))
                c.sync()
                c.did(nc.vector.tensor_scalar(inc[:, :], inc[:, :], 1.0, None, ALU.add))
                c.sync()
                c.did(nc.vector.tensor_tensor_scan(row[:, 0, :], inc[:, :], zero[:, :], 0.0, ALU.add, ALU.add))
                c.sync()
                c.did(nc.vector.tensor_tensor(row[:, 0, :], row[:, 0, :], inc[:, :], ALU.subtract))
                c.sync()
                nc.vector.tensor_tensor(row[:, 1, :], endf[:, 0, :], row[:, 0, :], ALU.subtract).then_inc(spread, 1)
                dve.wait_ge(spreadback, 1)
                for i in range(4):
                    c.did(nc.vector.tensor_copy(bc[:, i // 2, (i % 2) * ndst:(i % 2 + 1) * ndst], bank[i][:, 0:ndst]))
                c.sync()
                dve.wait_ge(ioted, 4)
                for j in range(SJ):
                    c.did(nc.vector.tensor_scalar(junk[:, :], bc[:, 0, :], sval[:, j:j + 1], None, ALU.is_le, ALU.add,
                                                  accum_out=cnt[:, j:j + 1]))
                    c.sync()
                c.did(nc.vector.tensor_scalar(tsel[:, :], cnt[:, :], -1.0, None, ALU.add))
                c.sync()
                nc.vector.tensor_copy(tidx[:, :], tsel[:, :]).then_inc(planned, 1)
                for j in range(SJ):
                    c.did(nc.vector.scalar_tensor_tensor(junk[:, :], tio[:, :], tsel[:, j:j + 1], bc[:, 1, :],
                                                         ALU.is_equal, ALU.mult, accum_out=qsel[:, j:j + 1]))
                    c.sync()
                c.did(nc.vector.tensor_tensor(breal[:, :], qsel[:, :], sval[:, :], ALU.add))
                c.sync()
                c.did(nc.vector.tensor_scalar(boff[:, :], breal[:, :], float(P), None, ALU.mult))
                c.did(nc.vector.tensor_scalar(bcl[:, :], breal[:, :], float(NB - 1), None, ALU.min))
                c.sync()
                nc.vector.tensor_copy(bint[:, :], bcl[:, :]).then_inc(planned, 1)
                dve.wait_ge(xin, 16 * 5)
                for b in range(NB):
                    nc.vector.bn_stats(m.st[:, b, :], x[:, b, :])
                dve.wait_ge(rowsin, 16 * 3 * SJ)
                nc.vector.tensor_copy(fd[:, :, :], rd[:, :, :]).then_inc(floats, 1)
                nc.vector.tensor_copy(fs[:, :, :], rs[:, :, :]).then_inc(floats, 1)
                dve.wait_ge(floats, 1)
                for j in range(SJ):
                    ins = nc.vector.tensor_scalar(fl[:, j, :], fd[:, j, :], boff[:, j:j + 1], None, ALU.subtract)
                ins.then_inc(floats, 1)
                for q, (out, w) in enumerate(((m.src, 4), (m.src, 3), (m.dl, 4), (m.dl, 3), (m.w, 4), (m.w, 3))):
                    dve.wait_ge(turned, q + 1)
                    o = 4 * P * (q % 2)
                    nc.vector.tensor_copy(out[:, o:o + w * P], bank[q % 4][:, 0:w * P]).then_inc(turnedback, 1)

            @block.tensor
            def _(pe):
                pe.wait_ge(spread, 1)
                for i in range(4):
                    last = nc.tensor.matmul(bank[i][:, 0:ndst], ones[:, :], row[:, i // 2, (i % 2) * ndst:(i % 2 + 1) * ndst],
                                            start=True, stop=True)
                last.then_inc(spreadback, 1)
                pe.wait_ge(floats, 3)
                pe.wait_ge(ioted, 4)
                for q in range(6):
                    rows = (fs, fl, rw)[q // 2]
                    if q >= 4:
                        pe.wait_ge(turnedback, q - 3)
                    for i in range(4 if q % 2 == 0 else SJ - 4):
                        last = nc.tensor.transpose(bank[q % 4][:, i * P:(i + 1) * P], rows[:, 4 * (q % 2) + i, :], m.ident[:, :])
                    last.then_inc(turned, 1)


def blocks_of(nc, m, engine, step, n):
    return nc.values_load_multi_w_load_instructions(m.btab[0:1, bass.ds(step, n)], engines=(engine,), min_val=0, max_val=NB - 1)[1]


def experts_of(nc, m, engine, tile, n):
    return nc.values_load_multi_w_load_instructions(m.etab[0:1, bass.ds(tile, n)], engines=(engine,), min_val=0, max_val=NE - 1)[1]


def finish_stats(dve, act, which, nc, m, st, c, s_var, s_std):
    if which == 1:
        act.wait_ge(s_var, 1)
        nc.scalar.activation(m.tmp1[:, :], m.tmp0[:, :], ACT.Sqrt).then_inc(s_std, 1)
        return
    c.did(nc.vector.tensor_tensor(m.tmp0[:, :], st[:, :, 1], st[:, :, 4], ALU.subtract))
    c.did(nc.vector.tensor_tensor(m.tmp1[:, :], st[:, :, 2], st[:, :, 5], ALU.add))
    c.did(nc.vector.tensor_tensor(m.mean[:, :], st[:, :, 1], st[:, :, 4], ALU.add))
    c.sync()
    c.did(nc.vector.tensor_tensor(m.tmp0[:, :], m.tmp0[:, :], m.tmp0[:, :], ALU.mult))
    c.did(nc.vector.tensor_scalar(m.mean[:, :], m.mean[:, :], 0.5, None, ALU.mult))
    c.sync()
    c.did(nc.vector.scalar_tensor_tensor(m.tmp0[:, :], m.tmp0[:, :], D / 4.0, m.tmp1[:, :], ALU.mult, ALU.add))
    c.sync()
    nc.vector.tensor_scalar(m.tmp0[:, :], m.tmp0[:, :], 1.0 / D, EPS, ALU.mult, ALU.add).then_inc(s_var, 1)
    dve.wait_ge(s_std, 1)
    c.did(nc.vector.reciprocal(m.rstd[:, :], m.tmp1[:, :]))
    c.sync()


def project_nodes(nc, m, a):
    with ExitStack() as ctx:
        def sb(name, shape, dt=F32):
            return ctx.enter_context(nc.sbuf_tensor("pn_" + name, shape, dt))

        x = m.big1[:, 0:NB * D].rearrange("p (b d) -> p b d", d=D)
        xr = m.big0[:, 0:NB * LW].rearrange("p (b d) -> p b d", d=LW)
        m.xr = xr
        st = m.st
        wl, wr = sb("wl", [P, KC, LW]), sb("wr", [P, KC, LW])
        wlt, wrt = sb("wlt", [P, KC, D]), sb("wrt", [P, KC, D])
        bl, br = sb("bl", [P, LW]), sb("br", [P, LW])
        bcol = sb("bcol", [P, 2, KC])
        bwide = sb("bwide", [P, 2, KC, P])
        attc = sb("attc", [P, KC])
        attm = sb("attm", [P, KC, H])
        attl = sb("attl", [P, KC, H])
        xn = sb("xn", [P, 2, D + 1])
        xt = sb("xt", [P, 2, D])
        xls = sb("xls", [P, 2, LW])
        bank = [ctx.enter_context(nc.psum_tensor(f"pn_bank{i}", [P, 512], F32)) for i in range(8)]
        xt_ps, xl_ps, xr_ps, gram_ps = bank[0:2], bank[2:4], bank[4:6], bank[6:8]

        names = ("weights masked attset folded foldedback var std "
                 "xn_ready xt_made xt_ready xtst0 xtst1 xl_made xr_made xl_back xr_back "
                 "xlst0 xlst1 gram_made onesset chain consts").split()
        s = {n: m.sem("pn_" + n) for n in names}
        xt_stored, xl_stored = [s["xtst0"], s["xtst1"]], [s["xlst0"], s["xlst1"]]

        with nc.Block() as block:
            @block.sync
            def _(sp):
                for out, w in ((wl[:, :, 0:D], "L0_gnn_W_l"), (wr[:, :, 0:D], "L0_gnn_W_r"), (wlt[:, :, :], "W_lT"),
                               (wrt[:, :, :], "W_rT")):
                    sp.dma_start(out, a[w].rearrange("(c p) n -> p c n", p=P)).then_inc(s["weights"], 16)
                for out, w in ((bl[:, 0:D], "L0_gnn_b_l"), (br[:, 0:D], "L0_gnn_b_r")):
                    sp.dma_start(out, a[w].partition_broadcast(P)).then_inc(s["weights"], 16)
                for out, w in ((bcol[:, 0, :], "L0_gnn_b_l"), (bcol[:, 1, :], "L0_gnn_b_r")):
                    sp.dma_start(out, a[w].rearrange("(c p) -> p c", p=P), allow_slow_non_contiguous=True).then_inc(s["weights"], 16)
                sp.dma_start(attc[:, :], a["L0_gnn_att"].rearrange("h c -> (h c)").rearrange("(c p) -> p c", p=P), allow_slow_non_contiguous=True).then_inc(s["weights"], 16)

                def store_xt(k, u, r):
                    sp.wait_ge(s["xt_ready"], k + 1)
                    sp.dma_start(m.xnt_d[k] if isinstance(k, int) else m.xnt_d[bass.ds(k, 1)].rearrange("a p d -> (a p) d"),
                                 xt[:, u, :]).then_inc(xt_stored[u], 16)

                def store_xl(k, u, r):
                    sp.wait_ge(s["xl_back"], k + 1)
                    sp.dma_start(m.xl_d[k] if isinstance(k, int) else m.xl_d[bass.ds(k, 1)].rearrange("a p d -> (a p) d"),
                                 xls[:, u, :]).then_inc(xl_stored[u], 16)
                pipeline(sp, NB, 2, (0, store_xt), (0, store_xl))
                for u in range(2):
                    sp.wait_ge(xt_stored[u], 16 * ((NB + 1 - u) // 2))
                    sp.wait_ge(xl_stored[u], 16 * ((NB + 1 - u) // 2))

            @block.gpsimd
            def _(pool):
                nc.gpsimd.memset(attm[:, :, :], 1.0).then_inc(s["masked"], 1)
                pool.wait_ge(s["masked"], 1)
                nc.gpsimd.affine_select(out=attm[:, :, :], in_=attm[:, :, :], compare_op=ALU.is_ge, fill=0.0, base=0,
                                        pattern=[[P, KC], [-HC, H]], channel_multiplier=1).then_inc(s["masked"], 1)
                pool.wait_ge(s["masked"], 2)
                nc.gpsimd.affine_select(out=attm[:, :, :], in_=attm[:, :, :], compare_op=ALU.is_ge, fill=0.0, base=HC - 1,
                                        pattern=[[-P, KC], [HC, H]], channel_multiplier=-1).then_inc(s["masked"], 1)

            @block.vector
            def _(dve):
                c = Chain(dve, s["chain"])
                dve.wait_ge(s["weights"], 16 * 9)
                dve.wait_ge(s["masked"], 3)
                for q in range(KC):
                    c.did(nc.vector.tensor_scalar(m.atta[:, q, :], attm[:, q, :], attc[:, q:q + 1], (1 - SLOPE) / 2,
                                                  ALU.mult, ALU.mult))
                    c.did(nc.vector.tensor_scalar(attl[:, q, :], attm[:, q, :], attc[:, q:q + 1], (1 + SLOPE) / 2,
                                                  ALU.mult, ALU.mult))
                    for w in range(2):
                        c.did(nc.vector.tensor_scalar(bwide[:, w, q, :], m.iota[:, :], 0.0, bcol[:, w, q:q + 1],
                                                      ALU.mult, ALU.add))
                c.sync()
                nc.vector.memset(m.ones[:, :], 1.0).then_inc(s["attset"], 1)
                dve.wait_ge(s["folded"], 1)
                for w, (wt, bt) in enumerate(((wl, bl), (wr, br))):
                    for q in range(KC):
                        c.did(nc.vector.tensor_copy(wt[:, q, D:LW], bank[w][:, H * q:H * q + H]))
                    c.did(nc.vector.tensor_copy(bt[:, D:LW], bank[w][:, H * KC:H * KC + H]))
                c.sync()
                nc.vector.memset(m.tmp0[:, 0:1], 0.0).then_inc(s["foldedback"], 1)
                dve.wait_ge(s["foldedback"], 1)
                finish_stats(dve, None, 0, nc, m, st, c, s["var"], s["std"])

                nc.vector.memset(xn[:, :, D:D + 1], 1.0).then_inc(s["onesset"], 1)

                def normalise(k, u, r):
                    if at_least(k, 2):
                        dve.wait_ge(s["gram_made"], k - 1)
                    xk = x[:, k, :] if isinstance(k, int) else x[:, bass.ds(k, 1), :].rearrange("p a d -> p (a d)")
                    nc.vector.tensor_scalar(xn[:, u, 0:D], xk, m.mean[:, bass.ds(k, 1)], m.rstd[:, bass.ds(k, 1)],
                                            ALU.subtract, ALU.mult).then_inc(s["xn_ready"], 1)

                def evacuate(k, u, r):
                    dve.wait_ge(s["xl_made"], k + 1)
                    if at_least(k, 2):
                        dve.wait_ge(xl_stored[u], 16 * r)
                    nc.vector.tensor_tensor(xls[:, u, :], xl_ps[u][:, 0:LW], bl[:, :], ALU.add).then_inc(s["xl_back"], 1)
                    dve.wait_ge(s["xr_made"], k + 1)
                    nc.vector.tensor_tensor(xr[:, bass.ds(k, 1), :].rearrange("p a d -> p (a d)"), xr_ps[u][:, 0:LW], br[:, :],
                                            ALU.add).then_inc(s["xr_back"], 1)
                pipeline(dve, NB, 2, (0, normalise), (2, evacuate))
                dve.wait_ge(s["gram_made"], NB)
                for q in range(KC):
                    ins = nc.vector.tensor_copy(m.gram[:, q, :], gram_ps[q][:, 0:D + 1])
                ins.then_inc(s["consts"], 1)

            @block.scalar
            def _(act):
                finish_stats(None, act, 1, nc, m, st, None, s["var"], s["std"])

                def evacuate(k, u, r):
                    act.wait_ge(s["xt_made"], k + 1)
                    if at_least(k, 2):
                        act.wait_ge(s["xr_made"], k - 1)
                        act.wait_ge(xt_stored[u], 16 * r)
                    nc.scalar.copy(xt[:, u, :], xt_ps[u][:, 0:D]).then_inc(s["xt_ready"], 1)
                pipeline(act, NB, 2, (0, evacuate))

            @block.tensor
            def _(pe):
                pe.wait_ge(s["attset"], 1)
                for w, wt in enumerate((wlt, wrt)):
                    for q in range(KC):
                        for h in range(KC):
                            nc.tensor.matmul(bank[w][:, H * q:H * q + H], wt[:, h, q * P:(q + 1) * P], attl[:, h, :],
                                             start=(h == 0), stop=(h == KC - 1))
                    for h in range(KC):
                        last = nc.tensor.matmul(bank[w][:, H * KC:H * KC + H], bwide[:, w, h, :], attl[:, h, :],
                                                start=(h == 0), stop=(h == KC - 1))
                last.then_inc(s["folded"], 1)
                pe.wait_ge(s["foldedback"], 1)

                def turn(k, u, r):
                    pe.wait_ge(s["xn_ready"], k + 1)
                    if at_least(k, 2):
                        pe.wait_ge(s["xt_ready"], k - 1)
                    for q in range(KC):
                        last = nc.tensor.transpose(xt_ps[u][:, q * P:(q + 1) * P], xn[:, u, q * P:(q + 1) * P], m.ident[:, :])
                    last.then_inc(s["xt_made"], 1)

                def project(k, u, r):
                    pe.wait_ge(s["xt_ready"], k + 1)
                    for out, w, made, back in ((xl_ps[u], wl, "xl_made", "xl_back"), (xr_ps[u], wr, "xr_made", "xr_back")):
                        if at_least(k, 2):
                            pe.wait_ge(s[back], k - 1)
                        for q in range(KC):
                            last = nc.tensor.matmul(out[:, 0:LW], xt[:, u, q * P:(q + 1) * P], w[:, q, :],
                                                    start=(q == 0), stop=(q == KC - 1))
                        last.then_inc(s[made], 1)

                def gram(k, u, r):
                    rows = LAST if isinstance(k, int) and k == NB - 1 else P
                    first, final = isinstance(k, int) and k == 0, isinstance(k, int) and k == NB - 1
                    for q in range(KC):
                        last = nc.tensor.matmul(gram_ps[q][:, 0:D + 1], xn[0:rows, u, q * P:(q + 1) * P], xn[0:rows, u, :],
                                                start=first, stop=final)
                    last.then_inc(s["gram_made"], 1)
                pe.wait_ge(s["onesset"], 1)
                pipeline(pe, NB, 2, (0, turn), (0, gram), (1, project))


def score_edges(nc, m, a):
    with ExitStack() as ctx:
        def sb(name, shape, dt=F32):
            return ctx.enter_context(nc.sbuf_tensor("se_" + name, shape, dt))

        def ps(name, shape, dt=F32):
            return ctx.enter_context(nc.psum_tensor("se_" + name, shape, dt))

        GP = GS // 2
        HS = GS // 2
        idx = sb("idx", [P, 4, HS], U32)
        xj = sb("xj", [P, 2, GS, LW])
        half_of = lambda u: xj[:, u // 2, (u % 2) * HS:(u % 2 + 1) * HS, :]
        oh, identb = sb("oh", [P, 2, GS, P], BF16), sb("identb", [P, P], BF16)
        oht = sb("oht", [P, 2, GS, P])
        z = sb("z", [P, 2, GS, LW])
        zt = sb("zt", [P, 2, 512])
        oht_ps = ps("oht_ps", [P, 4 * P], BF16)
        z_ps = [ps(f"z_ps{i}", [P, 2, 512]) for i in range(2)]
        zt_ps = [ps(f"zt_ps{i}", [P, 512]) for i in range(2)]
        al_ps = ps("al_ps", [P, 512])
        s = {n: m.sem("se_" + n) for n in
             "indexed issued xj0 xj1 xj2 xj3 st0 st1 st2 st3 oh_ready oht_made oht_ready z_made z_ready zt_made zt_ready att_made al_ready keys".split()}
        landed, stored = [s[f"xj{u}"] for u in range(4)], [s[f"st{u}"] for u in range(4)]
        key = m.big1[:, 0:CL]
        table = m.xl_d.rearrange("b p d -> (b p) d")

        with nc.Block() as block:
            @block.gpsimd
            def _(pool):
                def gather(h, u, r):
                    if at_least(h, 4):
                        pool.wait_ge(landed[u], 16 * HS * r)
                        pool.wait_ge(s["z_ready"], 2 * h - 6)
                        pool.wait_ge(stored[u], 16 * r)
                    nc.gpsimd.tensor_copy(idx[:, u, :], m.src[:, bass.ds(h * HS, HS)]).then_inc(s["indexed"], 1)
                    pool.wait_ge(s["indexed"], h + 1)
                    pool.sem_inc(s["issued"], 1)
                    for k in range(HS):
                        nc.gpsimd.indirect_dma_start(half_of(u)[:, k, :], None, table,
                                                     bass.IndirectOffsetOnAxis(ap=idx[:, u, k:k + 1], axis=0)).then_inc(landed[u], 16)
                pipeline(pool, 2 * NG, 4, (0, gather))

            @block.sync
            def _(sp):
                kd = m.key_d[0:NS, :].rearrange("(c j) e -> c (j e)", c=CH)
                for c in range(CH):
                    sp.dma_start(key[c * H:(c + 1) * H, :], kd[c].partition_broadcast(H)).then_inc(s["keys"], 16)

                def store(h, u, r):
                    sp.wait_ge(landed[u], 16 * HS * (r + 1))
                    sp.dma_start(m.xj_d[bass.ds(h, 1)].rearrange("a p n -> (a p) n"),
                                 half_of(u).rearrange("p k d -> p (k d)")).then_inc(stored[u], 16)
                pipeline(sp, 2 * NG, 4, (0, store))
                sp.wait_ge(s["keys"], 16 * CH)
                for u in range(4):
                    sp.wait_ge(stored[u], 16 * (2 * NG // 4))

            @block.vector
            def _(dve):
                nc.vector.tensor_copy(identb[:, :], m.ident[:, :])
                def one_hot(q, v, r):
                    if v % GP:
                        return
                    u, g = v // GP, 2 * r + v // GP
                    if at_least(q, 2 * GP):
                        dve.wait_ge(s["oht_made"], 2 * (g - 1))
                    nc.vector.tensor_tensor(oh[:, u, :, :], m.iota[:, :].unsqueeze(1).to_broadcast([P, GS, P]),
                                            m.dl[:, bass.ds(g * GS, GS)].unsqueeze(2).to_broadcast([P, GS, P]),
                                            ALU.is_equal).then_inc(s["oh_ready"], 1)

                def add(q, v, r):
                    u, k = v // GP, 2 * (v % GP)
                    if v % 2 == 0:
                        dve.wait_ge(landed[v // 2], 16 * HS * (r + 1))
                    if v % GP == 0:
                        if at_least(q, 2 * GP):
                            dve.wait_ge(s["al_ready"], 2 * r + v // GP - 1)
                    dve.wait_ge(s["z_made"], q + 1)
                    if at_least(q, 2 * GP):
                        dve.wait_ge(s["zt_made"], q - (2 * GP - 1))
                    nc.vector.tensor_tensor(z[:, u, k:k + 2, :], z_ps[v % 2][:, :, 0:LW], xj[:, u, k:k + 2, :],
                                            ALU.add).then_inc(s["z_ready"], 1)

                def scores(q, v, r):
                    if v % GP != GP - 1:
                        return
                    u, g = v // GP, 2 * r + v // GP
                    dve.wait_ge(s["att_made"], q + 1)
                    dve.wait_ge(s["z_ready"], q + 1)
                    nc.vector.tensor_tensor(m.ex[:, bass.ds(g * GS * H, GS * H)].rearrange("p (k h) -> p k h", h=H),
                                            al_ps[:, 0:GS * H].rearrange("p (k h) -> p k h", h=H), z[:, u, :, D:LW],
                                            ALU.add).then_inc(s["al_ready"], 1)
                pipeline(dve, NS // 2, 2 * GP, (7, scores), (0, one_hot), (3, add))

            @block.scalar
            def _(act):
                def one_hot_turned(q, v, r):
                    if v % 2:
                        return
                    u, g, half = v // GP, 2 * r + v // GP, (v % GP) // 2
                    act.wait_ge(s["oht_made"], 2 * g + half + 1)
                    if at_least(q, 2 * GP):
                        act.wait_ge(s["z_made"], GP * (g - 1))
                    nc.scalar.copy(oht[:, u, 4 * half:4 * half + 4, :].rearrange("p k n -> p (k n)"), oht_ps[:, :]).then_inc(s["oht_ready"], 1)

                def absolute(q, v, r):
                    act.wait_ge(s["zt_made"], q + 1)
                    if at_least(q, 2):
                        act.wait_ge(s["att_made"], q - 1)
                    nc.scalar.activation(zt[:, v % 2, :], zt_ps[v % 2][:, :], ACT.Abs).then_inc(s["zt_ready"], 1)
                pipeline(act, NS // 2, 2 * GP, (0, one_hot_turned), (5, absolute))

            @block.tensor
            def _(pe):
                def turn_one_hot(q, v, r):
                    if v % 2:
                        return
                    u, g, half = v // GP, 2 * r + v // GP, (v % GP) // 2
                    pe.wait_ge(s["oh_ready"], g + 1)
                    if at_least(q, 2):
                        pe.wait_ge(s["oht_ready"], 2 * g + half)
                    for k in range(4):
                        last = nc.tensor.transpose(oht_ps[:, k * P:(k + 1) * P], oh[:, u, 4 * half + k, :], identb[:, :])
                    last.then_inc(s["oht_made"], 1)

                def expand(q, v, r):
                    u, k = v // GP, 2 * (v % GP)
                    g = 2 * r + v // GP
                    pe.wait_ge(s["oht_ready"], 2 * g + (v % GP) // 2 + 1)
                    if at_least(q, 2):
                        pe.wait_ge(s["z_ready"], q - 1)
                    blocks = blocks_of(nc, m, mybir.EngineType.PE, q * 2, 2)
                    for i in range(2):
                        last = nc.tensor.matmul(z_ps[v % 2][:, i, 0:LW], oht[:, u, k + i, :], of_block(m.xr, blocks[i]),
                                                start=True, stop=True)
                    last.then_inc(s["z_made"], 1)

                def turn(q, v, r):
                    u, k = v // GP, 2 * (v % GP)
                    pe.wait_ge(s["z_ready"], q + 1)
                    if at_least(q, 2):
                        pe.wait_ge(s["zt_ready"], q - 1)
                    for i in range(2):
                        for c in range(KC):
                            last = nc.tensor.transpose(zt_ps[v % 2][:, i * D + c * P:i * D + (c + 1) * P],
                                                       z[:, u, k + i, c * P:(c + 1) * P], m.ident[:, :])
                    last.then_inc(s["zt_made"], 1)

                def attend(q, v, r):
                    k, g = 2 * (v % GP), 2 * r + v // GP
                    pe.wait_ge(s["zt_ready"], q + 1)
                    if v % GP == 0 and at_least(q, GP):
                        pe.wait_ge(s["al_ready"], g)
                    for i in range(2):
                        for c in range(KC):
                            last = nc.tensor.matmul(al_ps[:, (k + i) * H:(k + i + 1) * H],
                                                    zt[:, v % 2, i * D + c * P:i * D + (c + 1) * P], m.atta[:, c, :],
                                                    start=(c == 0), stop=(c == KC - 1))
                    last.then_inc(s["att_made"], 1)
                pipeline(pe, NS // 2, 2 * GP, (0, turn_one_hot), (2, expand), (4, turn), (6, attend))



def normalise_edges(nc, m, a):
    with ExitStack() as ctx:
        def sb(name, shape, dt=F32):
            return ctx.enter_context(nc.sbuf_tensor("ne_" + name, shape, dt))

        small, lnw, empty = sb("small", [P, NS]), sb("lnw", [P, NS]), sb("empty", [P, NS])
        cols = sb("cols", [P, 4])
        cki, carry = sb("cki", [P, 1]), sb("carry", [P, 2])
        rows = sb("rows", [1, 6, P])
        bank = [ctx.enter_context(nc.psum_tensor(f"ne_bank{i}", [P, 512], F32)) for i in range(4)]
        s = {n: m.sem("ne_" + n) for n in "w ln logw turned back cols rowps rows colps exps exped unturned done chain".split()}
        key, run = m.big1[:, 0:CL], m.big1[:, CL:2 * CL + 1]
        al, top = m.big0[:, 0:CL], m.big0[:, CL:2 * CL]
        exv = m.ex[:, :].rearrange("p (c j h) -> p c j h", c=CH, h=H)
        NQ4 = CS // 4
        assert CS % 4 == 0

        with nc.Block() as block:
            @block.vector
            def _(dve):
                c = Chain(dve, s["chain"])
                V = nc.vector
                w = m.w[:, 0:NS]
                c.did(V.tensor_scalar(small[:, :], w, 2.0 ** -60, None, ALU.is_lt))
                c.did(V.tensor_scalar(empty[:, :], w, 0.0, MASKED, ALU.is_le, ALU.mult))
                c.sync()
                c.did(V.tensor_scalar(lnw[:, :], small[:, :], 2.0 ** 60, 1.0, ALU.mult, ALU.add))
                c.sync()
                c.did(V.tensor_tensor(lnw[:, :], lnw[:, :], w, ALU.mult))
                c.sync()
                V.tensor_scalar(lnw[:, :], lnw[:, :], 2.0 ** -63, None, ALU.max).then_inc(s["w"], 1)
                c.did(V.memset(run[:, 0:1], 0.0))
                c.did(V.memset(run[:, CL:CL + 1], 0.0))
                c.did(V.tensor_tensor(run[:, 1:CL], key[:, 1:CL], key[:, 0:CL - 1], ALU.is_equal))
                c.sync()
                c.did(V.tensor_scalar(run[:, 1:CL], run[:, 1:CL], -1.0, -MASKED, ALU.add, ALU.mult))
                dve.wait_ge(s["ln"], 1)
                c.did(V.scalar_tensor_tensor(lnw[:, :], small[:, :], -60.0 * float(np.log(2.0)), lnw[:, :], ALU.mult, ALU.add))
                c.sync()
                c.did(V.tensor_tensor(lnw[:, :], lnw[:, :], empty[:, :], ALU.add))
                c.sync()
                V.tensor_tensor(top.rearrange("p (j c h) -> p c j h", c=CH, h=H), exv,
                                lnw[:, :].rearrange("p (c j) -> p c j", c=CH).unsqueeze(3).to_broadcast([P, CH, CS, H]),
                                ALU.add).then_inc(s["logw"], 1)
                for q in range(NQ4):
                    dve.wait_ge(s["turned"], q + 1)
                    V.tensor_copy(al[:, q * 512:(q + 1) * 512], bank[q % 4][:, :]).then_inc(s["back"], 1)
                dve.wait_ge(s["back"], NQ4)
                dve.wait_ge(s["turned"], NQ4)
                c.sync()

                def scan(out, forward, initial):
                    if forward:
                        c.did(V.tensor_tensor_scan(out, run[:, 0:CL], al, initial, ALU.add, ALU.max))
                    else:
                        c.did(V.tensor_tensor_scan(out[:, ::-1], run[:, 1:CL + 1][:, ::-1], top[:, ::-1], initial, ALU.add, ALU.max))
                    c.sync()

                c.did(V.tensor_copy(cols[:, 1:2], key[:, 0:1]))
                c.did(V.tensor_copy(cols[:, 2:3], key[:, CL - 1:CL]))
                c.sync()
                for turn, (out, forward) in enumerate(((top, True), (key, False))):
                    scan(out, forward, MASKED)
                    V.tensor_copy(cols[:, 0:1], out[:, CL - 1:CL] if forward else out[:, 0:1]).then_inc(s["cols"], 1)
                    dve.wait_ge(s["rowps"], turn + 1)
                    for i in range(3):
                        v = bank[0][0:1, i * P:(i + 1) * P].rearrange("a (c h) -> a h c", h=H)
                        c.did(V.tensor_copy(rows[:, i, :].rearrange("a (h c) -> a h c", h=H), v if forward else v[:, :, ::-1]))
                    c.sync()
                    far, near = (rows[:, 2, :], rows[:, 1, :]) if forward else (rows[:, 1, :], rows[:, 2, :])
                    hc = lambda r: r.rearrange("a (h c) -> a h c", h=H)
                    c.did(V.memset(rows[:, 3, :], 0.0))
                    c.sync()
                    c.did(V.tensor_tensor(hc(rows[:, 3, :])[:, :, 1:CH], hc(near)[:, :, 1:CH], hc(far)[:, :, 0:CH - 1], ALU.is_equal))
                    c.did(V.tensor_tensor(rows[:, 4, :], near, far, ALU.is_equal))
                    c.sync()
                    c.did(V.tensor_tensor(rows[:, 4, :], rows[:, 4, :], rows[:, 3, :], ALU.mult))
                    c.sync()
                    c.did(V.tensor_scalar(rows[:, 3:5, :], rows[:, 3:5, :], -1.0, -MASKED, ALU.add, ALU.mult))
                    c.sync()
                    c.did(V.tensor_tensor_scan(rows[:, 5, :], rows[:, 4, :], rows[:, 0, :], MASKED, ALU.add, ALU.max))
                    c.did(V.memset(rows[:, 1, :], MASKED))
                    c.sync()
                    c.did(V.tensor_tensor(hc(rows[:, 1, :])[:, :, 1:CH], hc(rows[:, 5, :])[:, :, 0:CH - 1],
                                          hc(rows[:, 3, :])[:, :, 1:CH], ALU.add))
                    c.sync()
                    v = rows[:, 2, :].rearrange("a (c h) -> a h c", h=H)
                    V.tensor_copy(v if forward else v[:, :, ::-1], hc(rows[:, 1, :])).then_inc(s["rows"], 1)
                    dve.wait_ge(s["colps"], turn + 1)
                    c.did(V.tensor_copy(carry[:, turn:turn + 1], bank[1][:, 0:1]))
                    c.sync()
                    scan(out, forward, carry[:, turn:turn + 1])
                for q in range(4):
                    o = slice(q * CL // 4, (q + 1) * CL // 4)
                    V.tensor_tensor(al[:, o], al[:, o], key[:, o], ALU.subtract).then_inc(s["exps"], 1)
                for q in range(NQ4):
                    dve.wait_ge(s["unturned"], q + 1)
                    V.tensor_copy(exv[:, :, 4 * q:4 * q + 4, :].rearrange("p c j h -> p j c h"),
                                  bank[q % 4][:, :].rearrange("p (j c h) -> p j c h", j=4, h=H)).then_inc(s["done"], 1)

            @block.scalar
            def _(act):
                act.wait_ge(s["w"], 1)
                nc.scalar.activation(lnw[:, :], lnw[:, :], ACT.Ln).then_inc(s["ln"], 1)
                for q in range(4):
                    act.wait_ge(s["exps"], q + 1)
                    o = slice(q * CL // 4, (q + 1) * CL // 4)
                    nc.scalar.activation(al[:, o], al[:, o], ACT.Exp).then_inc(s["exped"], 1)

            @block.tensor
            def _(pe):
                pe.wait_ge(s["logw"], 1)
                for q in range(NQ4):
                    if q >= 4:
                        pe.wait_ge(s["back"], q - 3)
                    for i in range(4):
                        last = nc.tensor.transpose(bank[q % 4][:, i * P:(i + 1) * P], top[:, (4 * q + i) * P:(4 * q + i + 1) * P], m.ident[:, :])
                    last.then_inc(s["turned"], 1)
                for turn in range(2):
                    pe.wait_ge(s["cols"], turn + 1)
                    for i in range(3):
                        last = nc.tensor.matmul(bank[0][0:1, i * P:(i + 1) * P], cols[:, i:i + 1], m.ident[:, :], start=True, stop=True)
                    last.then_inc(s["rowps"], 1)
                    pe.wait_ge(s["rows"], turn + 1)
                    nc.tensor.matmul(bank[1][:, 0:1], rows[:, 2, :], m.ones[0:1, 0:1], start=True, stop=True).then_inc(s["colps"], 1)
                for q in range(NQ4):
                    if q >= 4:
                        pe.wait_ge(s["done"], q - 3)
                    pe.wait_ge(s["exped"], min(4, (512 * (q + 1) * 4 - 1) // CL + 1))
                    for i in range(4):
                        j = 4 * q + i
                        last = nc.tensor.transpose(bank[q % 4][:, i * P:(i + 1) * P], al[:, j * P:(j + 1) * P], m.ident[:, :])
                    last.then_inc(s["unturned"], 1)


def aggregate_edges(nc, m, a):
    with ExitStack() as ctx:
        def sb(name, shape, dt=F32):
            return ctx.enter_context(nc.sbuf_tensor("ae_" + name, shape, dt))

        v = sb("v", [P, 3, GS, AW])
        oh = sb("oh", [P, 2, GS, P])
        bank = [ctx.enter_context(nc.psum_tensor(f"ae_bank{i}", [P, 512], F32)) for i in range(8)]
        acc = m.big1[:, 0:NB * AW].rearrange("p (b d) -> p b d", d=AW)
        m.acc = acc
        acc1 = m.big0[:, 0:NB * AW].rearrange("p (b d) -> p b d", d=AW)
        s = {n: m.sem("ae_" + n) for n in "in0 in1 in2 oh_ready low_ready high_ready ex_ready summed added zeroed".split()}
        landed = [s["in0"], s["in1"], s["in2"]]
        LOW = 2
        U = 6

        def exps(g, k0, k1):
            return m.ex[:, bass.ds((g * GS + k0) * H, (k1 - k0) * H)].rearrange("p (k h) -> p k h", h=H)

        def scaled(u, g, k0, k1):
            x = v[:, u, k0:k1, 0:D].rearrange("p k (h c) -> p k h c", h=H)
            return x, exps(g, k0, k1).unsqueeze(3).to_broadcast([P, k1 - k0, H, HC])

        with nc.Block() as block:
            @block.sync
            def _(sp):
                sp.wait_ge(s["zeroed"], 2)

                def load(g, w, r):
                    if at_least(g, 3):
                        sp.wait_ge(s["summed"], GS * (g - 2))
                    for i in range(2):
                        sp.dma_start(v[:, w % 3, i * GS // 2:(i + 1) * GS // 2, 0:LW],
                                     m.xj_d[bass.ds(2 * g + i, 1)].rearrange("a p (k d) -> (a p) k d", d=LW)).then_inc(landed[w % 3], 16)
                pipeline(sp, NG, U, (0, load))

            @block.scalar
            def _(act):
                def weights(g, w, r):
                    act.wait_ge(landed[w % 3], 32 * (2 * r + w // 3 + 1))
                    nc.scalar.copy(v[:, w % 3, :, D:LW], exps(g, 0, GS)).then_inc(s["ex_ready"], 1)
                pipeline(act, NG, U, (0, weights))

            @block.gpsimd
            def _(pool):
                def scale_high(g, w, r):
                    pool.wait_ge(landed[w % 3], 32 * (2 * r + w // 3 + 1))
                    x, ex = scaled(w % 3, g, LOW, GS)
                    nc.gpsimd.tensor_tensor(x, x, ex, ALU.mult).then_inc(s["high_ready"], 1)
                pipeline(pool, NG, U, (0, scale_high))

            @block.vector
            def _(dve):
                V = nc.vector
                V.memset(v[:, :, :, LW:AW], 1.0).then_inc(s["zeroed"], 1)
                V.memset(acc[:, :, :], 0.0).then_inc(s["zeroed"], 1)
                V.memset(acc1[:, :, :], 0.0).then_inc(s["zeroed"], 1)
                dve.wait_ge(s["zeroed"], 3)

                def prepare(g, w, r):
                    if at_least(g, 2):
                        dve.wait_ge(s["summed"], GS * (g - 1))
                    V.tensor_tensor(oh[:, w % 2, :, :], m.iota[:, :].unsqueeze(1).to_broadcast([P, GS, P]),
                                    m.dl[:, bass.ds(g * GS, GS)].unsqueeze(2).to_broadcast([P, GS, P]),
                                    ALU.is_equal).then_inc(s["oh_ready"], 1)
                    dve.wait_ge(landed[w % 3], 32 * (2 * r + w // 3 + 1))
                    x, ex = scaled(w % 3, g, 0, LOW)
                    V.tensor_tensor(x, x, ex, ALU.mult).then_inc(s["low_ready"], 1)

                def add(g, w, r):
                    blocks = blocks_of(nc, m, mybir.EngineType.DVE, g * GS, GS)
                    for k in range(GS):
                        t = g * GS + k
                        dve.wait_ge(s["summed"], t + 1)
                        if at_least(t, 2):
                            dve.wait_ge(s["added"], t - 1)
                        to = of_block((acc, acc1)[k % 2], blocks[k])
                        V.tensor_tensor(to, to, bank[k][:, 0:AW], ALU.add).then_inc(s["added"], 1)
                pipeline(dve, NG, U, (0, prepare), (1, add))
                dve.wait_ge(s["added"], NS)
                V.tensor_tensor(acc[:, :, :], acc[:, :, :], acc1[:, :, :], ALU.add)

            @block.tensor
            def _(pe):
                def total(g, w, r):
                    pe.wait_ge(s["oh_ready"], g + 1)
                    pe.wait_ge(s["ex_ready"], g + 1)
                    pe.wait_ge(s["low_ready"], g + 1)
                    for k in range(GS):
                        if k == LOW:
                            pe.wait_ge(s["high_ready"], g + 1)
                        if at_least(g, 1):
                            pe.wait_ge(s["added"], GS * (g - 1) + k + 1)
                        nc.tensor.matmul(bank[k][:, 0:AW], oh[:, w % 2, k, :], v[:, w % 3, k, :], start=True, stop=True)\
                            .then_inc(s["summed"], 1)
                pipeline(pe, NG, U, (0, total))


def block_rows(table, k):
    return table[bass.ds(k, 1)].rearrange("a p d -> (a p) d")


def of_block(t, k):
    return t[:, bass.ds(k, 1), :].rearrange("p a d -> p (a d)")


def expert_weights0(nc, m, ctx):
    FC = F0 // P
    m.w1_0 = m.big0[:, 0:KC * NE * F0].rearrange("p (c n) -> p c n", c=KC)
    m.b1_0 = m.big0[:, KC * NE * F0:(KC + 1) * NE * F0].rearrange("p (e f) -> p e f", e=NE)
    n = NS * H // (NE * D)
    rest = ctx.enter_context(nc.sbuf_tensor("w2_0", [P, FC - n, NE * D], F32))
    m.w2_0 = [m.ex[:, c * NE * D:(c + 1) * NE * D] for c in range(n)] + [rest[:, c, :] for c in range(FC - n)]
    m.b2_0 = ctx.enter_context(nc.sbuf_tensor("b2_0", [P, NE, D], F32))


def load_expert_weights0(act, m, a, loaded):
    for c in range(KC):
        act.dma_start(m.w1_0[:, c, :].rearrange("p (e f) -> p e f", e=NE),
                      a["L0_ffn_W1"][:, c * P:(c + 1) * P, :].rearrange("e p f -> p e f")).then_inc(loaded, 16)
    for c in range(F0 // P):
        act.dma_start(m.w2_0[c].rearrange("p (e f) -> p e f", e=NE),
                      a["L0_ffn_W2"][:, c * P:(c + 1) * P, :].rearrange("e p f -> p e f")).then_inc(loaded, 16)
    act.dma_start(m.b1_0.rearrange("p e f -> p (e f)"), a["L0_ffn_b1"].rearrange("e f -> (e f)").partition_broadcast(P)).then_inc(loaded, 16)
    act.dma_start(m.b2_0[:, :, :].rearrange("p e f -> p (e f)"), a["L0_ffn_b2"].rearrange("e f -> (e f)").partition_broadcast(P))\
        .then_inc(loaded, 16)
    return 16 * (KC + F0 // P + 2)


def finish_attention(nc, m, a):
    with ExitStack() as ctx:
        def sb(name, shape, dt=F32):
            return ctx.enter_context(nc.sbuf_tensor("fa_" + name, shape, dt))

        wfct, wq = sb("wfct", [P, KC, D]), sb("wq", [P, KC, D])
        bq = sb("bq", [P, KC])
        wkt, wvt = sb("wkt", [P, KC, D]), sb("wvt", [P, KC, D])
        bkv, sums = sb("bkv", [1, 2, D]), sb("sums", [1, 2, D])
        bqw = sb("bqw", [P, KC, P])
        bias, bfc = sb("bias", [P, D]), sb("bfc", [P, D])
        bd = m.bd
        t1, m0 = sb("t1", [P, KC, D]), sb("m0", [P, KC, D])
        rden = sb("rden", [P, NB, H])
        xs, xt = sb("xs", [P, 4, D]), sb("xt", [P, 4, D])
        xb, ga = sb("xb", [P, 2, D]), sb("ga", [P, 2, D])
        bank = [ctx.enter_context(nc.psum_tensor(f"fa_bank{i}", [P, 512], F32)) for i in range(6)]
        s = {n: m.sem("fa_" + n) for n in ("weights masked sums_made sums_back a_made a_back kv_made t1_made t1_back m0_made m0_back x0 x1 x2 x3 xt0 xt1 xt2 xt3 xb_ready mixed "
                                           "ga_ready gb_ready res_ready sqrt_in sqrt chain stat").split()}
        x_in, xt_in = [s[f"x{u}"] for u in range(4)], [s[f"xt{u}"] for u in range(4)]

        with nc.Block() as block:
            @block.sync
            def _(sp):
                for i, w in enumerate(("L0_mix_bk", "L0_mix_bv")):
                    sp.dma_start(bkv[:, i, :], a[w].rearrange("(a n) -> a n", a=1)).then_inc(s["weights"], 16)
                for out, w in ((wkt, "WkT"), (wvt, "WvT"), (wfct, "WfcT"), (wq, "L0_mix_Wq")):
                    sp.dma_start(out[:, :, :], a[w].rearrange("(c p) n -> p c n", p=P)).then_inc(s["weights"], 16)
                sp.dma_start(bq[:, :], a["L0_mix_bq"].rearrange("(c p) -> p c", p=P), allow_slow_non_contiguous=True).then_inc(s["weights"], 16)
                sp.dma_start(bias[:, :], a["L0_gnn_bias"].partition_broadcast(P)).then_inc(s["weights"], 16)
                sp.dma_start(bfc[:, :], a["L0_mix_bfc"].partition_broadcast(P)).then_inc(s["weights"], 16)

                def load(k, u, r):
                    if at_least(k, 4):
                        sp.wait_ge(s["xb_ready"], k - 3)
                        sp.wait_ge(s["mixed"], k - 3)
                    if isinstance(k, int) and k == NB - 1:
                        sp.dma_start(xs[0:LAST, u, :], a["x"][k * P:N, :]).then_inc(x_in[u], 16)
                    else:
                        sp.dma_start(xs[:, u, :], a["x"][bass.ds(k * P, P), :]).then_inc(x_in[u], 16)
                    sp.dma_start(xt[:, u, :], block_rows(m.xnt_d, k)).then_inc(xt_in[u], 16)
                pipeline(sp, NB, 4, (0, load))

            @block.gpsimd
            def _(pool):
                nc.gpsimd.memset(bd[:, :, :], 1.0 / N).then_inc(s["masked"], 1)
                for h in range(P // HC):
                    o = bd[:, :, h * HC:(h + 1) * HC]
                    pool.wait_ge(s["masked"], 1 + 2 * h)
                    nc.gpsimd.affine_select(out=o, in_=o, compare_op=ALU.is_ge, fill=0.0, base=-HC * h,
                                            pattern=[[0, KC], [0, HC]], channel_multiplier=1).then_inc(s["masked"], 1)
                    pool.wait_ge(s["masked"], 2 + 2 * h)
                    nc.gpsimd.affine_select(out=o, in_=o, compare_op=ALU.is_ge, fill=0.0, base=HC * h + HC - 1,
                                            pattern=[[0, KC], [0, HC]], channel_multiplier=-1).then_inc(s["masked"], 1)
                pool.wait_ge(s["m0_back"], 2)

                def add_bias(k, u, r):
                    pool.wait_ge(x_in[u], 16 * (r + 1))
                    if at_least(k, 2):
                        pool.wait_ge(s["gb_ready"], k - 1)
                    nc.gpsimd.tensor_tensor(xb[:, u % 2, :], xs[:, u, :], bias[:, :], ALU.add).then_inc(s["xb_ready"], 1)
                pipeline(pool, NB, 4, (0, add_bias))

            @block.vector
            def _(dve):
                c = Chain(dve, s["chain"])
                V = nc.vector
                V.tensor_scalar(m.tmp0[:, :], m.acc[:, :, LW], 1.0, None, ALU.add).then_inc(s["sqrt_in"], 1)
                c.did(V.tensor_scalar(rden[:, :, :], m.acc[:, :, D:LW], 1e-16, None, ALU.add))
                c.sync()
                c.did(V.reciprocal(rden[:, :, :], rden[:, :, :]))
                dve.wait_ge(s["sqrt"], 1)
                c.did(V.reciprocal(m.dinv[:, :], m.tmp1[:, :]))
                dve.wait_ge(s["weights"], 16 * 9)
                dve.wait_ge(s["sums_made"], 1)
                V.tensor_copy(sums[:, 0, :], bank[0][0:1, 0:D]).then_inc(s["sums_back"], 1)
                V.scalar_tensor_tensor(sums[:, 1, :], bkv[:, 0, :], float(N), bank[1][0:1, 0:D], ALU.mult, ALU.add)\
                    .then_inc(s["sums_back"], 1)
                dve.wait_ge(s["a_made"], 1)
                for q in range(KC):
                    ins = V.tensor_copy(t1[:, q, :], bank[2 + q][:, 0:D])
                ins.then_inc(s["a_back"], 1)
                dve.wait_ge(s["masked"], 1 + 2 * P // HC)
                dve.wait_ge(s["kv_made"], 1)
                for q in range(KC):
                    c.did(V.tensor_tensor(m.kvt[:, q, :], bank[4 + q][:, 0:P], bd[:, q, :], ALU.mult))
                for q in range(KC):
                    c.did(V.tensor_scalar(bqw[:, q, :], m.iota[:, :], 0.0, bq[:, q:q + 1], ALU.mult, ALU.add))
                c.did(V.tensor_tensor(bias[:, :], bias[:, :], bfc[:, :], ALU.add))
                c.sync()
                V.memset(m.tmp0[:, 0:1], 0.0).then_inc(s["t1_back"], 1)
                dve.wait_ge(s["t1_made"], 1)
                for q in range(KC):
                    ins = V.tensor_copy(t1[:, q, :], bank[q][:, 0:D])
                ins.then_inc(s["t1_back"], 1)
                dve.wait_ge(s["m0_made"], 1)
                for q in range(KC):
                    ins = V.tensor_copy(m0[:, q, :], bank[2 + q][:, 0:D])
                ins.then_inc(s["m0_back"], 1)
                V.tensor_tensor(bias[:, :], bias[:, :], bank[4][:, 0:D], ALU.add).then_inc(s["m0_back"], 1)

                def combine(k, u, r):
                    rd = of_block(rden, k).unsqueeze(2).to_broadcast([P, H, HC])
                    if at_least(k, 2):
                        dve.wait_ge(s["gb_ready"], k - 1)
                    V.tensor_tensor(ga[:, u % 2, :].rearrange("p (h c) -> p h c", h=H),
                                    m.acc[:, bass.ds(k, 1), 0:D].rearrange("p a (h c) -> p (a h) c", h=H), rd,
                                    ALU.mult).then_inc(s["ga_ready"], 1)

                def add(k, u, r):
                    dve.wait_ge(s["ga_ready"], k + 1)
                    dve.wait_ge(s["xb_ready"], k + 1)
                    V.tensor_tensor(ga[:, u % 2, :], ga[:, u % 2, :], xb[:, u % 2, :], ALU.add).then_inc(s["gb_ready"], 1)

                def finish(k, u, r):
                    dve.wait_ge(s["gb_ready"], k + 1)
                    dve.wait_ge(s["mixed"], k + 1)
                    V.tensor_tensor(m.acc[:, bass.ds(k, 1), 0:D].rearrange("p a d -> p (a d)"), ga[:, u % 2, :], bank[u % 2][:, 0:D],
                                    ALU.add).then_inc(s["res_ready"], 1)

                def stats(k, u, r):
                    dve.wait_ge(s["res_ready"], k + 1)
                    V.bn_stats(of_block(m.st, k), m.acc[:, bass.ds(k, 1), 0:D].rearrange("p a d -> p (a d)")).then_inc(s["stat"], 1)
                pipeline(dve, NB, 4, (2, stats), (1, finish), (0, combine), (0, add))

            @block.scalar
            def _(act):
                act.wait_ge(s["sqrt_in"], 1)
                nc.scalar.activation(m.tmp1[:, :], m.tmp0[:, :], ACT.Sqrt).then_inc(s["sqrt"], 1)

            @block.tensor
            def _(pe):
                pe.wait_ge(s["weights"], 16 * 9)
                for q in range(KC):
                    nc.tensor.matmul(bank[0][0:1, q * P:(q + 1) * P], m.gram[:, q, D:D + 1], m.ident[:, :], start=True, stop=True)
                for q in range(KC):
                    last = nc.tensor.matmul(bank[1][0:1, 0:D], m.gram[:, q, D:D + 1], wkt[:, q, :], start=(q == 0), stop=(q == KC - 1))
                last.then_inc(s["sums_made"], 1)
                pe.wait_ge(s["sums_back"], 2)
                for q in range(KC):
                    for h in range(KC):
                        nc.tensor.matmul(bank[2 + q][:, 0:D], m.gram[:, h, q * P:(q + 1) * P], wkt[:, h, :], start=(h == 0), stop=False)
                    last = nc.tensor.matmul(bank[2 + q][:, 0:D], sums[:, 0, q * P:(q + 1) * P], bkv[:, 0, :], start=False, stop=True)
                last.then_inc(s["a_made"], 1)
                pe.wait_ge(s["a_back"], 1)
                for q in range(KC):
                    o = slice(q * P, (q + 1) * P)
                    for h in range(KC):
                        nc.tensor.matmul(bank[4 + q][:, 0:P], wvt[:, h, o], t1[:, h, o], start=(h == 0), stop=False)
                    last = nc.tensor.matmul(bank[4 + q][:, 0:P], bkv[:, 1, o], sums[:, 1, o], start=False, stop=True)
                last.then_inc(s["kv_made"], 1)
                pe.wait_ge(s["t1_back"], 1)
                for q in range(KC):
                    last = nc.tensor.matmul(bank[q][:, 0:D], m.kvt[:, q, :], wfct[:, q, :], start=True, stop=True)
                last.then_inc(s["t1_made"], 1)
                pe.wait_ge(s["t1_back"], 2)
                for q in range(KC):
                    for h in range(KC):
                        nc.tensor.matmul(bank[2 + q][:, 0:D], wq[:, h, q * P:(q + 1) * P], t1[:, h, :],
                                         start=(h == 0), stop=(h == KC - 1))
                for h in range(KC):
                    last = nc.tensor.matmul(bank[4][:, 0:D], bqw[:, h, :], t1[:, h, :], start=(h == 0), stop=(h == KC - 1))
                last.then_inc(s["m0_made"], 1)
                pe.wait_ge(s["m0_back"], 2)

                def mix(k, u, r):
                    pe.wait_ge(xt_in[u], 16 * (r + 1))
                    if at_least(k, 2):
                        pe.wait_ge(s["res_ready"], k - 1)
                    for q in range(KC):
                        last = nc.tensor.matmul(bank[u % 2][:, 0:D], xt[:, u, q * P:(q + 1) * P], m0[:, q, :],
                                                start=(q == 0), stop=(q == KC - 1))
                    last.then_inc(s["mixed"], 1)
                pipeline(pe, NB, 4, (0, mix))


def top_one(V, c, m, score, mask, best, cand):
    e8 = m.e8[:, :].unsqueeze(1).to_broadcast([P, NB, NE])
    c.did(V.tensor_reduce(best[:, :], score, AX.X, ALU.max))
    c.sync()
    c.did(V.tensor_tensor(cand, score, best[:, :].unsqueeze(2).to_broadcast([P, NB, NE]), ALU.is_equal))
    c.sync()
    c.did(V.tensor_tensor(cand, cand, e8, ALU.mult))
    c.sync()
    c.did(V.tensor_reduce(m.tmp1[:, :], cand, AX.X, ALU.min))
    c.sync()
    c.did(V.tensor_tensor(mask, e8, m.tmp1[:, :].unsqueeze(2).to_broadcast([P, NB, NE]), ALU.is_equal))
    c.sync()


def route(nc, m, a, layer):
    with ExitStack() as ctx:
        def sb(name, shape, dt=F32):
            return ctx.enter_context(nc.sbuf_tensor(f"r{layer}_" + name, shape, dt))

        wg, bg = sb("wg", [P, KC, NE]), sb("bg", [P, NE])
        xn, xt = sb("xn", [P, 4, D]), sb("xt", [P, 4, D])
        score = sb("score", [P, NB, NE])
        mask1, mask2, both = sb("mask1", [P, NB, NE]), sb("mask2", [P, NB, NE]), sb("both", [P, NB, NE])
        cand, tot, incl = sb("cand", [P, NB, NE]), sb("tot", [P, NE, NB]), sb("incl", [P, NE, NB])
        slot, notfirst = sb("slot", [P, NB, NE]), m.notfirst
        valid, best, tri = sb("valid", [P, NB]), sb("best", [P, NB]), sb("tri", [P, P])
        base, tiles, tint = sb("base", [P, NE]), sb("tiles", [P, NE]), sb("tint", [P, NE], I32)
        trow = sb("trow", [1, T0])
        sf = sb("sf", [P, 2, NB])
        disp = sb("disp", [P, 2, 7, D])
        didx = sb("didx", [P, 2, 2, 7], U32)
        bank = [ctx.enter_context(nc.psum_tensor(f"r{layer}_bank{i}", [P, 512], F32)) for i in range(8)]
        s = {n: m.sem(f"r{layer}_" + n) for n in ("weights masks var std xn_ready xt_made xt_ready g_made g_back counted "
                                                  "totals chain l_in exped slots d_ready indexed issued sent0 sent1 experts").split()}
        sent = [s["sent0"], s["sent1"]]
        buf = (m.buf0_d, m.buf1_d)[layer]
        res = m.acc
        pairs = 2 - layer

        def rows_of(k):
            return res[:, bass.ds(k, 1), 0:D].rearrange("p a d -> p (a d)")

        with nc.Block() as block:
            @block.sync
            def _(sp):
                w, b = (("L0_ffn_Wg", "L0_ffn_bg"), ("L1_ffn_gate_w", "L1_ffn_gate_b"))[layer]
                sp.dma_start(wg[:, :, :], a[w].rearrange("(c p) n -> p c n", p=P)).then_inc(s["weights"], 16)
                sp.dma_start(bg[:, :], a[b].partition_broadcast(P)).then_inc(s["weights"], 16)

            @block.gpsimd
            def _(pool):
                nc.gpsimd.memset(tri[:, :], 1.0).then_inc(s["masks"], 1)
                nc.gpsimd.memset(valid[:, :], 1.0).then_inc(s["masks"], 1)
                nc.gpsimd.memset(notfirst[:, :, :], 1.0).then_inc(s["masks"], 1)
                nc.gpsimd.iota(m.e8[:, :], [[1, NE]], base=-NE, channel_multiplier=0,
                               allow_small_or_imprecise_dtypes=True).then_inc(s["masks"], 1)
                pool.wait_ge(s["masks"], 4)
                nc.gpsimd.affine_select(out=tri[:, :], in_=tri[:, :], compare_op=ALU.is_ge, fill=0.0, base=-1,
                                        pattern=[[1, P]], channel_multiplier=-1).then_inc(s["masks"], 1)
                nc.gpsimd.affine_select(out=valid[:, :], in_=valid[:, :], compare_op=ALU.is_ge, fill=0.0, base=N - 1,
                                        pattern=[[-P, NB]], channel_multiplier=-1).then_inc(s["masks"], 1)
                nc.gpsimd.affine_select(out=notfirst[:, :, :], in_=notfirst[:, :, :], compare_op=ALU.is_ge, fill=0.0, base=-1,
                                        pattern=[[0, NE], [1, NB]], channel_multiplier=0).then_inc(s["masks"], 1)
                pool.wait_ge(s["slots"], 1)

                def dispatch(g, u, r):
                    if at_least(g, 2):
                        pool.wait_ge(sent[u], 16 * 7 * pairs * r)
                    for e in range(pairs):
                        nc.gpsimd.tensor_copy(didx[:, u, e, :], m.slots[:, e, bass.ds(g * 7, 7)]).then_inc(s["indexed"], 1)
                    pool.wait_ge(s["d_ready"], 7 * g + 7)
                    pool.sem_inc(s["issued"], 1)
                    pool.wait_ge(s["indexed"], pairs * (g + 1))
                    pool.sem_inc(s["issued"], 1)
                    for i in range(7):
                        for e in range(pairs):
                            nc.gpsimd.indirect_dma_start(buf, bass.IndirectOffsetOnAxis(ap=didx[:, u, e, i:i + 1], axis=0),
                                                         disp[:, u, i, :], None, bounds_check=buf.shape[0] - 1,
                                                         oob_is_err=False).then_inc(sent[u], 16)
                pipeline(pool, NB // 7, 2, (0, dispatch))
                for u in range(2):
                    pool.wait_ge(sent[u], 16 * 7 * pairs * ((NB // 7 + 1 - u) // 2))

            @block.vector
            def _(dve):
                c = Chain(dve, s["chain"])
                V = nc.vector
                finish_stats(dve, None, 0, nc, m, m.st, c, s["var"], s["std"])
                dve.wait_ge(s["weights"], 32)

                def normalise(k, u, r):
                    if at_least(k, 4):
                        dve.wait_ge(s["xt_made"], k - 3)
                    V.tensor_scalar(xn[:, u, :], rows_of(k), m.mean[:, bass.ds(k, 1)], m.rstd[:, bass.ds(k, 1)],
                                    ALU.subtract, ALU.mult).then_inc(s["xn_ready"], 1)

                def gate(k, u, r):
                    dve.wait_ge(s["g_made"], k + 1)
                    V.tensor_tensor(of_block(score, k), bank[4 + u % 2][:, 0:NE], bg[:, :], ALU.add).then_inc(s["g_back"], 1)
                pipeline(dve, NB, 4, (0, normalise), (5, gate))
                dve.wait_ge(s["g_back"], NB)
                dve.wait_ge(s["masks"], 7)
                vb = valid[:, :].unsqueeze(2).to_broadcast([P, NB, NE])
                top_one(V, c, m, score[:, :, :], mask1[:, :, :], best, cand[:, :, :])
                if layer == 0:
                    c.did(V.scalar_tensor_tensor(slot[:, :, :], mask1[:, :, :], MASKED, score[:, :, :], ALU.mult, ALU.add))
                    c.sync()
                    top_one(V, c, m, slot[:, :, :], mask2[:, :, :], best, cand[:, :, :])
                    c.did(V.tensor_tensor(mask2[:, :, :], mask2[:, :, :], vb, ALU.mult))
                else:
                    c.did(V.tensor_tensor(slot[:, :, :], score[:, :, :], best[:, :].unsqueeze(2).to_broadcast([P, NB, NE]), ALU.subtract))
                    c.sync()
                    V.memset(m.tmp0[:, 0:1], 0.0).then_inc(s["l_in"], 1)
                    dve.wait_ge(s["exped"], 1)
                    c.did(V.tensor_reduce(m.prob[:, :], slot[:, :, :], AX.X, ALU.add))
                    c.sync()
                    c.did(V.reciprocal(m.prob[:, :], m.prob[:, :]))
                c.did(V.tensor_tensor(mask1[:, :, :], mask1[:, :, :], vb, ALU.mult))
                c.sync()
                if layer == 0:
                    V.tensor_tensor(both[:, :, :], mask1[:, :, :], mask2[:, :, :], ALU.add).then_inc(s["counted"], 1)
                else:
                    V.tensor_copy(both[:, :, :], mask1[:, :, :]).then_inc(s["counted"], 1)
                dve.wait_ge(s["totals"], 1)
                c.did(V.tensor_copy(tot[:, :, :], bank[7][:, 0:NB * NE].rearrange("p (b e) -> p e b", e=NE)))
                c.sync()
                flat = lambda t: t[:, :, :].rearrange("p e b -> p (e b)")
                c.did(V.tensor_tensor_scan(flat(incl), flat(notfirst), flat(tot), 0.0, ALU.mult, ALU.add))
                c.sync()
                c.did(V.tensor_tensor(flat(tot), flat(incl), flat(tot), ALU.subtract))
                c.did(V.tensor_scalar(tiles[:, :], incl[:, :, NB - 1], float(P - 1), None, ALU.add))
                c.sync()
                c.did(V.tensor_tensor(slot[:, :, :], bank[6][:, 0:NB * NE].rearrange("p (b e) -> p b e", e=NE),
                                      tot[:, :, :].rearrange("p e b -> p b e"), ALU.add))
                if layer == 0:
                    c.did(V.tensor_copy(tint[:, :], tiles[:, :]))
                    c.sync()
                    c.did(V.tensor_scalar(tint[:, :], tint[:, :], 7, None, ALU.arith_shift_right))
                    c.sync()
                    c.did(V.tensor_copy(tiles[:, :], tint[:, :]))
                    c.did(V.memset(best[:, 0:NE], 0.0))
                    c.sync()
                    c.did(V.tensor_tensor_scan(base[:, :], tiles[:, :], best[:, 0:NE], 0.0, ALU.add, ALU.add))
                    c.sync()
                    c.did(V.tensor_tensor(base[:, :], base[:, :], tiles[:, :], ALU.subtract))
                    c.sync()
                    c.did(V.memset(trow[:, :], -1.0))
                    c.sync()
                    for e in range(NE):
                        c.did(V.scalar_tensor_tensor(trow[:, :], m.iota[0:1, 0:T0], base[0:1, e:e + 1], trow[:, :], ALU.is_ge, ALU.add))
                        c.sync()
                    c.did(V.tensor_copy(m.etab[:, :], trow[:, :]))
                    c.did(V.tensor_scalar(base[:, :], base[:, :], float(P), None, ALU.mult))
                    c.sync()
                    c.did(V.tensor_tensor(slot[:, :, :], slot[:, :, :], base[:, :].unsqueeze(1).to_broadcast([P, NB, NE]), ALU.add))
                c.sync()
                for e, mask in enumerate((mask1, mask2)[0:pairs]):
                    c.did(V.tensor_tensor(cand[:, :, :], mask[:, :, :], slot[:, :, :], ALU.mult))
                    c.sync()
                    c.did(V.tensor_reduce(sf[:, e, :], cand[:, :, :], AX.X, ALU.add))
                    c.sync()
                c.did(V.tensor_scalar(valid[:, :], valid[:, :], -1.0, -1.0e6, ALU.add, ALU.mult))
                c.sync()
                if layer == 0:
                    for e in range(2):
                        c.did(V.tensor_copy(m.back[:, e, :], sf[:, e, :]))
                        c.did(V.tensor_tensor(m.slots[:, e, :], sf[:, e, :], valid[:, :], ALU.add))
                else:
                    e8 = m.e8[:, :].unsqueeze(1).to_broadcast([P, NB, NE])
                    c.did(V.tensor_tensor(cand[:, :, :], mask1[:, :, :], e8, ALU.mult))
                    c.did(V.tensor_scalar(m.tmp0[:, :], sf[:, 0, :], float(CAP), None, ALU.is_ge))
                    c.did(V.tensor_scalar(sf[:, 1, :], sf[:, 0, :], float(CAP - 1), None, ALU.min))
                    c.sync()
                    c.did(V.tensor_reduce(best[:, :], cand[:, :, :], AX.X, ALU.add))
                    c.sync()
                    c.did(V.tensor_scalar(best[:, :], best[:, :], -1.0, None, ALU.min))
                    c.sync()
                    c.did(V.tensor_scalar(best[:, :], best[:, :], float(NE), float(CT * P), ALU.add, ALU.mult))
                    c.sync()
                    for e in range(2):
                        c.did(V.tensor_tensor(sf[:, e, :], sf[:, e, :], best[:, :], ALU.add))
                    c.did(V.scalar_tensor_tensor(valid[:, :], m.tmp0[:, :], 1.0e6, valid[:, :], ALU.mult, ALU.add))
                    c.did(V.tensor_scalar(m.tmp1[:, :], m.tmp0[:, :], -1.0, 1.0, ALU.mult, ALU.add))
                    c.sync()
                    c.did(V.tensor_tensor(m.prob[:, :], m.prob[:, :], m.tmp1[:, :], ALU.mult))
                    c.did(V.tensor_copy(m.back[:, 0, :], sf[:, 1, :]))
                    c.did(V.tensor_tensor(m.slots[:, 0, :], sf[:, 0, :], valid[:, :], ALU.add))
                c.sync()
                V.memset(m.tmp0[:, 0:1], 0.0).then_inc(s["slots"], 1)

                def disperse(k, v, r):
                    g = 2 * r + v // 7
                    if v % 7 == 0 and at_least(k, 14):
                        dve.wait_ge(sent[v // 7], 16 * 7 * pairs * r)
                    V.tensor_scalar(disp[:, v // 7, v % 7, :], rows_of(k), m.mean[:, bass.ds(k, 1)], m.rstd[:, bass.ds(k, 1)],
                                    ALU.subtract, ALU.mult).then_inc(s["d_ready"], 1)
                pipeline(dve, NB, 14, (0, disperse))

            @block.scalar
            def _(act):
                if layer == 0:
                    loads = load_expert_weights0(act, m, a, s["experts"])
                else:
                    for e in range(2):
                        load_expert_weights1(act, m, a, e, e, s["experts"])
                    loads = 64
                finish_stats(None, act, 1, nc, m, m.st, None, s["var"], s["std"])

                def evacuate(k, u, r):
                    act.wait_ge(s["xt_made"], k + 1)
                    if at_least(k, 4):
                        act.wait_ge(s["g_made"], k - 3)
                    nc.scalar.copy(xt[:, u, :], bank[u][:, 0:D]).then_inc(s["xt_ready"], 1)
                pipeline(act, NB, 4, (0, evacuate))
                if layer == 1:
                    act.wait_ge(s["l_in"], 1)
                    nc.scalar.activation(slot[:, :, :], slot[:, :, :], ACT.Exp).then_inc(s["exped"], 1)
                act.wait_ge(s["experts"], loads)

            @block.tensor
            def _(pe):
                def turn(k, u, r):
                    pe.wait_ge(s["xn_ready"], k + 1)
                    if at_least(k, 4):
                        pe.wait_ge(s["xt_ready"], k - 3)
                    for q in range(KC):
                        last = nc.tensor.transpose(bank[u][:, q * P:(q + 1) * P], xn[:, u, q * P:(q + 1) * P], m.ident[:, :])
                    last.then_inc(s["xt_made"], 1)

                def gate(k, u, r):
                    pe.wait_ge(s["xt_ready"], k + 1)
                    if at_least(k, 2):
                        pe.wait_ge(s["g_back"], k - 1)
                    else:
                        pe.wait_ge(s["weights"], 32)
                    for q in range(KC):
                        last = nc.tensor.matmul(bank[4 + u % 2][:, 0:NE], xt[:, u, q * P:(q + 1) * P], wg[:, q, :],
                                                start=(q == 0), stop=(q == KC - 1))
                    last.then_inc(s["g_made"], 1)
                pipeline(pe, NB, 4, (0, turn), (3, gate))
                pe.wait_ge(s["counted"], 1)
                flat = both[:, :, :].rearrange("p b e -> p (b e)")
                nc.tensor.matmul(bank[6][:, 0:NB * NE], tri[:, :], flat, start=True, stop=True)
                nc.tensor.matmul(bank[7][:, 0:NB * NE], m.ones[:, :], flat, start=True, stop=True).then_inc(s["totals"], 1)



def experts0(nc, m, a):
    with ExitStack() as ctx:
        def sb(name, shape, dt=F32):
            return ctx.enter_context(nc.sbuf_tensor("e0_" + name, shape, dt))

        FC = F0 // P
        w1, b1, w2, b2 = m.w1_0, m.b1_0, m.w2_0, m.b2_0
        xs, xt = sb("xs", [P, 2, D]), sb("xt", [P, 2, D])
        hb, hg, ht = sb("hb", [P, F0]), sb("hg", [P, F0]), sb("ht", [P, 2, F0])
        y = sb("y", [P, 2, D])
        bank = [ctx.enter_context(nc.psum_tensor(f"e0_bank{i}", [P, 512], F32)) for i in range(8)]
        xt_ps, h_ps, ht_ps, y_ps = bank[0:2], bank[2:4], bank[4:6], bank[6:8]
        s = {n: m.sem("e0_" + n) for n in ("x0 x1 y0 y1 xt_made xt_ready h_made hb_ready hg_ready ht_made ht_ready "
                                           "y_made y_ready").split()}
        x_in, y_out = [s["x0"], s["x1"]], [s["y0"], s["y1"]]

        with nc.Block() as block:
            @block.sync
            def _(sp):
                def load(j, u, r):
                    if at_least(j, 2):
                        sp.wait_ge(s["xt_made"], j - 1)
                    sp.dma_start(xs[:, u, :], m.buf0_d[bass.ds(j * P, P), :]).then_inc(x_in[u], 16)

                def store(j, u, r):
                    sp.wait_ge(s["y_ready"], j + 1)
                    sp.dma_start(m.y0_d[bass.ds(j * P, P), :], y[:, u, :]).then_inc(y_out[u], 16)
                pipeline(sp, T0, 2, (0, load), (6, store))
                for u in range(2):
                    sp.wait_ge(y_out[u], 16 * T0 // 2)

            @block.vector
            def _(dve):
                V = nc.vector

                bias1_e = []

                def bias1(j, u, r):
                    if u == 0:
                        bias1_e[:] = experts_of(nc, m, mybir.EngineType.DVE, j, 2)
                    e = bias1_e[u]
                    dve.wait_ge(s["h_made"], j + 1)
                    if at_least(j, 1):
                        dve.wait_ge(s["hg_ready"], j)
                    V.tensor_tensor(hb[:, :], h_ps[u][:, :], of_block(b1, e), ALU.add).then_inc(s["hb_ready"], 1)

                def turned(j, u, r):
                    dve.wait_ge(s["ht_made"], j + 1)
                    if at_least(j, 2):
                        dve.wait_ge(s["y_made"], j - 1)
                    V.tensor_copy(ht[:, u, :], ht_ps[u][:, :]).then_inc(s["ht_ready"], 1)

                bias2_e = []

                def bias2(j, u, r):
                    if u == 0:
                        bias2_e[:] = experts_of(nc, m, mybir.EngineType.DVE, j, 2)
                    e = bias2_e[u]
                    dve.wait_ge(s["y_made"], j + 1)
                    if at_least(j, 2):
                        dve.wait_ge(y_out[u], 16 * r)
                    V.tensor_tensor(y[:, u, :], y_ps[u][:, 0:D], of_block(b2, e), ALU.add).then_inc(s["y_ready"], 1)
                pipeline(dve, T0, 2, (0, bias1), (1, turned), (2, bias2))

            @block.scalar
            def _(act):
                def evacuate(j, u, r):
                    act.wait_ge(s["xt_made"], j + 1)
                    if at_least(j, 2):
                        act.wait_ge(s["h_made"], j - 1)
                    nc.scalar.copy(xt[:, u, :], xt_ps[u][:, 0:D]).then_inc(s["xt_ready"], 1)

                def gelu(j, u, r):
                    act.wait_ge(s["hb_ready"], j + 1)
                    if at_least(j, 1):
                        act.wait_ge(s["ht_made"], j)
                    nc.scalar.activation(hg[:, :], hb[:, :], ACT.Gelu).then_inc(s["hg_ready"], 1)
                pipeline(act, T0, 2, (0, evacuate), (1, gelu))

            @block.tensor
            def _(pe):
                def turn(j, u, r):
                    pe.wait_ge(x_in[u], 16 * (r + 1))
                    if at_least(j, 2):
                        pe.wait_ge(s["xt_ready"], j - 1)
                    for c in range(KC):
                        last = nc.tensor.transpose(xt_ps[u][:, c * P:(c + 1) * P], xs[:, u, c * P:(c + 1) * P], m.ident[:, :])
                    last.then_inc(s["xt_made"], 1)

                up_e = []

                def up(j, u, r):
                    if u == 0:
                        up_e[:] = experts_of(nc, m, mybir.EngineType.PE, j, 2)
                    e = up_e[u]
                    pe.wait_ge(s["xt_ready"], j + 1)
                    if at_least(j, 2):
                        pe.wait_ge(s["hb_ready"], j - 1)
                    for c in range(KC):
                        last = nc.tensor.matmul(h_ps[u][:, :], xt[:, u, c * P:(c + 1) * P], w1[:, c, bass.ds(e * F0, F0)],
                                                start=(c == 0), stop=(c == KC - 1))
                    last.then_inc(s["h_made"], 1)

                def turn_h(j, u, r):
                    pe.wait_ge(s["hg_ready"], j + 1)
                    if at_least(j, 2):
                        pe.wait_ge(s["ht_ready"], j - 1)
                    for c in range(FC):
                        last = nc.tensor.transpose(ht_ps[u][:, c * P:(c + 1) * P], hg[:, c * P:(c + 1) * P], m.ident[:, :])
                    last.then_inc(s["ht_made"], 1)

                down_e = []

                def down(j, u, r):
                    if u == 0:
                        down_e[:] = experts_of(nc, m, mybir.EngineType.PE, j, 2)
                    e = down_e[u]
                    pe.wait_ge(s["ht_ready"], j + 1)
                    if at_least(j, 2):
                        pe.wait_ge(s["y_ready"], j - 1)
                    for c in range(FC):
                        last = nc.tensor.matmul(y_ps[u][:, 0:D], ht[:, u, c * P:(c + 1) * P], w2[c][:, bass.ds(e * D, D)],
                                                start=(c == 0), stop=(c == FC - 1))
                    last.then_inc(s["y_made"], 1)
                pipeline(pe, T0, 2, (0, turn), (2, up), (4, down), (3, turn_h))


def combine_and_project(nc, m, a):
    with ExitStack() as ctx:
        def sb(name, shape, dt=F32):
            return ctx.enter_context(nc.sbuf_tensor("cp_" + name, shape, dt))

        G = 7
        NGR = NB // G
        idx = sb("idx", [P, 2, 2, G], U32)
        y = sb("y", [P, 2, 2, G, D])
        w1 = sb("w1", [P, KC, MH])
        xn, xt = sb("xn", [P, G, D]), sb("xt", [P, G, D])
        bank = [ctx.enter_context(nc.psum_tensor(f"cp_bank{i}", [P, 512], F32)) for i in range(6)]
        s = {n: m.sem("cp_" + n) for n in ("indexed issued y0 y1 used chain weights var std xn_ready xt_made xt_ready "
                                           "xt_stored h_made t_ready stored").split()}
        y_in = [s["y0"], s["y1"]]

        def group(t, g):
            return t[:, bass.ds(g * G, G)]

        with nc.Block() as block:
            @block.gpsimd
            def _(pool):
                def gather(g, u, r):
                    if at_least(g, 2):
                        pool.wait_ge(y_in[u], 16 * G * 2 * r)
                        pool.wait_ge(s["used"], g - 1)
                    for e in range(2):
                        nc.gpsimd.tensor_copy(idx[:, u, e, :], m.back[:, e, bass.ds(g * G, G)]).then_inc(s["indexed"], 1)
                    pool.wait_ge(s["indexed"], 2 * (g + 1))
                    pool.sem_inc(s["issued"], 1)
                    for i in range(G):
                        for e in range(2):
                            nc.gpsimd.indirect_dma_start(y[:, u, e, i, :], None, m.y0_d,
                                                         bass.IndirectOffsetOnAxis(ap=idx[:, u, e, i:i + 1], axis=0))\
                                .then_inc(y_in[u], 16)
                pipeline(pool, NGR, 2, (0, gather))

            @block.sync
            def _(sp):
                sp.dma_start(w1[:, :, :], a["L1_gnn_W1"].rearrange("(c p) n -> p c n", p=P)).then_inc(s["weights"], 16)

                def store(g, u, r):
                    sp.wait_ge(s["xt_ready"], G * (g + 1))
                    sp.dma_start(m.xnt_d[bass.ds(g * G, G)].rearrange("b p d -> p b d"), xt[:, :, :]).then_inc(s["xt_stored"], 16)
                    sp.wait_ge(s["t_ready"], G * (g + 1))
                    sp.dma_start(m.t_d[bass.ds(g * G, G)].rearrange("b p n -> p b n"), m.table[:, bass.ds(g * G, G), :])\
                        .then_inc(s["stored"], 16)
                pipeline(sp, NGR, 2, (0, store))
                sp.wait_ge(s["xt_stored"], 16 * NGR)
                sp.wait_ge(s["stored"], 16 * NGR)

            @block.vector
            def _(dve):
                V = nc.vector
                c = Chain(dve, s["chain"])
                c.begin(9)

                def combine(g, u, r):
                    dve.wait_ge(y_in[u], 16 * G * 2 * (r + 1))
                    c.at(g)
                    y0, res = y[:, u, 0, :, :], m.acc[:, bass.ds(g * G, G), 0:D]
                    c.did(V.tensor_tensor(y0, y0, y[:, u, 1, :, :], ALU.add))
                    c.sync()
                    V.tensor_tensor(res, res, y0, ALU.add).then_inc(s["used"], 1)
                    dve.wait_ge(s["used"], g + 1)
                    for i in range(G):
                        last = V.bn_stats(of_block(m.st, g * G + i), of_block(m.acc, g * G + i)[:, 0:D])
                    c.did(last)
                    c.sync()
                    st = m.st[:, bass.ds(g * G, G), :]
                    mean, rstd, tmp0, tmp1 = (group(t, g) for t in (m.mean, m.rstd, m.tmp0, m.tmp1))
                    c.did(V.tensor_tensor(tmp0, st[:, :, 1], st[:, :, 4], ALU.subtract))
                    c.did(V.tensor_tensor(tmp1, st[:, :, 2], st[:, :, 5], ALU.add))
                    c.did(V.tensor_tensor(mean, st[:, :, 1], st[:, :, 4], ALU.add))
                    c.sync()
                    c.did(V.tensor_tensor(tmp0, tmp0, tmp0, ALU.mult))
                    c.did(V.tensor_scalar(mean, mean, 0.5, None, ALU.mult))
                    c.sync()
                    c.did(V.scalar_tensor_tensor(tmp0, tmp0, D / 4.0, tmp1, ALU.mult, ALU.add))
                    c.sync()
                    V.tensor_scalar(tmp0, tmp0, 1.0 / D, EPS, ALU.mult, ALU.add).then_inc(s["var"], 1)
                    dve.wait_ge(s["std"], g + 1)
                    c.did(V.reciprocal(rstd, tmp1))
                    c.sync()
                    for i in range(G):
                        k = g * G + i
                        if at_least(g, 1):
                            dve.wait_ge(s["xt_made"], k - (G - 1))
                        V.tensor_scalar(xn[:, i, :], of_block(m.acc, k)[:, 0:D], m.mean[:, bass.ds(k, 1)],
                                        m.rstd[:, bass.ds(k, 1)], ALU.subtract, ALU.mult).then_inc(s["xn_ready"], 1)

                def scale(g, u, r):
                    for i in range(G):
                        k = g * G + i
                        dve.wait_ge(s["h_made"], k + 1)
                        V.tensor_scalar(of_block(m.table, k), bank[4 + i % 2][:, 0:MH], m.dinv[:, bass.ds(k, 1)], None,
                                        ALU.mult).then_inc(s["t_ready"], 1)
                pipeline(dve, NGR, 2, (0, combine), (0, scale))

            @block.scalar
            def _(act):
                def finish(g, u, r):
                    act.wait_ge(s["var"], g + 1)
                    nc.scalar.activation(group(m.tmp1, g), group(m.tmp0, g), ACT.Sqrt).then_inc(s["std"], 1)
                    for i in range(G):
                        k = g * G + i
                        act.wait_ge(s["xt_made"], k + 1)
                        if at_least(g, 1):
                            act.wait_ge(s["h_made"], k - (G - 1))
                            if i == 0:
                                act.wait_ge(s["xt_stored"], 16 * g)
                        nc.scalar.copy(xt[:, i, :], bank[i % 4][:, 0:D]).then_inc(s["xt_ready"], 1)
                pipeline(act, NGR, 2, (0, finish))

            @block.tensor
            def _(pe):
                def turn(g, i):
                    k = g * G + i
                    pe.wait_ge(s["xn_ready"], k + 1)
                    if at_least(g, 1) or i >= 3:
                        pe.wait_ge(s["xt_ready"], k - 2)
                    for q in range(KC):
                        last = nc.tensor.transpose(bank[i % 4][:, q * P:(q + 1) * P], xn[:, i, q * P:(q + 1) * P], m.ident[:, :])
                    last.then_inc(s["xt_made"], 1)

                def project(g, i):
                    k = g * G + i
                    pe.wait_ge(s["xt_ready"], k + 1)
                    if i >= 2:
                        pe.wait_ge(s["t_ready"], k - 1)
                    elif at_least(g, 1):
                        pe.wait_ge(s["t_ready"], k)
                    for q in range(KC):
                        last = nc.tensor.matmul(bank[4 + i % 2][:, 0:MH], xt[:, i, q * P:(q + 1) * P], w1[:, q, :],
                                                start=(q == 0), stop=(q == KC - 1))
                    last.then_inc(s["h_made"], 1)

                def work(g, u, r):
                    for i in range(G + 2):
                        if i < G:
                            turn(g, i)
                        if i >= 2:
                            project(g, i - 2)
                pe.wait_ge(s["weights"], 16)
                pipeline(pe, NGR, 2, (0, work))


def convolve(nc, m, a, which):
    with ExitStack() as ctx:
        def sb(name, shape, dt=F32):
            return ctx.enter_context(nc.sbuf_tensor(f"v{which}_" + name, shape, dt))

        NR = NG // 2
        idx, rows = sb("idx", [P, 4, GS], U32), sb("rows", [P, 2, GS, MH])
        oh = sb("oh", [P, 2, GS, P])
        xt = sb("xt", [P, D])
        bank = [ctx.enter_context(nc.psum_tensor(f"v{which}_bank{i}", [P, 512], F32)) for i in range(8)]
        s = {n: m.sem(f"v{which}_" + n) for n in "indexed issued in0 in1 oh_ready summed added zeroed xt_in weights".split()}
        landed = [s["in0"], s["in1"]]
        table = m.t_d.rearrange("b p n -> (b p) n")
        if which == 0:
            wkv, bkv = sb("wkv", [P, KC, 2, H, HC]), sb("bkv", [P, 2, H, HC])
            wmean, bmean = sb("wmean", [P, KC, 2, H]), sb("bmean", [P, 2, H])
            kvb, sq = sb("kvb", [P, 2, H, HC]), sb("sq", [P, 2, H, HC])
            var, std, rstd = sb("var", [P, 2, H]), sb("std", [P, 2, H]), sb("rstd", [P, 2, H])
            kn, vn = sb("kn", [P, KC, P + 1]), sb("vn", [P, D])
            s.update({n: m.sem("v0_" + n) for n in ("chain centred kv_made kvb_ready squared summed16 var_ready std_ready rstd_ready "
                                                    "kn_ready kv_used").split()})
            mixed = s["kv_made"]
        else:
            w2, b2 = sb("w2", [P, KC, D]), sb("b2", [P, D])
            ht, xb = sb("ht", [P, KC, P]), sb("xb", [P, D])
            s.update({n: m.sem("v1_" + n) for n in "ht_made ht_ready out_made xn_ready xb_ready mixed res_ready".split()})
            mixed = s["ht_made"]

        with nc.Block() as block:
            @block.gpsimd
            def _(pool):
                def copy_indices(g, w, r):
                    if at_least(g, 4):
                        pool.wait_ge(landed[w % 2], 16 * GS * (2 * r + w // 2 - 1))
                    nc.gpsimd.tensor_copy(idx[:, w, :], m.src[:, bass.ds(g * GS, GS)]).then_inc(s["indexed"], 1)

                def gather(g, w, r):
                    u = w % 2
                    if at_least(g, 2):
                        pool.wait_ge(s["summed"], g - 1)
                    pool.wait_ge(s["indexed"], g + 1)
                    pool.sem_inc(s["issued"], 1)
                    for k in range(GS):
                        nc.gpsimd.indirect_dma_start(rows[:, u, k, :], None, table,
                                                     bass.IndirectOffsetOnAxis(ap=idx[:, w, k:k + 1], axis=0)).then_inc(landed[u], 16)
                pipeline(pool, NG, 4, (0, copy_indices), (1, gather))

            @block.sync
            def _(sp):
                if which == 0:
                    w = a["L1_mix_w_qkv"].rearrange("(c p) (h t d) -> c t p h d", p=P, h=H, t=3)
                    b = a["L1_mix_b_qkv"].rearrange("(h t d) -> t h d", h=H, t=3)
                    for t in range(2):
                        for c in range(KC):
                            sp.dma_start(wkv[:, c, t, :, :], w[c, 1 + t]).then_inc(s["weights"], 16)
                        sp.dma_start(bkv[:, t, :, :], b[1 + t].partition_broadcast(P)).then_inc(s["weights"], 16)
                else:
                    sp.dma_start(w2[:, :, :], a["L1_mix_w2"].rearrange("(c p) n -> p c n", p=P)).then_inc(s["weights"], 16)
                    sp.dma_start(b2[:, :], a["L1_mix_b2"].partition_broadcast(P)).then_inc(s["weights"], 16)

                def load(k, u, r):
                    if at_least(k, 1):
                        sp.wait_ge(mixed, k)
                    sp.dma_start(xt[:, :], block_rows(m.xnt_d, k)).then_inc(s["xt_in"], 16)
                pipeline(sp, NB, 1, (0, load))

            @block.vector
            def _(dve):
                V = nc.vector
                V.memset(m.agg[:, :, :], 0.0).then_inc(s["zeroed"], 1)
                dve.wait_ge(s["zeroed"], 1)
                if which == 0:
                    c = Chain(dve, s["chain"])
                    dve.wait_ge(s["weights"], 16 * 2 * (KC + 1))
                    for w, mean in [(wkv[:, q], wmean[:, q]) for q in range(KC)] + [(bkv, bmean)]:
                        for t in range(2):
                            c.did(V.tensor_reduce(mean[:, t, :], w[:, t, :, :], AX.X, ALU.add))
                            c.sync()
                            c.did(V.scalar_tensor_tensor(w[:, t, :, :], mean[:, t, :].unsqueeze(2).to_broadcast([P, H, HC]),
                                                         -1.0 / HC, w[:, t, :, :], ALU.mult, ALU.add))
                    c.sync()
                    V.memset(kn[:, :, P:P + 1], 1.0).then_inc(s["centred"], 1)

                def one_hot(g, u):
                    if at_least(g, 2):
                        dve.wait_ge(s["summed"], g - 1)
                    V.tensor_tensor(oh[:, u, :, :], m.iota[:, :].unsqueeze(1).to_broadcast([P, GS, P]),
                                    m.dl[:, bass.ds(g * GS, GS)].unsqueeze(2).to_broadcast([P, GS, P]),
                                    ALU.is_equal).then_inc(s["oh_ready"], 1)

                def add(g, u):
                    dve.wait_ge(s["summed"], g + 1)
                    blocks = blocks_of(nc, m, mybir.EngineType.DVE, g * GS, GS)
                    for k in range(GS):
                        t = g * GS + k
                        if at_least(t, 1):
                            dve.wait_ge(s["added"], t)
                        V.tensor_tensor(of_block(m.agg, blocks[k]), of_block(m.agg, blocks[k]), bank[u][:, k * MH:(k + 1) * MH],
                                        ALU.add).then_inc(s["added"], 1)

                def variance(k, u, r):
                    dve.wait_ge(s["squared"], k + 1)
                    V.tensor_reduce(var[:, :, :], sq[:, :, :, :], AX.X, ALU.add).then_inc(s["summed16"], 1)
                    dve.wait_ge(s["summed16"], k + 1)
                    if at_least(k, 1):
                        dve.wait_ge(s["std_ready"], k)
                    V.tensor_scalar(var[:, :, :], var[:, :, :], 1.0 / HC, EPS, ALU.mult, ALU.add).then_inc(s["var_ready"], 1)

                def scale(k, u, r):
                    dve.wait_ge(s["std_ready"], k + 1)
                    if at_least(k, 1):
                        dve.wait_ge(s["kv_used"], k)
                        dve.wait_ge(s["kn_ready"], 2 * k)
                    V.reciprocal(rstd[:, :, :], std[:, :, :]).then_inc(s["rstd_ready"], 1)
                    dve.wait_ge(s["rstd_ready"], k + 1)
                    wide = rstd[:, :, :].unsqueeze(3).to_broadcast([P, 2, H, HC])
                    V.tensor_tensor(kn[:, :, 0:P].rearrange("p c (h d) -> p c h d", d=HC),
                                    kvb[:, 0, :, :].rearrange("p (c h) d -> p c h d", c=KC),
                                    rstd[:, 0, :].rearrange("p (c h) -> p c h", c=KC).unsqueeze(3).to_broadcast([P, KC, H // KC, HC]),
                                    ALU.mult).then_inc(s["kn_ready"], 1)
                    V.tensor_tensor(vn[:, :].rearrange("p (h d) -> p h d", d=HC), kvb[:, 1, :, :], wide[:, 1],
                                    ALU.mult).then_inc(s["kn_ready"], 1)

                def add_bias(k, u, r):
                    dve.wait_ge(s["kv_made"], k + 1)
                    if at_least(k, 1):
                        dve.wait_ge(s["kn_ready"], 2 * k)
                    V.tensor_tensor(kvb[:, :, :, :].rearrange("p t h d -> p (t h d)"), bank[2][:, :],
                                    bkv[:, :, :, :].rearrange("p t h d -> p (t h d)"), ALU.add).then_inc(s["kvb_ready"], 1)

                def normalise(k, u, r):
                    if at_least(k, 1):
                        dve.wait_ge(s["res_ready"], k)
                    V.tensor_scalar(xb[:, :], of_block(m.acc, k)[:, 0:D], m.mean[:, bass.ds(k, 1)], m.rstd[:, bass.ds(k, 1)],
                                    ALU.subtract, ALU.mult).then_inc(s["xn_ready"], 1)
                    dve.wait_ge(s["xn_ready"], k + 1)
                    V.tensor_tensor(xb[:, :], xb[:, :], b2[:, :], ALU.add).then_inc(s["xb_ready"], 1)

                def finish(k, u, r):
                    dve.wait_ge(s["xb_ready"], k + 1)
                    dve.wait_ge(s["out_made"], k + 1)
                    V.tensor_tensor(xb[:, :], xb[:, :], bank[3][:, 0:D], ALU.add).then_inc(s["mixed"], 1)
                    dve.wait_ge(s["mixed"], k + 1)
                    res = of_block(m.acc, k)[:, 0:D]
                    V.tensor_tensor(res, res, xb[:, :], ALU.add).then_inc(s["res_ready"], 1)

                conv = ((0, lambda k, u, r: one_hot(2 * k, 0)), (1, lambda k, u, r: add(2 * k + 1, 1)),
                        (0, lambda k, u, r: one_hot(2 * k + 1, 1)), (0, lambda k, u, r: add(2 * k, 0)))
                if which == 0:
                    pipeline(dve, NR, 1, conv[0], conv[1], (1, variance, NB), conv[2], conv[3], (1, scale, NB), (0, add_bias, NB))
                else:
                    dve.wait_ge(s["weights"], 32)
                    pipeline(dve, NR, 1, conv[0], conv[1], (1, normalise, NB), conv[2], conv[3], (1, finish, NB))

            @block.scalar
            def _(act):
                def root(k, u, r):
                    act.wait_ge(s["var_ready"], k + 1)
                    if at_least(k, 1):
                        act.wait_ge(s["rstd_ready"], k)
                    nc.scalar.activation(std[:, :, :], var[:, :, :], ACT.Sqrt).then_inc(s["std_ready"], 1)

                def square(k, u, r):
                    act.wait_ge(s["kvb_ready"], k + 1)
                    if at_least(k, 1):
                        act.wait_ge(s["summed16"], k)
                    nc.scalar.activation(sq[:, :, :, :], kvb[:, :, :, :], ACT.Square).then_inc(s["squared"], 1)

                def gelu(k, u, r):
                    act.wait_ge(s["ht_made"], k + 1)
                    if at_least(k, 1):
                        act.wait_ge(s["out_made"], k)
                    for q in range(KC):
                        last = nc.scalar.activation(ht[:, q, :], bank[2][:, q * P:(q + 1) * P], ACT.Gelu, bias=m.c2[:, q:q + 1])
                    last.then_inc(s["ht_ready"], 1)
                if which == 0:
                    pipeline(act, NB, 1, (1, root), (0, square))
                else:
                    pipeline(act, NB, 1, (0, gelu))

            @block.tensor
            def _(pe):
                def total(g, u):
                    pe.wait_ge(s["oh_ready"], g + 1)
                    pe.wait_ge(landed[u], 16 * GS * ((g - u) // 2 + 1))
                    if at_least(g, 2):
                        pe.wait_ge(s["added"], GS * (g - 1))
                    for k in range(GS):
                        last = nc.tensor.matmul(bank[u][:, k * MH:(k + 1) * MH], oh[:, u, k, :], rows[:, u, k, :],
                                                start=True, stop=True)
                    last.then_inc(s["summed"], 1)

                def project(k, u, r):
                    pe.wait_ge(s["xt_in"], 16 * (k + 1))
                    if at_least(k, 1):
                        pe.wait_ge(s["kvb_ready"], k)
                    for q in range(KC):
                        last = nc.tensor.matmul(bank[2][:, :], xt[:, q * P:(q + 1) * P],
                                                wkv[:, q, :, :, :].rearrange("p t h d -> p (t h d)"), start=(q == 0), stop=(q == KC - 1))
                    last.then_inc(s["kv_made"], 1)

                def sum_kv(k, u, r):
                    rows_ = LAST if isinstance(k, int) and k == NB - 1 else P
                    first, final = isinstance(k, int) and k == 0, isinstance(k, int) and k == NB - 1
                    pe.wait_ge(s["kn_ready"], 2 * k + 2)
                    for q in range(KC):
                        nc.tensor.matmul(bank[4 + q][:, 0:P + 1], vn[0:rows_, q * P:(q + 1) * P], kn[0:rows_, q, :],
                                         start=first, stop=final)
                        last = nc.tensor.matmul(bank[6 + q][:, 0:P], m.ones[0:rows_, :], kn[0:rows_, q, 0:P],
                                                start=first, stop=final)
                    last.then_inc(s["kv_used"], 1)

                def up(k, u, r):
                    pe.wait_ge(s["xt_in"], 16 * (k + 1))
                    if at_least(k, 1):
                        pe.wait_ge(s["ht_ready"], k)
                    for j in range(KC):
                        for q in range(KC):
                            last = nc.tensor.matmul(bank[2][:, j * P:(j + 1) * P], m.m2[:, q, j * P:(j + 1) * P],
                                                    xt[:, q * P:(q + 1) * P], start=(q == 0), stop=(q == KC - 1))
                    last.then_inc(s["ht_made"], 1)

                def down(k, u, r):
                    pe.wait_ge(s["ht_ready"], k + 1)
                    if at_least(k, 1):
                        pe.wait_ge(s["mixed"], k)
                    for q in range(KC):
                        last = nc.tensor.matmul(bank[3][:, 0:D], ht[:, q, :], w2[:, q, :], start=(q == 0), stop=(q == KC - 1))
                    last.then_inc(s["out_made"], 1)

                even, odd = (0, lambda k, u, r: total(2 * k, 0)), (0, lambda k, u, r: total(2 * k + 1, 1))
                if which == 0:
                    pe.wait_ge(s["centred"], 1)
                    pipeline(pe, NR, 1, even, (2, sum_kv, NB), (0, project, NB), odd)
                else:
                    pe.wait_ge(s["weights"], 32)
                    pipeline(pe, NR, 1, even, (1, down, NB), (0, up, NB), odd)

        if which == 0:
            fold_mixer(nc, m, a, bank)


def fold_mixer(nc, m, a, bank):
    with ExitStack() as ctx:
        def sb(name, shape, dt=F32):
            return ctx.enter_context(nc.sbuf_tensor("fm_" + name, shape, dt))

        b1row = sb("b1row", [P, MH])
        wqt, w1 = sb("wqt", [P, KC, D]), sb("w1", [P, KC, D])
        bq, b1 = sb("bq", [P, KC]), sb("b1", [P, KC])
        kg, kb = sb("kg", [P, HC]), sb("kb", [P, HC])
        vg, vb = sb("vg", [P, 1]), sb("vb", [P, 1])
        kvt, sk, t = sb("kvt", [P, KC, P]), sb("sk", [P, KC, P]), sb("t", [P, KC, D])
        s = {n: m.sem("fm_" + n) for n in "weights chain table stored kvt t_made t_back m_made".split()}
        chunks = lambda x: x[:, :, :].rearrange("p c (h d) -> p c h d", d=HC)
        wide = lambda row: row[:, :].unsqueeze(1).to_broadcast([P, P // HC, HC])
        heads = lambda x: x.rearrange("p (h d) -> p h d", d=HC)

        with nc.Block() as block:
            @block.sync
            def _(sp):
                n = 0
                for out, v in ((b1row[:, :], a["L1_gnn_b1"].partition_broadcast(P)), (kg[:, :], a["L1_mix_kln_g"].partition_broadcast(P)),
                               (kb[:, :], a["L1_mix_kln_b"].partition_broadcast(P)),
                               (wqt[:, :, :], a["WqT1"].rearrange("(c p) n -> p c n", p=P)),
                               (w1[:, :, :], a["L1_mix_w1"].rearrange("(c p) n -> p c n", p=P))):
                    sp.dma_start(out, v).then_inc(s["weights"], 16)
                for h in range(P // HC):
                    o = slice(h * HC, (h + 1) * HC)
                    for out, v in ((vg, "L1_mix_vln_g"), (vb, "L1_mix_vln_b")):
                        sp.dma_start(out[o, :], a[v].rearrange("(p c) -> p c", c=1), allow_slow_non_contiguous=True).then_inc(s["weights"], 16)
                sp.dma_start(b1[:, :], a["L1_mix_b1"].rearrange("(c p) -> p c", p=P), allow_slow_non_contiguous=True).then_inc(s["weights"], 16)
                for h in range(H):
                    p0 = h * HC % P
                    sp.dma_start(bq[p0:p0 + HC, h * HC // P:h * HC // P + 1],
                                 a["L1_mix_b_qkv"][3 * h * HC:(3 * h + 1) * HC].rearrange("(p c) -> p c", c=1),
                                 allow_slow_non_contiguous=True).then_inc(s["weights"], 16)
                sp.wait_ge(s["table"], 1)
                sp.dma_start(m.t_d.rearrange("b p n -> p b n"), m.table[:, :, :]).then_inc(s["stored"], 16)
                sp.wait_ge(s["stored"], 16)

            @block.vector
            def _(dve):
                V, c = nc.vector, Chain(dve, s["chain"])
                dve.wait_ge(s["weights"], 16 * (5 + 2 * (P // HC) + 1 + H))
                dinv = m.dinv[:, :].unsqueeze(2).to_broadcast([P, NB, MH])
                for q in range(KC):
                    S, sv = bank[4 + q][:, 0:P], bank[4 + q][:, P:P + 1]
                    c.did(V.tensor_tensor(heads(kvt[:, q, :]), heads(S), wide(kg), ALU.mult))
                    c.did(V.tensor_tensor(heads(sk[:, q, :]), heads(bank[6 + q][:, 0:P]), wide(kg), ALU.mult))
                    c.did(V.tensor_copy(t[:, q, 0:1], sv))
                c.sync()
                for q in range(KC):
                    c.did(V.scalar_tensor_tensor(heads(kvt[:, q, :]), wide(kb), t[:, q, 0:1], heads(kvt[:, q, :]), ALU.mult, ALU.add))
                    c.did(V.scalar_tensor_tensor(heads(sk[:, q, :]), wide(kb), float(N), heads(sk[:, q, :]), ALU.mult, ALU.add))
                c.sync()
                c.did(V.tensor_scalar(kvt[:, :, :], kvt[:, :, :], vg[:, 0:1], None, ALU.mult))
                c.sync()
                c.did(V.scalar_tensor_tensor(kvt[:, :, :], sk[:, :, :], vb[:, 0:1], kvt[:, :, :], ALU.mult, ALU.add))
                c.sync()
                V.tensor_tensor(kvt[:, :, :], kvt[:, :, :], m.bd[:, :, :], ALU.mult).then_inc(s["kvt"], 1)
                c.did(V.tensor_tensor(m.agg[:, :, :], m.agg[:, :, :], m.table[:, :, :], ALU.add))
                c.sync()
                c.did(V.tensor_tensor(m.agg[:, :, :], m.agg[:, :, :], dinv, ALU.mult))
                c.sync()
                c.did(V.tensor_tensor(m.agg[:, :, :], m.agg[:, :, :], b1row[:, :].unsqueeze(1).to_broadcast([P, NB, MH]), ALU.add))
                c.sync()
                V.scalar_tensor_tensor(m.table[:, :, :], m.agg[:, :, :], 0.0, dinv, ALU.max, ALU.mult).then_inc(s["table"], 1)
                dve.wait_ge(s["t_made"], 1)
                for q in range(KC):
                    ins = V.tensor_copy(t[:, q, :], bank[q][:, 0:D])
                ins.then_inc(s["t_back"], 1)
                dve.wait_ge(s["m_made"], 1)
                for q in range(KC):
                    V.tensor_tensor(m.m2[:, q, :], w1[:, q, :], bank[2 + q][:, 0:D], ALU.add)
                    V.tensor_tensor(m.c2[:, q:q + 1], b1[:, q:q + 1], bank[4][:, q:q + 1], ALU.add)

            @block.tensor
            def _(pe):
                pe.wait_ge(s["kvt"], 1)
                for q in range(KC):
                    last = nc.tensor.matmul(bank[q][:, 0:D], kvt[:, q, :], w1[:, q, :], start=True, stop=True)
                last.then_inc(s["t_made"], 1)
                pe.wait_ge(s["t_back"], 1)
                for q in range(KC):
                    for h in range(KC):
                        nc.tensor.matmul(bank[2 + q][:, 0:D], wqt[:, h, q * P:(q + 1) * P], t[:, h, :],
                                         start=(h == 0), stop=(h == KC - 1))
                for q in range(KC):
                    for h in range(KC):
                        last = nc.tensor.matmul(bank[4][:, q:q + 1], t[:, h, q * P:(q + 1) * P], bq[:, h:h + 1],
                                                start=(h == 0), stop=(h == KC - 1))
                last.then_inc(s["m_made"], 1)


def finish_convolution(nc, m, a):
    with ExitStack() as ctx:
        def sb(name, shape, dt=F32):
            return ctx.enter_context(nc.sbuf_tensor("fc_" + name, shape, dt))

        w2, ut, us = sb("w2", [MH + 1, D]), sb("ut", [MH + 1, 4, P]), sb("us", [P, 4, MH])
        bank = [ctx.enter_context(nc.psum_tensor(f"fc_bank{i}", [P, 512], F32)) for i in range(6)]
        s = {n: m.sem("fc_" + n) for n in "weights chain ones u_ready ut_made ut_ready made res_ready stat".split()}

        with nc.Block() as block:
            @block.sync
            def _(sp):
                sp.dma_start(w2[0:MH, :], a["L1_gnn_W2"]).then_inc(s["weights"], 16)
                sp.dma_start(w2[MH:MH + 1, :], a["L1_gnn_b2"].rearrange("(a n) -> a n", a=1)).then_inc(s["weights"], 16)

            @block.vector
            def _(dve):
                V, c = nc.vector, Chain(dve, s["chain"])
                V.memset(ut[MH:MH + 1, :, :], 1.0).then_inc(s["ones"], 1)
                c.did(V.tensor_tensor(m.agg[:, :, :], m.agg[:, :, :], m.table[:, :, :], ALU.add))
                c.sync()

                def scale(k, u, r):
                    if at_least(k, 4):
                        dve.wait_ge(s["ut_made"], k - 3)
                    V.tensor_scalar(us[:, u, :], of_block(m.agg, k), m.dinv[:, bass.ds(k, 1)], None, ALU.mult).then_inc(s["u_ready"], 1)

                def finish(k, u, r):
                    dve.wait_ge(s["made"], k + 1)
                    res = of_block(m.acc, k)[:, 0:D]
                    V.scalar_tensor_tensor(res, bank[4 + u % 2][:, 0:D], 0.0, res, ALU.max, ALU.add).then_inc(s["res_ready"], 1)

                def stats(k, u, r):
                    dve.wait_ge(s["res_ready"], k + 1)
                    V.bn_stats(of_block(m.st, k), of_block(m.acc, k)[:, 0:D]).then_inc(s["stat"], 1)
                pipeline(dve, NB, 4, (0, scale), (5, finish), (6, stats))

            @block.scalar
            def _(act):
                def evacuate(k, u, r):
                    act.wait_ge(s["ut_made"], k + 1)
                    if at_least(k, 4):
                        act.wait_ge(s["made"], k - 3)
                    nc.scalar.copy(ut[0:MH, u, :], bank[u][0:MH, 0:P]).then_inc(s["ut_ready"], 1)
                pipeline(act, NB, 4, (0, evacuate))

            @block.tensor
            def _(pe):
                def turn(k, u, r):
                    if at_least(k, 4):
                        pe.wait_ge(s["ut_ready"], k - 3)
                    pe.wait_ge(s["u_ready"], k + 1)
                    nc.tensor.matmul(bank[u][0:MH, 0:P], us[:, u, :], m.ident[:, :], start=True, stop=True).then_inc(s["ut_made"], 1)

                def project(k, u, r):
                    pe.wait_ge(s["ut_ready"], k + 1)
                    if at_least(k, 2):
                        pe.wait_ge(s["res_ready"], k - 1)
                    nc.tensor.matmul(bank[4 + u % 2][:, 0:D], ut[:, u, :], w2[:, :], start=True, stop=True).then_inc(s["made"], 1)
                pe.wait_ge(s["weights"], 32)
                pe.wait_ge(s["ones"], 1)
                pipeline(pe, NB, 4, (0, turn), (3, project))


def weights1(m):
    W = KC * F1
    return (m.big0[:, 0:2 * W].rearrange("p (u c f) -> p u c f", u=2, c=KC),
            m.big0[:, 2 * W:4 * W].rearrange("p (u f d) -> p u f d", u=2, d=D))


def load_expert_weights1(eng, m, a, u, e, loaded):
    w1, w2 = weights1(m)
    eng.dma_start(w1[:, u, :, :], a["L1_ffn_w1"][bass.ds(e, 1)].rearrange("a (c p) f -> p (a c) f", p=P)).then_inc(loaded, 16)
    eng.dma_start(w2[:, u, :, :], a["L1_ffn_w2"][bass.ds(e, 1)].rearrange("a (f p) d -> p (a f) d", p=P)).then_inc(loaded, 16)


def experts1(nc, m, a):
    with ExitStack() as ctx:
        def sb(name, shape, dt=F32):
            return ctx.enter_context(nc.sbuf_tensor("e1_" + name, shape, dt))

        FC, UT = F1 // P, CT // 2
        UR = UT * P
        used = (UR, CAP - UR)
        NU = 2 * NE
        w1, w2 = weights1(m)
        b1, b2 = sb("b1", [P, NE, FC]), sb("b2", [P, NE, D])
        b1e = sb("b1e", [P, 2, FC])
        xs, xt = sb("xs", [P, UT, D]), sb("xt", [P, KC, UR])
        ht, y = sb("ht", [P, FC, UR]), sb("y", [P, UT, D])
        bank = [ctx.enter_context(nc.psum_tensor(f"e1_bank{i}", [P, 512], F32)) for i in range(8)]
        xt_ps, h_ps, y_ps = bank[0:2], bank[2:5], bank[5:8]
        s = {n: m.sem("e1_" + n) for n in "biases w0 w1 x_in y_out xt_made xt_ready h_made h_ready down y_made y_ready".split()}
        w_in = [s["w0"], s["w1"]]

        with nc.Block() as block:
            @block.sync
            def _(sp):
                sp.dma_start(b1[:, :, :], a["L1_ffn_b1"].rearrange("e (f p) -> p e f", p=P), allow_slow_non_contiguous=True)\
                    .then_inc(s["biases"], 16)
                sp.dma_start(b2[:, :, :].rearrange("p e f -> p (e f)"), a["L1_ffn_b2"].rearrange("e f -> (e f)").partition_broadcast(P))\
                    .then_inc(s["biases"], 16)

                def load(j, v, r):
                    if at_least(j, 1):
                        sp.wait_ge(s["xt_made"], j)
                    sp.dma_start(xs[:, :, :], m.buf1_d[bass.ds(j * UR, UR), :].rearrange("(t p) d -> p t d", p=P)).then_inc(s["x_in"], 16)
                    if v % 2 == 0 and at_least(j, 4):
                        u, e = v // 2, 2 * r + v // 2
                        sp.wait_ge(s["down"], j - 2)
                        load_expert_weights1(sp, m, a, u, e, w_in[u])

                def store(j, v, r):
                    sp.wait_ge(s["y_ready"], UT * (j + 1))
                    sp.dma_start(m.y1_d[bass.ds(j * UR, UR), :].rearrange("(t p) d -> p t d", p=P), y[:, :, :]).then_inc(s["y_out"], 16)
                pipeline(sp, NU, 4, (0, load), (3, store))
                sp.wait_ge(s["y_out"], 16 * NU)

            @block.vector
            def _(dve):
                V = nc.vector

                def turned(j, v, r):
                    dve.wait_ge(s["xt_made"], j + 1)
                    if at_least(j, 1):
                        dve.wait_ge(s["h_made"], FC * j)
                    if v % 2 == 0:
                        if at_least(j, 4):
                            dve.wait_ge(s["h_ready"], FC * (j - 2))
                        V.tensor_copy(b1e[:, v // 2, :], of_block(b1, 2 * r + v // 2))
                    for q in range(KC):
                        V.tensor_copy(xt[:, q, :], xt_ps[q][:, :]).then_inc(s["xt_ready"], 1)

                def finish(j, v, r):
                    e = 2 * r + v // 2
                    if at_least(j, 1):
                        dve.wait_ge(s["y_out"], 16 * j)
                    for t in range(UT):
                        dve.wait_ge(s["y_made"], UT * j + t + 1)
                        V.tensor_tensor(y[:, t, :], y_ps[(UT * v + t) % 2][:, 0:D], of_block(b2, e), ALU.add).then_inc(s["y_ready"], 1)
                dve.wait_ge(s["biases"], 32)
                pipeline(dve, NU, 4, (0, turned), (1, finish))

            @block.scalar
            def _(act):
                def relu(j, v, r):
                    if at_least(j, 1):
                        act.wait_ge(s["down"], j)
                    act.wait_ge(s["xt_ready"], KC * (j + 1))
                    for f in range(FC):
                        act.wait_ge(s["h_made"], FC * j + f + 1)
                        nc.scalar.activation(ht[:, f, 0:used[v % 2]], h_ps[f % 2][:, 0:used[v % 2]], ACT.Relu,
                                             bias=b1e[:, v // 2, f:f + 1]).then_inc(s["h_ready"], 1)
                pipeline(act, NU, 4, (0, relu))

            @block.tensor
            def _(pe):
                def turn(j, v, r):
                    pe.wait_ge(s["x_in"], 16 * (j + 1))
                    if at_least(j, 1):
                        pe.wait_ge(s["xt_ready"], KC * j)
                    for q in range(KC):
                        for t in range(UT):
                            last = nc.tensor.transpose(xt_ps[q][:, t * P:(t + 1) * P], xs[:, t, q * P:(q + 1) * P], m.ident[:, :])
                    last.then_inc(s["xt_made"], 1)

                def up(j, v, r):
                    u, n = v // 2, used[v % 2]
                    if v % 2 == 0 and at_least(j, 4):
                        pe.wait_ge(w_in[u], 32 * r)
                    pe.wait_ge(s["xt_ready"], KC * (j + 1))
                    for f in range(FC):
                        if f >= 2 or at_least(j, 1):
                            pe.wait_ge(s["h_ready"], FC * j + f - 1)
                        for q in range(KC):
                            last = nc.tensor.matmul(h_ps[f % 2][:, 0:n], w1[:, u, q, f * P:(f + 1) * P], xt[:, q, 0:n],
                                                    start=(q == 0), stop=(q == KC - 1))
                        last.then_inc(s["h_made"], 1)

                def down(j, v, r):
                    u = v // 2
                    pe.wait_ge(s["h_ready"], FC * (j + 1))
                    for t in range(UT):
                        if t >= 2 or at_least(j, 1):
                            pe.wait_ge(s["y_ready"], UT * j + t - 1)
                        for f in range(FC):
                            last = nc.tensor.matmul(y_ps[(UT * v + t) % 2][:, 0:D], ht[:, f, t * P:(t + 1) * P], w2[:, u, f, :],
                                                    start=(f == 0), stop=(f == FC - 1))
                        last.then_inc(s["y_made"], 1)
                    nc.tensor.transpose(xt_ps[0][0:1, 0:P], m.ident[:, 0:1], m.ident[:, :]).then_inc(s["down"], 1)
                pipeline(pe, NU, 4, (1, up), (0, turn), (1, down))


def combine_experts1(nc, m, a):
    with ExitStack() as ctx:
        def sb(name, shape, dt=F32):
            return ctx.enter_context(nc.sbuf_tensor("c1_" + name, shape, dt))

        G = 7
        NGR = NB // G
        idx = sb("idx", [P, 2, G], U32)
        y = sb("y", [P, 2, G, D])
        consts, bad = sb("consts", [P, 3]), sb("bad", [P, 3, G, D], mybir.dt.uint8)
        s = {n: m.sem("c1_" + n) for n in "indexed issued y0 y1 used chain out0 out1".split()}
        y_in, out_done = [s["y0"], s["y1"]], [s["out0"], s["out1"]]

        with nc.Block() as block:
            @block.gpsimd
            def _(pool):
                def gather(g, u, r):
                    if at_least(g, 2):
                        pool.wait_ge(y_in[u], 16 * G * r)
                        pool.wait_ge(s["used"], g - 1)
                        pool.wait_ge(out_done[u], 16 * r)
                    nc.gpsimd.tensor_copy(idx[:, u, :], m.back[:, 0, bass.ds(g * G, G)]).then_inc(s["indexed"], 1)
                    pool.wait_ge(s["indexed"], g + 1)
                    pool.sem_inc(s["issued"], 1)
                    for i in range(G):
                        nc.gpsimd.indirect_dma_start(y[:, u, i, :], None, m.y1_d,
                                                     bass.IndirectOffsetOnAxis(ap=idx[:, u, i:i + 1], axis=0)).then_inc(y_in[u], 16)
                pipeline(pool, NGR, 2, (0, gather))

            @block.vector
            def _(dve):
                V = nc.vector
                c = Chain(dve, s["chain"])
                for i, v in enumerate((0.0, 10000.0, -10000.0)):
                    c.did(V.memset(consts[:, i:i + 1], v))
                c.sync()
                c.begin(7)

                def combine(g, u, r):
                    dve.wait_ge(y_in[u], 16 * G * (r + 1))
                    c.at(g)
                    yk, res = y[:, u, :, :], m.acc[:, bass.ds(g * G, G), 0:D]
                    c.did(V.tensor_tensor(yk, yk, m.prob[:, bass.ds(g * G, G)].unsqueeze(2).to_broadcast([P, G, D]), ALU.mult))
                    c.sync()
                    c.did(V.tensor_tensor(bad[:, 0], yk, yk, ALU.not_equal))
                    c.did(V.tensor_scalar(bad[:, 1], yk, FMAX, None, ALU.is_gt))
                    c.did(V.tensor_scalar(bad[:, 2], yk, -FMAX, None, ALU.is_lt))
                    for i in range(3):
                        c.sync()
                        dve.sem_inc(s["issued"], 1)
                        c.did(V.copy_predicated(yk, bad[:, i], consts[:, i:i + 1].unsqueeze(2).to_broadcast([P, G, D])))
                    c.sync()
                    V.tensor_tensor(yk, res, yk, ALU.add).then_inc(s["used"], 1)
                pipeline(dve, NGR, 2, (0, combine))

            @block.sync
            def _(sp):
                def store(g, u, r):
                    sp.wait_ge(s["used"], g + 1)
                    if isinstance(g, int) and g == NGR - 1:
                        b = (NB - 1) * P
                        sp.dma_start(m.out[g * G * P:b, :].rearrange("(b p) d -> p b d", p=P), y[:, u, 0:G - 1, :]).then_inc(out_done[u], 16)
                        sp.dma_start(m.out[b:N, :], y[0:LAST, u, G - 1, :]).then_inc(out_done[u], 16)
                    else:
                        sp.dma_start(m.out[bass.ds(g * G * P, G * P), :].rearrange("(b p) d -> p b d", p=P), y[:, u, :, :])\
                            .then_inc(out_done[u], 16)
                pipeline(sp, NGR, 2, (0, store))
                sp.wait_ge(out_done[0], 16 * (NGR // 2 + 2))
                sp.wait_ge(out_done[1], 16 * (NGR // 2))


def memory(nc, ctx):
    m = Chip()

    def sb(name, shape, dt=F32):
        return ctx.enter_context(nc.sbuf_tensor(name, shape, dt))

    def dram(name, shape, dt=F32):
        return nc.dram_tensor(name, shape, dt).ap()

    m.live = []

    def sem(name):
        m.live.append(nc.alloc_semaphore(name=name))
        return m.live[-1]
    m.sem = sem
    m.src_p, m.dst_p, m.w_p = dram("src_p", [EP], I32), dram("dst_p", [EP], I32), dram("w_p", [EP])
    m.btab_d, m.key_d = dram("btab_d", [SPAD], I32), dram("key_d", [SPAD, P])
    m.xnt_d, m.xl_d = dram("xnt_d", [NB, P, D]), dram("xl_d", [NB, P, LW])
    m.ident, m.iota, m.ones = sb("ident", [P, P]), sb("iota", [P, P]), sb("ones", [P, P])
    m.btab = sb("btab", [1, SPAD], I32)
    m.src, m.dl = sb("src_steps", [P, SPAD], U32), sb("dl_steps", [P, SPAD])
    m.w = sb("w_steps", [P, SPAD])
    m.buf0_d, m.y0_d = dram("buf0_d", [T0 * P, D]), dram("y0_d", [T0 * P, D])
    m.buf1_d, m.y1_d = dram("buf1_d", [NE * CT * P, D]), dram("y1_d", [NE * CT * P, D])
    m.dinv, m.prob, m.st, m.e8 = sb("dinv", [P, NB]), sb("prob", [P, NB]), sb("st", [P, NB, 6]), sb("e8", [P, NE])
    m.slots, m.back, m.etab = sb("slots", [P, 2, NB], U32), sb("back", [P, 2, NB], U32), sb("etab", [1, T0], I32)
    m.xj_d = dram("xj_d", [2 * NG, P, GS // 2 * LW])
    m.ex = sb("ex", [P, NS * H])
    m.mean, m.rstd = sb("mean", [P, NB]), sb("rstd", [P, NB])
    m.tmp0, m.tmp1 = sb("tmp0", [P, NB]), sb("tmp1", [P, NB])
    m.atta = sb("atta", [P, KC, H])
    m.kvt, m.bd = sb("kvt", [P, KC, P]), sb("bd", [P, KC, P])
    gram = sb("gram", [P, KC * (D + 1)])
    m.gram = gram[:, :].rearrange("p (c n) -> p c n", c=KC)
    m.notfirst = gram[:, 0:NE * NB].rearrange("p (e b) -> p e b", e=NE)
    m.t_d = dram("t_d", [NB, P, MH])
    m.m2, m.c2 = sb("m2", [P, KC, D]), sb("c2", [P, KC])
    m.big0, m.big1 = sb("big0", [P, 2 * CL]), sb("big1", [P, 2 * CL + 8])
    m.table = m.big0[:, 0:NB * MH].rearrange("p (b n) -> p b n", n=MH)
    m.agg = m.big0[:, NB * MH:2 * NB * MH].rearrange("p (b n) -> p b n", n=MH)
    return m


def build(nc, a, out):
    with ExitStack() as ctx:
        m = memory(nc, ctx)
        m.out = out
        edge_steps(nc, m, a)
        end_stage(nc, m)
        for stage in (project_nodes, score_edges, normalise_edges, aggregate_edges, finish_attention):
            stage(nc, m, a)
            end_stage(nc, m)
        with ExitStack() as ffn:
            expert_weights0(nc, m, ffn)
            route(nc, m, a, 0)
            end_stage(nc, m)
            experts0(nc, m, a)
            end_stage(nc, m)
        combine_and_project(nc, m, a)
        end_stage(nc, m)
        for which in range(2):
            convolve(nc, m, a, which)
            end_stage(nc, m)
        finish_convolution(nc, m, a)
        end_stage(nc, m)
        route(nc, m, a, 1)
        end_stage(nc, m)
        experts1(nc, m, a)
        end_stage(nc, m)
        combine_experts1(nc, m, a)


TURNED = {"L0_gnn_W_l": "W_lT", "L0_gnn_W_r": "W_rT", "L0_mix_Wk": "WkT", "L0_mix_Wv": "WvT", "L0_mix_Wfc": "WfcT"}


def laid_out(inputs):
    arrays = {n: np.ascontiguousarray(v) for n, v in inputs.items() if n not in ("L0_mix_Wk", "L0_mix_Wv", "L0_mix_Wfc")}
    for name, turned in TURNED.items():
        arrays[turned] = np.ascontiguousarray(np.asarray(inputs[name]).T)
    qkv = np.asarray(inputs["L1_mix_w_qkv"]).reshape(D, H, 3 * HC)
    arrays["WqT1"] = np.ascontiguousarray(qkv[:, :, 0:HC].reshape(D, D).T)
    return arrays


def kernel(**inputs):
    import concourse.bacc as bacc
    from concourse.bass_utils import run_bass_kernel_spmd

    nc = bacc.Bacc("TRN2", target_bir_lowering=False, num_devices=1)
    arrays = laid_out(inputs)
    a = {n: nc.dram_tensor("in_" + n, v.shape, mybir.dt.from_np(v.dtype), kind="ExternalInput").ap() for n, v in arrays.items()}
    out = nc.dram_tensor("out", (N, D), F32, kind="ExternalOutput").ap()
    build(nc, a, out)
    r = run_bass_kernel_spmd(nc, [{"in_" + n: v for n, v in arrays.items()}], core_ids=[0])
    return r.results[0]["out"]
```
